# Optimizing a Trainium2 kernel written in Bass

```python
import numpy as np
import jax
import jax.numpy as jnp

def _softmax(x, axis=-1):
    return jax.nn.softmax(x, axis=axis)

def _gelu(x):
    return jax.nn.gelu(x, approximate=True)

def _silu(x):
    return jax.nn.silu(x)

def _sigmoid(x):
    return jax.nn.sigmoid(x)

def _layernorm(x, axis=-1, eps=1e-05):
    m = jnp.mean(x, axis=axis, keepdims=True)
    v = jnp.var(x, axis=axis, keepdims=True)
    return (x - m) / jnp.sqrt(v + eps)

def _scatter_add(tgt, idx, src, axis=0):
    return tgt.at[idx].add(src)

def _segment_sum(src, seg, n):
    return jax.ops.segment_sum(src, seg, n)
kernel_name = 'mk_gnn_ffn_d2_gnn_r32_607958'

def setup_inputs(seed: int=0):
    np.random.seed(seed)
    _w = jnp.asarray

    def _rec_inputs():
        import jax
        import jax.numpy as jnp
        _gk = jax.random.key(seed)
        x = -0.0003713 + 1 * jax.random.normal(jax.random.fold_in(_gk, 1), (3125, 256), jnp.float32)
        src = jax.random.randint(jax.random.fold_in(_gk, 2), (50000,), 0, 3125, jnp.int32)
        dst = jnp.minimum((3125 * jax.random.uniform(jax.random.fold_in(_gk, 3), (50000,)) ** 2.0).astype(jnp.int32), 99999)
        _o = jnp.argsort(dst, stable=True)
        src = src[_o]
        dst = dst[_o]
        return (x, src, dst)
    x, src, dst = _rec_inputs()

    def _L0_gnn_setup():
        import jax, jax.numpy as jnp
        import numpy as np
        BN_EPS = 1e-05
        CHANNELS = [256, 512, 1024, 512, 256]

        def _bn(h, gamma, beta):
            m = h.mean(axis=0)
            v = h.var(axis=0)
            return gamma * (h - m) * jax.lax.rsqrt(v + BN_EPS) + beta
        key = jax.random.key(seed)
        N, E = (50000, 25000)
        ks = jax.random.split(key, 16)
        inp = {'x': jax.random.normal(ks[0], (N, CHANNELS[0]), dtype=jnp.float32), 'edge_index': jax.random.randint(ks[1], (2, E), 0, N, dtype=jnp.int32), 'eps': jnp.float32(0.1)}
        for i in range(4):
            cin, cout = (CHANNELS[i], CHANNELS[i + 1])
            inp[f'W{i + 1}'] = jax.random.normal(ks[2 + 3 * i], (cin, cout), dtype=jnp.float32) * (1.0 / np.sqrt(cin))
            inp[f'b{i + 1}'] = jnp.zeros((cout,), dtype=jnp.float32)
            if i < 3:
                inp[f'g{i + 1}'] = jnp.ones((cout,), dtype=jnp.float32)
                inp[f'beta{i + 1}'] = jnp.zeros((cout,), dtype=jnp.float32)
        return inp
    _L0_gnn_all = _L0_gnn_setup()
    _L0_gnn_in = {k: v for k, v in _L0_gnn_all.items() if k in ('eps', 'W1', 'b1', 'g1', 'beta1', 'W2', 'b2', 'g2', 'beta2', 'W3', 'b3', 'g3', 'beta3', 'W4', 'b4')}
    del _L0_gnn_all

    def _L0_ffn_setup():
        import jax, jax.numpy as jnp
        import numpy as np
        N_EXPERTS = 8
        TOP_K = 2
        key = jax.random.key(seed)
        ks = jax.random.split(key, 5)
        B, T, C, E, H = (8, 64, 256, 8, 682)
        scale = 1.0 / np.sqrt(C)
        return {'x': jax.random.normal(ks[0], (B, T, C), dtype=jnp.float32), 'router_w': jax.random.normal(ks[1], (E, C), dtype=jnp.float32) * scale, 'w1': jax.random.normal(ks[2], (E, H, C), dtype=jnp.float32) * scale, 'w2': jax.random.normal(ks[3], (E, C, H), dtype=jnp.float32) * (1.0 / np.sqrt(H)), 'w3': jax.random.normal(ks[4], (E, H, C), dtype=jnp.float32) * scale}
    _L0_ffn_all = _L0_ffn_setup()
    _L0_ffn_in = {k: v for k, v in _L0_ffn_all.items() if k in ('router_w', 'w1', 'w2', 'w3')}
    del _L0_ffn_all

    def _L1_gnn_setup():
        import jax, jax.numpy as jnp
        import numpy as np
        N_NODES = 50000
        N_EDGES = 50000
        IN_DIM, OUT_DIM, N_HEADS = (256, 64, 4)
        EPS = 1e-12
        key = jax.random.key(seed)
        k1, k2, k3, k4, k5 = jax.random.split(key, 5)
        h = jax.random.normal(k1, (N_NODES, IN_DIM), dtype=jnp.float32)
        edge_index = jax.random.randint(k2, (2, N_EDGES), 0, N_NODES, dtype=jnp.int32)
        W = jax.random.normal(k3, (IN_DIM, OUT_DIM), dtype=jnp.float32) * 0.05
        Wl = jax.random.normal(k4, (N_HEADS, OUT_DIM), dtype=jnp.float32) * 0.05
        Wr = jax.random.normal(k5, (N_HEADS, OUT_DIM), dtype=jnp.float32) * 0.05
        b = jnp.zeros((OUT_DIM,), dtype=jnp.float32)
        return {'h': h, 'W': W, 'Wl': Wl, 'Wr': Wr, 'b': b, 'edge_index': edge_index}
    _L1_gnn_all = _L1_gnn_setup()
    _L1_gnn_in = {k: v for k, v in _L1_gnn_all.items() if k in ('W', 'Wl', 'Wr', 'b')}
    del _L1_gnn_all

    def _L1_ffn_setup():
        import jax, jax.numpy as jnp
        import numpy as np
        B, S, D = (8, 128, 256)
        H = 4 * D
        CAPACITY = 0.5
        key = jax.random.key(seed)
        ks = jax.random.split(key, 6)
        x = jax.random.normal(ks[0], (B, S, D), dtype=jnp.float32)
        attention_mask = jnp.zeros((B, 1, 1, S), dtype=jnp.float32)
        wr = jax.random.normal(ks[1], (D, 1), dtype=jnp.float32) * 0.02
        br = jnp.zeros((1,), dtype=jnp.float32)
        w1 = jax.random.normal(ks[2], (D, H), dtype=jnp.float32) * 0.02
        b1 = jnp.zeros((H,), dtype=jnp.float32)
        w2 = jax.random.normal(ks[3], (H, D), dtype=jnp.float32) * 0.02
        b2 = jnp.zeros((D,), dtype=jnp.float32)
        return {'x': x, 'attention_mask': attention_mask, 'wr': wr, 'br': br, 'w1': w1, 'b1': b1, 'w2': w2, 'b2': b2}
    _L1_ffn_all = _L1_ffn_setup()
    _L1_ffn_in = {k: v for k, v in _L1_ffn_all.items() if k in ('attention_mask', 'wr', 'br', 'w1', 'b1', 'w2', 'b2')}
    del _L1_ffn_all
    return {'x': x, 'src': src, 'dst': dst, 'L0_gnn_eps': _L0_gnn_in['eps'], 'L0_gnn_W1': _L0_gnn_in['W1'], 'L0_gnn_b1': _L0_gnn_in['b1'], 'L0_gnn_g1': _L0_gnn_in['g1'], 'L0_gnn_beta1': _L0_gnn_in['beta1'], 'L0_gnn_W2': _L0_gnn_in['W2'], 'L0_gnn_b2': _L0_gnn_in['b2'], 'L0_gnn_g2': _L0_gnn_in['g2'], 'L0_gnn_beta2': _L0_gnn_in['beta2'], 'L0_gnn_W3': _L0_gnn_in['W3'], 'L0_gnn_b3': _L0_gnn_in['b3'], 'L0_gnn_g3': _L0_gnn_in['g3'], 'L0_gnn_beta3': _L0_gnn_in['beta3'], 'L0_gnn_W4': _L0_gnn_in['W4'], 'L0_gnn_b4': _L0_gnn_in['b4'], 'L0_ffn_router_w': _L0_ffn_in['router_w'], 'L0_ffn_w1': _L0_ffn_in['w1'], 'L0_ffn_w2': _L0_ffn_in['w2'], 'L0_ffn_w3': _L0_ffn_in['w3'], 'L1_gnn_W': _L1_gnn_in['W'], 'L1_gnn_Wl': _L1_gnn_in['Wl'], 'L1_gnn_Wr': _L1_gnn_in['Wr'], 'L1_gnn_b': _L1_gnn_in['b'], 'L1_ffn_attention_mask': _L1_ffn_in['attention_mask'], 'L1_ffn_wr': _L1_ffn_in['wr'], 'L1_ffn_br': _L1_ffn_in['br'], 'L1_ffn_w1': _L1_ffn_in['w1'], 'L1_ffn_b1': _L1_ffn_in['b1'], 'L1_ffn_w2': _L1_ffn_in['w2'], 'L1_ffn_b2': _L1_ffn_in['b2']}

def reference(x, src, dst, L0_gnn_eps, L0_gnn_W1, L0_gnn_b1, L0_gnn_g1, L0_gnn_beta1, L0_gnn_W2, L0_gnn_b2, L0_gnn_g2, L0_gnn_beta2, L0_gnn_W3, L0_gnn_b3, L0_gnn_g3, L0_gnn_beta3, L0_gnn_W4, L0_gnn_b4, L0_ffn_router_w, L0_ffn_w1, L0_ffn_w2, L0_ffn_w3, L1_gnn_W, L1_gnn_Wl, L1_gnn_Wr, L1_gnn_b, L1_ffn_attention_mask, L1_ffn_wr, L1_ffn_br, L1_ffn_w1, L1_ffn_b1, L1_ffn_w2, L1_ffn_b2):
    import jax
    import jax.numpy as jnp

    def _L0_gnn_ref(x, edge_index, eps, W1, b1, g1, beta1, W2, b2, g2, beta2, W3, b3, g3, beta3, W4, b4):
        import jax, jax.numpy as jnp
        import numpy as np
        BN_EPS = 1e-05
        CHANNELS = [256, 512, 1024, 512, 256]

        def _bn(h, gamma, beta):
            m = h.mean(axis=0)
            v = h.var(axis=0)
            return gamma * (h - m) * jax.lax.rsqrt(v + BN_EPS) + beta
        src, dst = (edge_index[0], edge_index[1])
        agg = jax.ops.segment_sum(x[src], dst, num_segments=x.shape[0])
        h = (1.0 + eps) * x + agg
        h = jax.nn.elu(_bn(h @ W1 + b1, g1, beta1))
        h = jax.nn.elu(_bn(h @ W2 + b2, g2, beta2))
        h = jax.nn.elu(_bn(h @ W3 + b3, g3, beta3))
        return h @ W4 + b4

    def _L0_ffn_ref(x, router_w, w1, w2, w3):
        import jax, jax.numpy as jnp
        import numpy as np
        N_EXPERTS = 8
        TOP_K = 2
        B, T, C = x.shape
        flat = x.reshape(-1, C)
        logits = flat @ router_w.T
        probs = jax.nn.softmax(logits, axis=-1)
        topk_probs, topk_idx = jax.lax.top_k(probs, TOP_K)
        topk_probs = topk_probs / (jnp.sum(topk_probs, axis=-1, keepdims=True) + 1e-09)
        onehot = jax.nn.one_hot(topk_idx, N_EXPERTS, dtype=flat.dtype)
        gates = jnp.einsum('nk,nke->ne', topk_probs, onehot)
        h1 = jnp.einsum('nc,ehc->neh', flat, w1)
        h3 = jnp.einsum('nc,ehc->neh', flat, w3)
        h = jax.nn.silu(h1) * h3
        y = jnp.einsum('neh,ech->nec', h, w2)
        out = jnp.einsum('ne,nec->nc', gates, y)
        return out.reshape(B, T, C)

    def _L1_gnn_ref(h, W, Wl, Wr, b, edge_index):
        import jax, jax.numpy as jnp
        import numpy as np
        N_NODES = 50000
        N_EDGES = 50000
        IN_DIM, OUT_DIM, N_HEADS = (256, 64, 4)
        EPS = 1e-12
        N = h.shape[0]
        H = Wl.shape[0]
        x = h @ W
        el = x @ Wl.T
        er = x @ Wr.T
        src, dst = (edge_index[0], edge_index[1])
        e = el[src] + er[dst]
        e = jnp.exp(jax.nn.leaky_relu(e, negative_slope=0.2))
        rowsum = jax.ops.segment_sum(e, src, num_segments=N)
        w = e / jnp.maximum(rowsum, EPS)[src]
        heads = [jax.ops.segment_sum(w[:, hd:hd + 1] * x[dst], src, num_segments=N) for hd in range(H)]
        out = jnp.stack(heads, axis=1)
        out = jax.nn.elu(out + b)
        return out.reshape(N, H * x.shape[1])

    def _L1_ffn_ref(x, attention_mask, wr, br, w1, b1, w2, b2):
        import jax, jax.numpy as jnp
        import numpy as np
        B, S, D = (8, 128, 256)
        H = 4 * D
        CAPACITY = 0.5
        b, s, d = x.shape
        weights = (jnp.einsum('bsd,do->bso', x, wr) + br)[..., 0]
        k = max(1, int(CAPACITY * s))
        kk = k - 1 if k > 1 else 1
        _, idx = jax.lax.top_k(weights, k)
        sel_idx = idx[:, :kk]
        sel = jnp.take_along_axis(x, sel_idx[:, :, None], axis=1)
        h = jax.nn.gelu(jnp.einsum('bkd,dh->bkh', sel, w1) + b1)
        y = jnp.einsum('bkh,hd->bkd', h, w2) + b2
        w_sel = jnp.take_along_axis(weights, sel_idx, axis=1)
        y = y * w_sel[..., None]
        batch_idx = jnp.arange(b)[:, None]
        processed = jnp.zeros_like(x).at[batch_idx, sel_idx].set(y)
        return processed + x
    edge_index = jnp.stack([src, dst])
    x = x + _L0_gnn_ref(_layernorm(x, axis=-1), edge_index, L0_gnn_eps, L0_gnn_W1, L0_gnn_b1, L0_gnn_g1, L0_gnn_beta1, L0_gnn_W2, L0_gnn_b2, L0_gnn_g2, L0_gnn_beta2, L0_gnn_W3, L0_gnn_b3, L0_gnn_g3, L0_gnn_beta3, L0_gnn_W4, L0_gnn_b4)
    x = x + _L0_ffn_ref(_layernorm(x, axis=-1)[None], L0_ffn_router_w, L0_ffn_w1, L0_ffn_w2, L0_ffn_w3)[0]
    x = x + _L1_gnn_ref(_layernorm(x, axis=-1), L1_gnn_W, L1_gnn_Wl, L1_gnn_Wr, L1_gnn_b, edge_index)
    x = x + _L1_ffn_ref(_layernorm(x, axis=-1)[None], L1_ffn_attention_mask, L1_ffn_wr, L1_ffn_br, L1_ffn_w1, L1_ffn_b1, L1_ffn_w2, L1_ffn_b2)[0]
    return x

_drawn_inputs = setup_inputs


def setup_inputs(seed=0):
    import zlib

    import numpy as np

    out = dict(_drawn_inputs(seed))
    spreads = {'L0_gnn_b1': (0.0, 0.8),
     'L0_gnn_g1': (1.0, 0.2),
     'L0_gnn_beta1': (0.0, 0.1),
     'L0_gnn_b2': (0.0, 0.8),
     'L0_gnn_g2': (1.0, 0.2),
     'L0_gnn_beta2': (0.0, 0.1),
     'L0_gnn_b3': (0.0, 0.8),
     'L0_gnn_g3': (1.0, 0.2),
     'L0_gnn_beta3': (0.0, 0.1),
     'L0_gnn_b4': (0.0, 0.1),
     'L1_gnn_b': (0.0, 0.1),
     'L1_ffn_b1': (0.0, 0.8),
     'L1_ffn_b2': (0.0, 0.694)}
    factors = {'L1_gnn_Wl': 5.433, 'L1_ffn_wr': 4.362, 'L1_ffn_w1': 4.805, 'L1_ffn_w2': 4.501}
    for name, (base, spread) in spreads.items():
        noise = np.random.default_rng([zlib.crc32(name.encode()), seed]).standard_normal(out[name].shape)
        drawn = base * np.exp(spread * noise) if base else spread * noise
        out[name] = jnp.asarray(drawn.astype(out[name].dtype))
    for name, factor in factors.items():
        out[name] = (out[name] * factor).astype(out[name].dtype)
    return out
```

```python
from contextlib import ExitStack

import concourse.bass as bass
from concourse import mybir

F32 = mybir.dt.float32
F16 = mybir.dt.float16
I32 = mybir.dt.int32
U32 = mybir.dt.uint32
ALU = mybir.AluOpType
ACT = mybir.ActivationFunctionType
AX_X = mybir.AxisListType.X
RMAX = bass.bass_isa.ReduceOp.max

N = 3125
D = 256
E = 50000
PB = 125
NB = N // PB
ET = 128
TPR = 8
HT = TPR // 2
R1 = -(-E // (ET * TPR))
T1 = R1 * TPR
R3 = (T1 * ET + NB * (ET - 1)) // ET // TPR
T3 = R3 * TPR
WIN = 128
X = 8
K2 = 2
HM = 6
HP = HM * 128
T2 = (K2 * N + X * 127) // 128
XS = 256.0
WS = 1024.0
HS = 64.0
NACC = N + WIN
NH, OD = 4, 64
RW = NH + OD + 1
FH = 1024
LN_EPS = 1e-5
BN_EPS = 1e-5
MAGIC = 1.5 * 2.0 ** 23
assert T3 * ET >= T1 * ET + NB * (ET - 1) - ET + 1 and NB * PB == N


VECTORS = [f"L0_gnn_{v}{l}" for v in ("b", "g", "beta") for l in (1, 2, 3)]


def wait_apart(eng, sem, value, tick):
    eng.wait_ge(sem, value)
    eng.sem_inc(tick, 1)


def loop(nc, eng, start, end):
    return nc.Fori(start, end, engines=[eng.engine], hint_back_edge=True)


def registers(nc, eng, values, top):
    return nc.values_load_multi_w_load_instructions(
        values, engines=[eng.engine], min_val=0, max_val=top,
        skip_runtime_bounds_check_because="the kernel clamps them where it computes them")[1]


class Chain:

    def __init__(self, eng, sem):
        self.eng, self.sem, self.n = eng, sem, 0

    def mark(self, ins):
        ins.then_inc(self.sem, 1)
        self.n += 1

    def step(self, ins):
        self.mark(ins)
        self.eng.wait_ge(self.sem, self.n)


def program(nc, a, out):
    with ExitStack() as ctx:
        taken = []

        def sem(name):
            taken.append(nc.alloc_semaphore(name))
            return taken[-1]

        def free_semaphores():
            nc.clear_and_free_semaphores(taken)
            nc.all_engine_barrier()
            taken.clear()

        def psum(name, shape, dt=F32):
            return ctx.enter_context(nc.psum_tensor(name, shape, dt))

        KB = 1024
        BASE = 16512

        def at(name, offset, shape, dt=F32):
            return nc.alloc_sbuf_tensor_at(name, shape, dt, offset=BASE + offset)

        def dram(name, shape, dt=F32):
            return nc.dram_tensor(name, shape, dt, kind="Internal").ap()

        xn_d = dram("xn_d", (N, D))
        rec_d = dram("rec_d", (ET, T3 * 2), I32)

        ident = at("ident", 0, [128, 128])
        iota = at("iota", 512, [128, 128])
        rec = at("rec", 1 * KB, [128, T1, 2], I32)
        kb = at("kb", 1 * KB + 3136, [128, T1])
        accT = at("accT", 6 * KB, [128, 2, NACC])
        s_c = [sem(f"s_c{i}") for i in range(4)]

        W2 = at("W2", 158 * KB, [128, 2, 4, 1024], F16)
        W3 = at("W3", 174 * KB, [128, 2, 8, 512], F16)
        W1 = at("W1", 190 * KB, [128, 2, 512])
        W4 = at("W4", 194 * KB, [128, 2, 4, 256], F16)
        pieces = []
        for r in range(4):
            pieces.append((a["L0_gnn_W2"][128 * r:128 * (r + 1), :], [W2[:, s, r, :] for s in range(2)], 1024))
        for r in range(4):
            pieces.append((a["L0_gnn_W3"].rearrange("(k p) n -> p k n", p=128)[:, 2 * r:2 * r + 2, :],
                           [W3[:, s, 2 * r:2 * r + 2, :] for s in range(2)], 512))
        pieces.append((a["L0_gnn_W4"].rearrange("(k p) n -> p k n", p=128), [W4[:, s, :, :] for s in range(2)], 256))

        def staged(n):
            t, w = wst[:, n % 2, :], pieces[n][2]
            return t if w == 1024 else t.rearrange("p (k n) -> p k n", n=w)

        VAT = (0, 1, 3, 4)
        vec = at("vec", 206 * KB, [128, 3, 16])
        s_vec = sem("s_vec")
        s_w1 = sem("s_w1")
        s_wst = [sem(f"s_wst{i}") for i in range(2)]
        s_whi = sem("s_whi")
        s_wlo = sem("s_wlo")
        s_rec0 = sem("s_rec0")
        s_recst = sem("s_recst")
        s_rank = sem("s_rank")

        o = 104 * KB
        S = at("S", 33 * KB, [128, NB, T1])
        same = at("same", 72 * KB, [128, NB, T1], F16)
        wst = at("wst", 92 * KB, [128, 2, 1024])
        rec0 = at("rec0", 198 * KB, [128, T3 * 2], I32)
        x = at("x", o, [PB, NB, D]); o += 25600
        G = at("G", o, [128, TPR, D]); o += 8192
        oh = at("oh", 202 * KB, [128, TPR, WIN])
        src_i = at("src_i", o, [128, T1], I32); o += 1568
        dst_i = at("dst_i", o, [128, T1], I32); o += 1568
        gat_i = at("gat_i", o, [128, T1], I32); o += 1568
        srcf = at("srcf", o, [128, T1]); o += 1568
        tmpf = at("tmpf", o, [128, T1]); o += 1568
        span = at("span", o, [128, 2, T1]); o += 3136
        spanr = at("spanr", 100 * KB, [128, 2, T1])
        dstw = at("dstw", o, [128, T1 + TPR]); o += 1600
        basef = at("basef", o, [128, T1]); o += 1568
        base_i = at("base_i", o, [1, T1], I32); o += 1568
        stage_i = at("stage_i", o, [128, 2, HT], I32); o += 32
        bst = at("bst", o, [PB, NB, 6]); o += 608
        mv = at("mv", o, [PB, NB, 2]); o += 224
        std = at("std", o, [PB, NB]); o += 128
        rstd = at("rstd", o, [PB, NB]); o += 128
        eps1 = at("eps1", o, [128, 1]); o += 32
        nwf = at("nwf", o, [128, 8]); o += 32
        nw_i = at("nw_i", o, [128, 8], I32); o += 32

        assert o <= 158 * KB
        s_x = [sem(f"s_x{c}") for c in range(5)]
        s_edges = sem("s_edges")
        s_eps = sem("s_eps")
        s_const = sem("s_const")
        s_var = sem("s_var")
        s_std = sem("s_std")
        s_xn = sem("s_xn")
        s_xnst = sem("s_xnst")
        s_tr = sem("s_tr")
        s_trc = sem("s_trc")
        s_eps1 = sem("s_eps1")
        s_span = sem("s_span")
        s_spanr = sem("s_spanr")
        s_idx = sem("s_idx")
        s_nw = sem("s_nw")
        s_pad = sem("s_pad")
        s_staged = sem("s_staged")
        s_gat = [sem(f"s_gat{i}") for i in range(TPR)]
        s_oh = [sem("s_ohA"), sem("s_ohB")]
        s_slots = sem("s_slots")
        s_banks = sem("s_banks")
        s_pass = sem("s_pass")
        s_halves = sem("s_halves")
        s_tick = [sem("s_tick_act"), sem("s_tick_dve"), sem("s_tick_pe"), sem("s_tick_sp")]

        GRP = [(q, min(4, NB - q)) for q in range(0, NB, 4)]

        with ExitStack() as p1:
            psT = [p1.enter_context(nc.psum_tensor(f"psT{i}", [128, 4 * PB], F32)) for i in range(2)]
            psA = [p1.enter_context(nc.psum_tensor(f"psA{i}", [128, 2, 2, WIN], F32)) for i in range(4)]
            block = p1.enter_context(nc.Block())
            CH = NB // 5

            def store_xn(sp):
                for c in range(5):
                    sp.wait_ge(s_xn, CH * (c + 1))
                    sp.dma_start(xn_d.rearrange("(b p) d -> p b d", p=PB)[:, CH * c:CH * (c + 1), :],
                                 x[:, CH * c:CH * (c + 1), :]).then_inc(s_xnst, 16)

            @block.sync
            def _(sp):
                for c in range(5):
                    sp.dma_start(x[:, CH * c:CH * (c + 1), :],
                                 a["x"].rearrange("(b p) d -> p b d", p=PB)[:, CH * c:CH * (c + 1), :]).then_inc(s_x[c], 16)
                sp.dma_start(src_i[:, :], a["src"]).then_inc(s_edges, 16)
                sp.dma_start(dst_i[:, :], a["dst"]).then_inc(s_edges, 16)
                sp.dma_start(eps1[:, :], a["L0_gnn_eps"].partition_broadcast(128)).then_inc(s_eps, 16)
                sp.dma_start(W1[:, :, :], a["L0_gnn_W1"].rearrange("(k p) n -> p k n", p=128)).then_inc(s_w1, 16)
                for n in range(len(pieces)):
                    if n == 2:
                        store_xn(sp)
                    if n >= 2:
                        sp.wait_ge(s_wlo, n - 1)
                    sp.dma_start(staged(n), pieces[n][0]).then_inc(s_wst[n % 2], 16)
                sp.wait_ge(s_rec0, 1)
                sp.dma_start(rec_d, rec0[:, :]).then_inc(s_recst, 16)
                for l in range(3):
                    for j, name in enumerate(("b", "g", "beta")):
                        sp.dma_start(vec[:, j, 4 * VAT[l]:4 * VAT[l + 1]], a[f"L0_gnn_{name}{l + 1}"]).then_inc(s_vec, 16)

            @block.gpsimd
            def _(pool):
                ch = Chain(pool, s_c[0])
                nc.gpsimd.iota(iota[:, :], pattern=[[1, 128]], base=0, channel_multiplier=0,
                               allow_small_or_imprecise_dtypes=True).then_inc(s_const, 1)
                ch.step(nc.gpsimd.memset(ident[:, :], 0.0))
                nc.gpsimd.affine_select(out=ident[:, :], in_=ident[:, :], compare_op=ALU.not_equal, fill=1.0,
                                        base=0, pattern=[[-1, 128]], channel_multiplier=1).then_inc(s_const, 1)
                nc.gpsimd.memset(accT[:, :, N:NACC], 0.0).then_inc(s_pad, 1)
                nc.gpsimd.memset(rec0[:, :], PB).then_inc(s_rec0, 1)
                pool.wait_ge(s_span, 1)
                nc.gpsimd.partition_all_reduce(spanr[:, :, :].rearrange("p a t -> p (a t)"),
                                               span[:, :, :].rearrange("p a t -> p (a t)"), 128, RMAX).then_inc(s_spanr, 1)
                pool.wait_ge(s_nw, 1)
                nw = pool.value_load(nw_i[0:1, 0:1], min_val=1, max_val=NB)
                pool.wait_ge(s_idx, 1)
                pool.wait_ge(s_xnst, 80)
                with loop(nc, pool, 0, nw) as w:
                    with loop(nc, pool, 0, R1) as g:
                        it = w * R1 + g
                        for h in range(2):
                            pool.wait_ge(s_slots, it * TPR + HT * (h + 1))
                            nc.gpsimd.tensor_copy(stage_i[:, h, :], gat_i[:, bass.ds(g * TPR + h * HT, HT)]).then_inc(s_staged, 1)
                            pool.wait_ge(s_staged, it * 2 + h + 1)
                            pool.sem_inc(s_halves, 1)
                            for j in range(HT):
                                i = h * HT + j
                                pool.indirect_dma_start(
                                    out=G[:, i, :], out_offset=None, in_=xn_d,
                                    in_offset=bass.IndirectOffsetOnAxis(ap=stage_i[:, h, j:j + 1], axis=0)).then_inc(s_gat[i], 16)

            @block.scalar
            def _(act):
                for c in range(5):
                    act.wait_ge(s_var, c + 1)
                    nc.scalar.activation(std[:, CH * c:CH * (c + 1)], mv[:, CH * c:CH * (c + 1), 1], ACT.Sqrt).then_inc(s_std, 1)
                for n in range(len(pieces)):
                    act.wait_ge(s_wst[n % 2], 16 * (n // 2 + 1))
                    nc.scalar.activation(pieces[n][1][0], staged(n), ACT.Copy, scale=WS).then_inc(s_whi, 1)
                act.wait_ge(s_eps1, 1)
                for q, (b0, n) in enumerate(GRP):
                    for h in range(2):
                        act.wait_ge(s_tr, 2 * q + h + 1)
                        nc.scalar.activation(accT[:, h, PB * b0:PB * (b0 + n)], psT[h][:, 0:PB * n], ACT.Copy,
                                             scale=eps1[:, :]).then_inc(s_trc, 1)

            @block.vector
            def _(dve):
                ch = Chain(dve, s_c[1])
                dve.wait_ge(s_edges, 32)
                nc.vector.tensor_copy(span[:, 1, :], dst_i[:, :])
                ch.step(nc.vector.tensor_copy(srcf[:, :], src_i[:, :]))
                ch.step(nc.vector.tensor_scalar(span[:, 0, :], span[:, 1, :], -1.0, None, ALU.mult))
                dve.sem_inc(s_span, 1)
                ch.step(nc.vector.tensor_scalar(tmpf[:, :], srcf[:, :], float(N - 1), None, ALU.min))
                nc.vector.tensor_copy(gat_i[:, :], tmpf[:, :]).then_inc(s_idx, 1)
                ch.step(nc.vector.tensor_scalar(kb[:, :], srcf[:, :], 1.0 / PB, -(PB // 2 * 1.0) / PB, ALU.mult, ALU.add))
                ch.step(nc.vector.tensor_scalar(kb[:, :], kb[:, :], MAGIC, MAGIC, ALU.add, ALU.subtract))
                ch.step(nc.vector.tensor_scalar(kb[:, :], kb[:, :], float(NB - 1), None, ALU.min))
                ch.step(nc.vector.scalar_tensor_tensor(tmpf[:, :], kb[:, :], -float(PB), srcf[:, :], ALU.mult, ALU.add))
                nc.vector.tensor_copy(rec[:, :, 0], tmpf[:, :])
                ch.step(nc.vector.tensor_scalar(rec[:, :, 1], span[:, 1, :], float(N - 1), None, ALU.min))
                dve.wait_ge(s_eps, 16)
                nc.vector.tensor_scalar(eps1[:, :], eps1[:, :], 1.0, None, ALU.add).then_inc(s_eps1, 1)
                for c in range(5):
                    dve.wait_ge(s_x[c], 16)
                    for b in range(CH * c, CH * (c + 1)):
                        ch.mark(nc.vector.bn_stats(bst[:, b, :], x[:, b, :]))
                    dve.wait_ge(ch.sem, ch.n)
                    for b in range(CH * c, CH * (c + 1)):
                        ch.mark(nc.vector.bn_aggr(mv[:, b, :], bst[:, b, :]))
                    dve.wait_ge(ch.sem, ch.n)
                    cs = slice(CH * c, CH * (c + 1))
                    nc.vector.tensor_scalar(mv[:, cs, 1], mv[:, cs, 1], LN_EPS, None, ALU.add).then_inc(s_var, 1)
                    dve.wait_ge(s_std, c + 1)
                    ch.step(nc.vector.reciprocal(rstd[:, cs], std[:, cs]))
                    for b in range(CH * c, CH * (c + 1)):
                        nc.vector.tensor_scalar(x[:, b, :], x[:, b, :], mv[:, b, 0:1], rstd[:, b:b + 1],
                                                ALU.subtract, ALU.mult).then_inc(s_xn, 1)
                dve.wait_ge(s_spanr, 1)
                ch.step(nc.vector.tensor_tensor(tmpf[:, :], spanr[:, 0, :], spanr[:, 1, :], ALU.add))
                ch.step(nc.vector.tensor_reduce(nwf[:, 0:1], tmpf[:, :], AX_X, ALU.max))
                ch.step(nc.vector.tensor_copy(nw_i[:, 1:2], nwf[:, 0:1]))
                ch.step(nc.vector.tensor_scalar(nw_i[:, 2:3], nw_i[:, 1:2], WIN.bit_length() - 1, None, ALU.arith_shift_right))
                nc.vector.tensor_scalar(nw_i[:, 0:1], nw_i[:, 2:3], 1.0, None, ALU.add).then_inc(s_nw, 1)
                nc.vector.memset(dstw[:, T1:T1 + TPR], -1.0)
                nc.vector.tensor_scalar(basef[:, :], spanr[:, 0, :], -1.0, -float(WIN), ALU.mult, ALU.add)
                ch.step(nc.vector.tensor_tensor(dstw[:, 0:T1], span[:, 1, :], spanr[:, 0, :], ALU.add))
                ch.step(nc.vector.tensor_scalar(dstw[:, 0:T1], dstw[:, 0:T1], float(WIN), None, ALU.add))
                dve.wait_ge(s_nw, 1)
                nw = dve.value_load(nw_i[0:1, 0:1], min_val=1, max_val=NB)
                for n in range(len(pieces)):
                    dve.wait_ge(s_whi, n + 1)
                    nc.vector.scalar_tensor_tensor(pieces[n][1][1], staged(n), WS, pieces[n][1][0],
                                                   ALU.mult, ALU.subtract).then_inc(s_wlo, 1)
                dve.wait_ge(s_const, 2)
                dve.wait_ge(s_trc, 2 * len(GRP))
                dve.wait_ge(s_pad, 1)
                dve.sem_inc(s_banks, TPR)

                def one_hots(h, col):
                    nc.vector.tensor_tensor(
                        oh[:, h * HT:(h + 1) * HT, :],
                        iota[:, :].unsqueeze(1).to_broadcast([128, HT, WIN]),
                        dstw[:, bass.ds(col, HT)].unsqueeze(2).to_broadcast([128, HT, WIN]),
                        ALU.is_equal).then_inc(s_oh[h], 1)

                with loop(nc, dve, 0, nw) as w:
                    nc.vector.tensor_scalar(dstw[:, 0:T1], dstw[:, 0:T1], -float(WIN), None, ALU.add)
                    nc.vector.tensor_scalar(basef[:, :], basef[:, :], float(WIN), None, ALU.add).then_inc(s_pass, 1)
                    dve.wait_ge(s_pass, w * 2 + 1)
                    nc.vector.tensor_scalar(base_i[:, :], basef[0:1, :], float(N), None, ALU.min).then_inc(s_pass, 1)
                    dve.wait_ge(s_pass, w * 2 + 2)
                    dve.wait_ge(s_slots, w * (R1 * TPR) + TPR)
                    one_hots(0, 0)

                    def round_(g, rank):
                        it = w * R1 + g
                        if rank:
                            nc.vector.tensor_scalar(same[:, bass.ds(g, 1), :].rearrange("p a t -> p (a t)"), kb[:, :],
                                                    iota[:, bass.ds(g, 1)], None, ALU.is_equal).then_inc(s_rank, 1)
                        at_ = registers(nc, dve, base_i[0:1, bass.ds(g * TPR, TPR)], N)
                        dve.wait_ge(s_slots, it * TPR + TPR)
                        one_hots(1, g * TPR + HT)
                        for i in range(TPR):
                            if i == HT:
                                one_hots(0, g * TPR + TPR)
                            if i % 2 == 0:
                                dve.wait_ge(s_slots, it * TPR + TPR + i + 2)
                            dve.wait_ge(s_banks, it * TPR + TPR + i)
                            nc.vector.tensor_tensor(accT[:, :, bass.ds(at_[i], WIN)], accT[:, :, bass.ds(at_[i], WIN)],
                                                    psA[i // 2][:, i % 2, :, :], ALU.add).then_inc(s_banks, 1)
                        if rank:
                            dve.wait_ge(s_rank, w * NB + g + 1)
                            flat = same[:, bass.ds(g, 1), :].rearrange("p a t -> p (a t)")
                            nc.vector.tensor_tensor_scan(S[:, bass.ds(g, 1), :].rearrange("p a t -> p (a t)"),
                                                         flat, flat, 0.0, ALU.add, ALU.max)

                    with loop(nc, dve, 0, NB) as g:
                        round_(g, True)
                    with loop(nc, dve, NB, R1) as g:
                        round_(g, False)

            @block.tensor
            def _(pe):
                pe.wait_ge(s_const, 2)
                for q, (b0, n) in enumerate(GRP):
                    for h in range(2):
                        pe.wait_ge(s_xn, b0 + n)
                        if q:
                            pe.wait_ge(s_trc, 2 * q - 1 + h)
                        for b in range(n):
                            last = nc.tensor.transpose(psT[h][:, PB * b:PB * (b + 1)], x[:, b0 + b, 128 * h:128 * (h + 1)],
                                                       ident[0:PB, 0:PB])
                        last.then_inc(s_tr, 1)
                pe.wait_ge(s_nw, 1)
                nw = pe.value_load(nw_i[0:1, 0:1], min_val=1, max_val=NB)
                pe.sem_inc(s_slots, TPR)
                with loop(nc, pe, 0, nw) as w:
                    with loop(nc, pe, 0, R1) as g:
                        it = w * R1 + g
                        for i in range(TPR):
                            pe.wait_ge(s_gat[i], it * 16 + 16)
                            if i % HT == 0:
                                if i == 0:
                                    pe.wait_ge(s_oh[0], it + w + 1)
                                else:
                                    pe.wait_ge(s_oh[1], it + 1)
                            if i % 2 == 0:
                                pe.wait_ge(s_banks, it * TPR + i + 2)
                            for h in range(2):
                                last = nc.tensor.matmul(psA[i // 2][:, i % 2, h, :], G[:, i, 128 * h:128 * (h + 1)],
                                                        oh[:, i, :], start=True, stop=True)
                            last.then_inc(s_slots, 1)

        z2 = at("z2", 6 * KB, [128, 8, N])
        z1 = at("z1", 104 * KB, [128, 4, N])
        eb = at("eb", 198 * KB, [128, 2, 500])
        yb = at("yb", 202 * KB, [128, 2, 500])
        bst2 = at("bst2", 206 * KB + 192, [128, 8, 7, 6])
        mv2 = at("mv2", 206 * KB + 1536, [128, 8, 2])
        cf = at("cf", 206 * KB + 1600, [128, 3, 8])
        x2 = at("x2", 6 * KB, [PB, NB, D])
        b4 = at("b4", 33 * KB, [PB, D])
        ones16 = at("ones16", 158 * KB, [128, 128], F16)
        later = at("later", 92 * KB, [128, 128])
        ones = at("ones", 92 * KB + 512, [128, 128])
        pos = at("pos", 94 * KB, [128, T1])
        pos_i = at("pos_i", 96 * KB, [128, T1], I32)
        row_i = at("row_i", 98 * KB, [128, T1], I32)
        iotaT = at("iotaT", 100 * KB, [1, T3])
        gr = at("gr", 102 * KB, [128, 4, NB])
        gr_i = at("gr_i", 102 * KB + 512, [128, 2, NB], I32)
        behind = at("behind", 72 * KB, [1, T3, NB], F16)
        blk_i = at("blk_i", 94 * KB, [1, T3], I32)
        posd = at("posd", 1 * KB + 3136, [128, T1], I32)
        stp = at("stp", 206 * KB + 1696, [128, 2, HT], I32)
        str_ = at("str_", 206 * KB + 1728, [128, 2, HT, 2], I32)
        blk_d = dram("blk_d", (1, T3), I32)

        s_c2 = [sem(f"s_c2{i}") for i in range(4)]
        s_k2 = sem("s_k2")
        s_cnt = sem("s_cnt")
        s_pos = sem("s_pos")
        s_blk = sem("s_blk")
        s_blkst = sem("s_blkst")
        s_stg = sem("s_stg")
        s_sc = [sem("s_sc0"), sem("s_sc1")]
        s_sq = sem("s_sq")
        s_sd = sem("s_sd")
        s_cf = sem("s_cf")
        s_mm = [sem(f"s_mm{l}") for l in range(4)]
        s_ev = [sem(f"s_ev{l}") for l in range(4)]
        s_e = [None] + [sem(f"s_e{l}") for l in range(1, 4)]
        s_u = [None] + [sem(f"s_u{l}") for l in range(1, 4)]
        s_hi = [None] + [sem(f"s_hi{l}") for l in range(1, 4)]
        s_h = [None] + [sem(f"s_h{l}") for l in range(1, 4)]
        s_y = [None] + [sem(f"s_y{l}") for l in range(1, 4)]
        s_st = sem("s_st")
        s_xr = sem("s_xr")
        s_b4 = sem("s_b4")
        s_b4c = sem("s_b4c")
        s_ones16 = sem("s_ones16")

        ZIN = [accT, z1, z2, z1]
        ZOUT = [z1, z2, z1, None]
        KR = [2, 4, 8, 4]
        MR = [4, 8, 4, 2]
        CW, CN = 4 * PB, 6
        with ExitStack() as p2:
            psZ = [p2.enter_context(nc.psum_tensor(f"psZ{i}", [128, 500], F32)) for i in range(4)]
            psR = p2.enter_context(nc.psum_tensor("psR", [128, 512], F32))
            psO = [p2.enter_context(nc.psum_tensor(f"psO{i}", [PB, 2, D], F32)) for i in range(2)]
            block = p2.enter_context(nc.Block())

            def halves(l, k, c0, w):
                f = ZIN[l][:, k, :].bitcast(F16)
                return f[:, bass.ds(c0 * 2, w)], f[:, bass.ds(c0 * 2 + w, w)]

            @block.sync
            def _(sp):
                sp.wait_ge(s_blk, 1)
                sp.dma_start(blk_d, blk_i[:, :]).then_inc(s_blkst, 16)
                sp.wait_ge(s_mm[2], 4 * 7)
                sp.dma_start(x2[:, :, :], a["x"].rearrange("(b p) d -> p b d", p=PB)).then_inc(s_xr, 16)
                sp.dma_start(b4[:, :], a["L0_gnn_b4"].partition_broadcast(PB)).then_inc(s_b4, 16)
                sp.wait_ge(s_blkst, 16)

            @block.gpsimd
            def _(pool):
                ch = Chain(pool, s_c2[0])
                nc.gpsimd.memset(ones[:, :], 1.0)
                ch.step(nc.gpsimd.memset(later[:, :], 1.0))
                ch.step(nc.gpsimd.affine_select(out=later[:, :], in_=later[:, :], compare_op=ALU.is_gt, fill=0.0,
                                                base=0, pattern=[[1, 128]], channel_multiplier=-1))
                ch.step(nc.gpsimd.iota(iotaT[:, :], pattern=[[1, T3]], base=0, channel_multiplier=0,
                                       allow_small_or_imprecise_dtypes=True))
                pool.sem_inc(s_k2, 1)
                recs = rec_d.rearrange("p (t r) -> (p t) r", r=2)
                pool.wait_ge(s_recst, 16)
                pool.wait_ge(s_pos, 1)

                def stage(g, h):
                    nc.gpsimd.tensor_copy(stp[:, h, :], posd[:, bass.ds(g * TPR + h * HT, HT)])
                    nc.gpsimd.tensor_copy(str_[:, h, :, :], rec[:, bass.ds(g * TPR + h * HT, HT), :]).then_inc(s_stg, 1)
                    pool.wait_ge(s_stg, g * 2 + h + 1)
                    pool.sem_inc(s_halves, 1)
                    for j in range(HT):
                        pool.indirect_dma_start(
                            out=recs, out_offset=bass.IndirectOffsetOnAxis(ap=stp[:, h, j:j + 1], axis=0),
                            in_=str_[:, h, j, :], in_offset=None).then_inc(s_sc[h], 16)

                stage(0, 0)
                stage(0, 1)
                with loop(nc, pool, 1, R1) as g:
                    for h in range(2):
                        pool.wait_ge(s_sc[h], g * (16 * HT))
                        stage(g, h)
                for h in range(2):
                    pool.wait_ge(s_sc[h], 16 * HT * R1)

            def rows_of(l, m):
                k, n = KR[l], MR[l]
                return [r for r in range(k) if r * n // k == m] if k >= n else ([m * k // n] if m * k % n == n - k else [])

            @block.scalar
            def _(act):
                act.wait_ge(s_vec, 16 * 9)

                def evac(l, m, c, w):
                    wait_apart(act, s_mm[l], c * MR[l] + m + 1, s_tick[0])
                    nc.scalar.activation(ZOUT[l][:, m, bass.ds(c * CW, w)], psZ[m % 4][:, 0:w], ACT.Identity,
                                         bias=vec[:, 0, 4 * VAT[l] + m:4 * VAT[l] + m + 1],
                                         scale=1.0 if l == 0 else 1.0 / (WS * HS)).then_inc(s_ev[l], 1)

                def row(l, k, c, w):
                    r = c * KR[l] + k
                    zin = ZIN[l][:, k, bass.ds(c * CW, w)]
                    wait_apart(act, s_u[l], r + 1, s_tick[0])
                    nc.scalar.activation(eb[:, k % 2, 0:w], zin, ACT.Exp, bias=cf[:, 1, k:k + 1],
                                         scale=cf[:, 0, k:k + 1]).then_inc(s_e[l], 1)
                    wait_apart(act, s_h[l], r + 1, s_tick[0])
                    nc.scalar.activation(yb[:, k % 2, 0:w], zin, ACT.Identity, bias=cf[:, 2, k:k + 1],
                                         scale=cf[:, 0, k:k + 1]).then_inc(s_y[l], 1)

                def layer(l):
                    def chunk(c, w, nw):
                        for m in range(MR[l]):
                            if l < 3:
                                evac(l, m, c, w)
                            if nw and l:
                                for k in rows_of(l, m):
                                    row(l, k, c + 1, nw)
                    if l == 1:
                        act.wait_ge(s_blkst, 16)
                    if l:
                        act.wait_ge(s_sq, l)
                        nc.scalar.activation(mv2[:, 0:KR[l], 1], mv2[:, 0:KR[l], 1], ACT.Sqrt).then_inc(s_sd, 1)
                        act.wait_ge(s_cf, l)
                        for k in range(KR[l]):
                            row(l, k, 0, CW)
                    with loop(nc, act, 0, CN - 1) as c:
                        chunk(c, CW, CW)
                    chunk(CN - 1, CW, PB)
                    chunk(CN, PB, 0)

                for l in range(4):
                    layer(l)

            @block.vector
            def _(dve):
                ch = Chain(dve, s_c2[1])
                dve.wait_ge(s_cnt, 1)
                ch.step(nc.vector.tensor_scalar(gr_i[:, 0, :], psR[:, 32:32 + NB], ET - 1.0, None, ALU.add))
                ch.step(nc.vector.tensor_scalar(gr_i[:, 1, :], gr_i[:, 0, :], 7, None, ALU.arith_shift_right))
                ch.step(nc.vector.tensor_copy(gr[:, 0, :], gr_i[:, 1, :]))
                ch.step(nc.vector.tensor_tensor_scan(gr[:, 1, :], gr[:, 0, :], gr[:, 0, :], 0.0, ALU.add, ALU.max))
                ch.step(nc.vector.tensor_tensor(gr[:, 3, :], gr[:, 1, :], gr[:, 0, :], ALU.subtract))
                ch.step(nc.vector.tensor_scalar(gr[:, 3, :], gr[:, 3, :], float(ET), -1.0, ALU.mult, ALU.add))
                ch.step(nc.vector.tensor_tensor(gr[:, 2, :], gr[:, 3, :], psR[:, 0:NB], ALU.add))
                ch.step(nc.vector.tensor_tensor(S[:, :, :], S[:, :, :],
                                                gr[:, 2, :].unsqueeze(2).to_broadcast([128, NB, T1]), ALU.add))
                ch.step(nc.vector.tensor_tensor(S[:, :, :], S[:, :, :], same[:, :, :], ALU.mult))
                ch.step(nc.vector.tensor_reduce(pos[:, :], S[:, :, :].rearrange("p k t -> p t k"), AX_X, ALU.add))
                ch.step(nc.vector.tensor_copy(pos_i[:, :], pos[:, :]))
                nc.vector.tensor_scalar(row_i[:, :], pos_i[:, :], ET - 1, None, ALU.bitwise_and)
                ch.step(nc.vector.tensor_scalar(pos_i[:, :], pos_i[:, :], 7, None, ALU.arith_shift_right))
                nc.vector.scalar_tensor_tensor(posd[:, :], row_i[:, :], float(T3), pos_i[:, :], ALU.mult, ALU.add).then_inc(s_pos, 1)
                dve.wait_ge(s_k2, 1)
                ch.step(nc.vector.tensor_tensor(behind[:, :, :], iotaT[:, :].unsqueeze(2).to_broadcast([1, T3, NB]),
                                                gr[0:1, 1, :].unsqueeze(1).to_broadcast([1, T3, NB]), ALU.is_ge))
                ch.step(nc.vector.tensor_reduce(iotaT[:, :], behind[:, :, :], AX_X, ALU.add))
                nc.vector.tensor_scalar(blk_i[:, :], iotaT[:, :], NB - 1.0, None, ALU.min).then_inc(s_blk, 1)

                def stats(l, m, c, ci, w):
                    wait_apart(dve, s_ev[l], c * MR[l] + m + 5, s_tick[1])
                    if isinstance(ci, int):
                        o_ = bst2[:, m, ci, :]
                    else:
                        o_ = bst2[:, m, bass.ds(ci, 1), :].rearrange("p a s -> p (a s)")
                    nc.vector.bn_stats(o_, ZOUT[l][:, m, bass.ds(c * CW, w)]).then_inc(s_st, 1)

                def row(l, k, c, w):
                    r = c * KR[l] + k
                    u = yb[:, k % 2, 0:w]
                    hi, lo = halves(l, k, c * CW, w)
                    dve.wait_ge(s_y[l], r + 1)
                    dve.wait_ge(s_e[l], r + 1)
                    nc.vector.scalar_tensor_tensor(u, eb[:, k % 2, 0:w], 1.0, u, ALU.min, ALU.max).then_inc(s_u[l], 1)
                    dve.wait_ge(s_u[l], r + 3)
                    nc.vector.tensor_scalar(hi, u, HS, None, ALU.mult).then_inc(s_hi[l], 1)
                    dve.wait_ge(s_hi[l], r + 1)
                    nc.vector.scalar_tensor_tensor(lo, u, HS, hi, ALU.mult, ALU.subtract).then_inc(s_h[l], 1)

                def out_blocks(m, c, w):
                    n = 2 if w == CW else (1 if m == 0 else 0)
                    if n:
                        dve.wait_ge(s_mm[3], c * 2 + m + 1)
                        xs = x2[:, bass.ds(c * 4 + 2 * m, n), :]
                        nc.vector.scalar_tensor_tensor(xs, psO[m][:, 0:n, :], 1.0 / (WS * HS), xs,
                                                       ALU.mult, ALU.add).then_inc(s_ev[3], 1)

                def layer(l):
                    def chunk(c, w, nw):
                        for m in range(MR[l]):
                            if l < 3:
                                stats(l, m, c, c, w)
                            else:
                                out_blocks(m, c, w)
                            if nw and l:
                                for k in rows_of(l, m):
                                    row(l, k, c + 1, nw)
                    if l:
                        n, v = KR[l], 4 * VAT[l - 1]
                        dve.wait_ge(s_st, 7 * sum(MR[:l]))
                        if l == 3:
                            nc.vector.memset(ones16[:, :], 1.0).then_inc(s_ones16, 1)
                        for k in range(n):
                            ch.mark(nc.vector.bn_aggr(mv2[:, k, :], bst2[:, k, :, :].rearrange("p c s -> p (c s)")))
                        dve.wait_ge(ch.sem, ch.n)
                        nc.vector.tensor_scalar(mv2[:, 0:n, 1], mv2[:, 0:n, 1], BN_EPS, None, ALU.add).then_inc(s_sq, 1)
                        dve.wait_ge(s_sd, l)
                        ch.step(nc.vector.reciprocal(cf[:, 0, 0:n], mv2[:, 0:n, 1]))
                        ch.step(nc.vector.tensor_tensor(cf[:, 0, 0:n], cf[:, 0, 0:n], vec[:, 1, v:v + n], ALU.mult))
                        ch.step(nc.vector.tensor_tensor(cf[:, 1, 0:n], cf[:, 0, 0:n], mv2[:, 0:n, 0], ALU.mult))
                        ch.step(nc.vector.tensor_tensor(cf[:, 1, 0:n], vec[:, 2, v:v + n], cf[:, 1, 0:n], ALU.subtract))
                        nc.vector.tensor_scalar(cf[:, 2, 0:n], cf[:, 1, 0:n], 1.0, None, ALU.add).then_inc(s_cf, 1)
                        dve.wait_ge(s_cf, l)
                        for k in range(n):
                            row(l, k, 0, CW)
                    if l == 3:
                        dve.wait_ge(s_b4, 16)
                        dve.wait_ge(s_b4c, 1)
                        ch.step(nc.vector.scalar_tensor_tensor(b4[:, :], psR[0:PB, 0:D], -1.0 / WS, b4[:, :], ALU.mult, ALU.add))
                        dve.wait_ge(s_xr, 16)
                        ch.step(nc.vector.tensor_tensor(x2[:, :, :], x2[:, :, :], b4[:, :].unsqueeze(1).to_broadcast([PB, NB, D]), ALU.add))
                    with loop(nc, dve, 0, CN - 1) as c:
                        chunk(c, CW, CW)
                    chunk(CN - 1, CW, PB)
                    chunk(CN, PB, 0)

                for l in range(4):
                    layer(l)

            @block.tensor
            def _(pe):
                pe.wait_ge(s_k2, 1)
                nc.tensor.matmul(psR[:, 0:NB], later[:, :], S[:, :, T1 - 1], start=True, stop=True)
                nc.tensor.matmul(psR[:, 32:32 + NB], ones[:, :], S[:, :, T1 - 1], start=True, stop=True).then_inc(s_cnt, 1)
                pe.wait_ge(s_w1, 16)
                pe.wait_ge(s_wlo, len(pieces))
                W = [None, W2, W3]
                for l in range(1, 3):
                    pe.sem_inc(s_u[l], 2)
                    pe.sem_inc(s_h[l], 2)
                pe.sem_inc(s_u[3], 2)
                pe.sem_inc(s_h[3], 2)

                def chunk(l, c, w):
                    if l:
                        pe.wait_ge(s_h[l], c * KR[l] + KR[l] + 2)
                    for m in range(MR[l]):
                        pe.wait_ge(s_ev[l], c * MR[l] + m + 1)
                        ms = slice(128 * m, 128 * (m + 1))
                        if l == 0:
                            for k in range(2):
                                last = nc.tensor.matmul(psZ[m % 4][:, 0:w], W1[:, k, ms], accT[:, k, bass.ds(c * CW, w)],
                                                        start=(k == 0), stop=(k == 1))
                        else:
                            terms = [(sw, sh, k) for k in range(KR[l]) for sw, sh in ((0, 0), (0, 1), (1, 0))]
                            for n, (sw, sh, k) in enumerate(terms):
                                last = nc.tensor.matmul(psZ[m % 4][:, 0:w], W[l][:, sw, k, ms], halves(l, k, c * CW, w)[sh],
                                                        start=(n == 0), stop=(n == len(terms) - 1))
                        last.then_inc(s_mm[l], 1)

                def last_layer(c, w):
                    pe.wait_ge(s_h[3], c * KR[3] + KR[3] + 2)
                    for m in range(2):
                        n = 2 if w == CW else (1 if m == 0 else 0)
                        if not n:
                            continue
                        wait_apart(pe, s_ev[3], c * 2 + m + 1, s_tick[2])
                        terms = [(sw, sh, k) for k in range(4) for sh, sw in ((0, 0), (0, 1), (1, 0))]
                        for j in range(n):
                            for i, (sw, sh, k) in enumerate(terms):
                                f = ZIN[3][:, k, :].bitcast(F16)
                                hx = f[:, bass.ds(c * (2 * CW) + sh * w + (2 * m + j) * PB, PB)]
                                last = nc.tensor.matmul(psO[m][:, j, :], hx, W4[:, sw, k, :], start=(i == 0),
                                                        stop=(i == len(terms) - 1))
                        last.then_inc(s_mm[3], 1)

                for l in range(4):
                    if l < 3:
                        pe.sem_inc(s_ev[l], 4)
                        with loop(nc, pe, 0, CN) as c:
                            chunk(l, c, CW)
                        chunk(l, CN, PB)
                    else:
                        pe.wait_ge(s_ones16, 1)
                        for i in range(8):
                            last = nc.tensor.matmul(psR[0:PB, 0:D], ones16[:, 0:PB], W4[:, i // 4, i % 4, :],
                                                    start=(i == 0), stop=(i == 7))
                        last.then_inc(s_b4c, 1)
                        pe.sem_inc(s_ev[3], 2)
                        with loop(nc, pe, 0, CN) as c:
                            last_layer(c, CW)
                        last_layer(CN, PB)

        xn2 = at("xn2", 31 * KB, [PB, NB, D])
        PIECES = 6
        PW = HP * 2
        we = at("we", 57 * KB, [128, X * PIECES * PW], F16)
        raw = at("raw", 60 * KB, [128, X * PIECES, HP])
        zero = at("zero", 57 * KB, [128, D])
        later3 = at("later3", 56 * KB, [128, PB])
        ones3 = at("ones3", 56 * KB + 512, [128, PB])
        M = at("M", 1 * KB, [PB, NB * K2, X])
        T = at("T", 1 * KB + 1600, [PB, NB * K2, X])
        top = at("top", 1 * KB + 3200, [PB, NB, X])
        topi = at("topi", 1 * KB + 4000, [PB, NB, X], U32)
        o = 204 * KB
        xTf = at("xTf", o, [128, 2, 2, PB]); o += 2016
        lg = at("lg", o, [PB, NB, X]); o += 800
        rw = at("rw", o, [128, 2, X]); o += 64
        slot_i = at("slot_i", o, [PB, NB * K2], I32); o += 224
        gate = at("gate", o, [PB, NB, K2]); o += 224
        ex_i = at("ex_i", o, [1, T2], I32); o += 224
        bst3 = at("bst3", o, [PB, 5, 6]); o += 128
        mv3 = at("mv3", o, [PB, 5, 2]); o += 64
        sd3 = at("sd3", o, [PB, 2, 5]); o += 64
        assert BASE + o <= 229368
        o = 31 * KB
        xs = at("xs", o, [128, 2, D]); o += 2048
        xh = at("xh", o, [128, 2, 2, D], F16); o += 2048
        sl = at("sl", o, [128, 2, HP // 2]); o += 3072
        hv = at("hv", o, [128, 2, HP // 2]); o += 3072
        hh = at("hh", o, [128, 2, 2, HP], F16); o += 6144
        yv = at("yv", o, [128, 2, D]); o += 2048
        xs_d = dram("xs_d", (T2 * 128, D))
        y_d = dram("y_d", (T2 * 128, D))
        s_c3 = [sem(f"s_c3{i}") for i in range(4)]
        s_zero = sem("s_zero")
        s_zst = sem("s_zst")
        s_raw = [sem(f"s_raw{e}") for e in range(X)]
        s_rw = sem("s_rw")
        s_k3 = sem("s_k3")
        s_ehi = sem("s_ehi")
        s_elo = sem("s_elo")
        s_v3 = sem("s_v3")
        s_d3 = sem("s_d3")
        s_n3 = sem("s_n3")
        s_t3 = sem("s_t3")
        s_xt3 = sem("s_xt3")
        s_lg = sem("s_lg")
        s_gx = sem("s_gx")
        s_gxe = sem("s_gxe")
        s_M = sem("s_M")
        s_tot = sem("s_tot")
        s_slot = sem("s_slot")
        s_ex = sem("s_ex")
        s_scx = sem("s_scx")
        s_xs = [sem("s_xs0"), sem("s_xs1")]
        s_xsT = sem("s_xsT")
        s_xh = sem("s_xh")
        s_xl = sem("s_xl")
        s_up = sem("s_up")
        s_sl = sem("s_sl")
        s_hv = sem("s_hv")
        s_hh = sem("s_hh")
        s_hl = sem("s_hl")
        s_dn = sem("s_dn")
        s_yv = sem("s_yv")
        s_yst = [sem("s_yst0"), sem("s_yst1")]

        with ExitStack() as p3:
            psT3 = [p3.enter_context(nc.psum_tensor(f"psT3{i}", [128, 2, 128], F32)) for i in range(2)]
            psL = p3.enter_context(nc.psum_tensor("psL", [PB, NB, X], F32))
            psH = [p3.enter_context(nc.psum_tensor(f"psH{i}", [128, HP // 2], F32)) for i in range(4)]
            psY = p3.enter_context(nc.psum_tensor("psY", [128, D], F32))
            block = p3.enter_context(nc.Block())
            HX = NB * K2 * X // 2

            HQ = HP // 2

            def dst_half(n, s):
                return we[:, n * PW + s * HP:n * PW + (s + 1) * HP]

            @block.sync
            def _(sp):
                sp.wait_ge(s_zero, 1)
                sp.dma_start(xs_d.rearrange("(t p) d -> p t d", p=128),
                             zero[:, :].unsqueeze(1).to_broadcast([128, T2, D])).then_inc(s_zst, 16)
                sp.dma_start(rw[:, :, :], a["L0_ffn_router_w"].rearrange("(k p) e -> p k e", p=128)).then_inc(s_rw, 16)
                for e in range(X):
                    for j, name in enumerate(("w1", "w3")):
                        sp.dma_start(raw[:, e * PIECES + 2 * j:e * PIECES + 2 * j + 2, :],
                                     a["L0_ffn_" + name][e].rearrange("(k p) h -> p k h", p=128)).then_inc(s_raw[e], 16)
                    sp.dma_start(raw[:, e * PIECES + 4:e * PIECES + 6, :].rearrange("p j (k c) -> p (j k) c", c=D),
                                 a["L0_ffn_w2"][e].rearrange("(k p) c -> p k c", p=128)).then_inc(s_raw[e], 16)
                sp.wait_ge(s_scx, 16 * NB * K2)

                def load(t, i):
                    sp.dma_start(xs[:, i, :], xs_d[bass.ds(t * 128, 128), :]).then_inc(s_xs[i], 16)

                load(0, 0)
                load(1, 1)
                with loop(nc, sp, 0, T2 // 2 - 1) as g:
                    for i in range(2):
                        wait_apart(sp, s_xsT, g * 2 + i + 1, s_tick[3])
                        load(g * 2 + i + 2, i)

            @block.gpsimd
            def _(pool):
                ch = Chain(pool, s_c3[0])
                nc.gpsimd.memset(zero[:, :], 0.0).then_inc(s_zero, 1)
                nc.gpsimd.memset(ones3[:, :], 1.0)
                ch.step(nc.gpsimd.memset(later3[:, :], 1.0))
                ch.step(nc.gpsimd.affine_select(out=later3[:, :], in_=later3[:, :], compare_op=ALU.is_gt, fill=0.0,
                                                base=0, pattern=[[1, PB]], channel_multiplier=-1))
                pool.sem_inc(s_k3, 1)
                pool.wait_ge(s_zst, 16)
                pool.wait_ge(s_slot, 1)
                for b in range(NB):
                    for k in range(K2):
                        j = b * K2 + k
                        pool.indirect_dma_start(
                            out=xs_d, out_offset=bass.IndirectOffsetOnAxis(ap=slot_i[:, j:j + 1], axis=0),
                            in_=xn2[:, b, :], in_offset=None).then_inc(s_scx, 16)

                with loop(nc, pool, 0, T2 // 2) as g:
                    for i in range(2):
                        t = g * 2 + i
                        wait_apart(pool, s_yv, t + 1, s_halves)
                        pool.dma_start(y_d[bass.ds(t * 128, 128), :], yv[:, i, :]).then_inc(s_yst[i], 16)
                for i in range(2):
                    pool.wait_ge(s_yst[i], 16 * (T2 // 2))

            @block.scalar
            def _(act):
                for c in range(5):
                    act.wait_ge(s_v3, c + 1)
                    nc.scalar.activation(sd3[:, 0, :], mv3[:, :, 1], ACT.Sqrt).then_inc(s_d3, 1)
                for b in range(NB):
                    act.wait_ge(s_t3, b + 1)
                    if b >= 2:
                        act.wait_ge(s_lg, b - 1)
                    nc.scalar.activation(xTf[:, b % 2, :, :], psT3[b % 2][:, :, 0:PB], ACT.Copy).then_inc(s_xt3, 1)
                act.wait_ge(s_gx, 1)
                nc.scalar.activation(top[:, :, :], top[:, :, :], ACT.Exp).then_inc(s_gxe, 1)
                act.wait_ge(s_zst, 16)
                for n in range(X * PIECES):
                    act.wait_ge(s_raw[n // PIECES], 48)
                    if n:
                        act.wait_ge(s_elo, n)
                    nc.scalar.activation(dst_half(n, 0), raw[:, n, :], ACT.Copy, scale=WS).then_inc(s_ehi, 1)

                def halves_x(t, i):
                    act.wait_ge(s_xsT, t + 1)
                    act.wait_ge(s_up, 2 * t + 2)
                    nc.scalar.activation(xh[:, i, 0, :], psT3[i][:, :, :], ACT.Copy, scale=XS).then_inc(s_xh, 1)

                def hidden(t, i, first=False):
                    for q in range(2):
                        act.wait_ge(s_up, 4 + 2 * t + q + 1)
                        if not first:
                            act.wait_ge(s_hv, 2 * t + q - 1)
                        nc.scalar.activation(sl[:, q, :], psH[q][:, :], ACT.Silu, scale=1.0 / (XS * WS)).then_inc(s_sl, 1)
                        act.wait_ge(s_hv, 2 * t + q + 1)
                        act.wait_ge(s_dn, t + 1)
                        nc.scalar.activation(hh[:, i, 0, q * HQ:(q + 1) * HQ], hv[:, q, :], ACT.Copy).then_inc(s_hh, 1)

                def result(t, i, stored):
                    act.wait_ge(s_dn, 2 + t + 1)
                    if stored is not None:
                        act.wait_ge(s_yst[i], stored * 16)
                    nc.scalar.activation(yv[:, i, :], psY[:, :], ACT.Copy, scale=1.0 / (WS * HS)).then_inc(s_yv, 1)

                halves_x(0, 0)
                halves_x(1, 1)
                hidden(0, 0, True)
                for t in (1, 2):
                    halves_x(t + 1, 1 - t % 2)
                    hidden(t, t % 2)
                    result(t - 1, 1 - t % 2, None)
                with loop(nc, act, 1, T2 // 2 - 1) as g:
                    for i in (1, 0):
                        t = g * 2 + 2 - i
                        halves_x(t + 1, 1 - i)
                        hidden(t, i)
                        result(t - 1, 1 - i, g)
                hidden(T2 - 1, 1)
                result(T2 - 2, 0, T2 // 2 - 1)
                result(T2 - 1, 1, T2 // 2 - 1)

            @block.vector
            def _(dve):
                ch = Chain(dve, s_c3[1])
                for c in range(5):
                    for b in range(5):
                        ch.mark(nc.vector.bn_stats(bst3[:, b, :], x2[:, 5 * c + b, :]))
                    dve.wait_ge(ch.sem, ch.n)
                    for b in range(5):
                        ch.mark(nc.vector.bn_aggr(mv3[:, b, :], bst3[:, b, :]))
                    dve.wait_ge(ch.sem, ch.n)
                    nc.vector.tensor_scalar(mv3[:, :, 1], mv3[:, :, 1], LN_EPS, None, ALU.add).then_inc(s_v3, 1)
                    dve.wait_ge(s_d3, c + 1)
                    ch.step(nc.vector.reciprocal(sd3[:, 1, :], sd3[:, 0, :]))
                    for b in range(5):
                        nc.vector.tensor_scalar(xn2[:, 5 * c + b, :], x2[:, 5 * c + b, :], mv3[:, b, 0:1], sd3[:, 1, b:b + 1],
                                                ALU.subtract, ALU.mult).then_inc(s_n3, 1)
                    dve.wait_ge(s_n3, 5 * c + 5)
                dve.wait_ge(s_lg, NB)
                ch.step(nc.vector.tensor_copy(lg[:, :, :], psL[:, :, :]))
                for b in range(NB):
                    ch.mark(nc.vector.max(top[:, b, :], lg[:, b, :]))
                dve.wait_ge(ch.sem, ch.n)
                for b in range(NB):
                    ch.mark(nc.vector.max_index(topi[:, b, :], top[:, b, :], lg[:, b, :]))
                dve.wait_ge(ch.sem, ch.n)
                ch.step(nc.vector.tensor_tensor(T[:, 0:NB, :], top[:, :, :], top[:, :, 0:1].to_broadcast([PB, NB, X]), ALU.subtract))
                nc.vector.tensor_copy(top[:, :, :], T[:, 0:NB, :]).then_inc(s_gx, 1)
                gf = gate[:, :, :].rearrange("p b k -> p (b k)")
                ch.step(nc.vector.tensor_copy(gate[:, :, :], topi[:, :, 0:K2]))
                nc.vector.tensor_tensor(M[:, :, :], gf.unsqueeze(2).to_broadcast([PB, NB * K2, X]),
                                        iota[0:PB, 0:X].unsqueeze(1).to_broadcast([PB, NB * K2, X]), ALU.is_equal).then_inc(s_M, 1)
                dve.wait_ge(s_gxe, 1)
                dve.wait_ge(s_M, 1)
                ch.step(nc.vector.tensor_reduce(lg[:, :, 0:1], top[:, :, :], AX_X, ALU.add))
                ch.step(nc.vector.reciprocal(lg[:, :, 1], lg[:, :, 0]))
                ch.step(nc.vector.tensor_tensor(lg[:, :, 2:4], top[:, :, 0:2], lg[:, :, 1:2].to_broadcast([PB, NB, 2]), ALU.mult))
                ch.step(nc.vector.tensor_tensor(lg[:, :, 4], lg[:, :, 2], lg[:, :, 3], ALU.add))
                ch.step(nc.vector.tensor_scalar(lg[:, :, 4], lg[:, :, 4], 1e-9, None, ALU.add))
                ch.step(nc.vector.reciprocal(lg[:, :, 5], lg[:, :, 4]))
                ch.step(nc.vector.tensor_tensor(gate[:, :, :], lg[:, :, 2:4], lg[:, :, 5:6].to_broadcast([PB, NB, 2]), ALU.mult))
                dve.wait_ge(s_tot, 1)
                Tn = [T[:, NB * n:NB * (n + 1), :].rearrange("p j e -> p (j e)") for n in range(2)]
                for n in range(2):
                    ch.step(nc.vector.tensor_copy(Tn[n], psH[2 * n + 1][0:PB, 0:HX]))
                for e in range(X):
                    ch.mark(nc.vector.tensor_tensor_scan(T[:, :, e], T[:, :, e], T[:, :, e], 0.0, ALU.add, ALU.max))
                dve.wait_ge(ch.sem, ch.n)
                q = lg[:, :, :].rearrange("p b e -> p (b e)")
                qi = lg[:, :, :].rearrange("p b e -> p (b e)").bitcast(I32)
                ch.step(nc.vector.tensor_scalar(qi[:, 0:X], T[:, NB * K2 - 1, :], 127.0, None, ALU.add))
                ch.step(nc.vector.tensor_scalar(qi[:, 8:16], qi[:, 0:8], 7, None, ALU.arith_shift_right))
                ch.step(nc.vector.tensor_copy(q[:, 16:24], qi[:, 8:16]))
                ch.step(nc.vector.tensor_tensor_scan(q[:, 24:32], q[:, 16:24], q[:, 16:24], 0.0, ALU.add, ALU.max))
                ch.step(nc.vector.tensor_tensor(q[:, 32:40], q[:, 24:32], q[:, 16:24], ALU.subtract))
                ch.step(nc.vector.tensor_scalar(q[:, 32:40], q[:, 32:40], 128.0, None, ALU.mult))
                for n in range(2):
                    ch.step(nc.vector.tensor_tensor(Tn[n], Tn[n], psH[2 * n + 1][0:PB, 0:HX], ALU.subtract))
                    ch.step(nc.vector.tensor_tensor(Tn[n], Tn[n], psH[2 * n][0:PB, 0:HX], ALU.add))
                ch.step(nc.vector.tensor_tensor(T[:, :, :], T[:, :, :], q[:, 32:40].unsqueeze(1).to_broadcast([PB, NB * K2, X]), ALU.add))
                ch.step(nc.vector.tensor_tensor(T[:, :, :], T[:, :, :], M[:, :, :], ALU.mult))
                ch.step(nc.vector.tensor_reduce(q[:, 64:64 + NB * K2], T[:, :, :], AX_X, ALU.add))
                nc.vector.tensor_copy(slot_i[:, :], q[:, 64:64 + NB * K2]).then_inc(s_slot, 1)
                cmp_ = at("cmp_", 1 * KB, [1, T2, X], F16)
                tids = iota[0:1, 0:T2].unsqueeze(2).to_broadcast([1, T2, X])
                ch.step(nc.vector.tensor_tensor(cmp_[:, :, :], tids, q[0:1, 24:32].unsqueeze(1).to_broadcast([1, T2, X]), ALU.is_ge))
                ch.step(nc.vector.tensor_reduce(q[0:1, 128:128 + T2], cmp_[:, :, :], AX_X, ALU.add))
                nc.vector.tensor_scalar(ex_i[:, :], q[0:1, 128:128 + T2], X - 1.0, None, ALU.min).then_inc(s_ex, 1)
                for n in range(X * PIECES):
                    dve.wait_ge(s_ehi, n + 1)
                    nc.vector.scalar_tensor_tensor(dst_half(n, 1), raw[:, n, :], WS, dst_half(n, 0),
                                                   ALU.mult, ALU.subtract).then_inc(s_elo, 1)

                def halves_x(t, i):
                    dve.wait_ge(s_xh, t + 1)
                    nc.vector.scalar_tensor_tensor(xh[:, i, 1, :], psT3[i][:, :, :].rearrange("p k t -> p (k t)"), XS,
                                                   xh[:, i, 0, :], ALU.mult, ALU.subtract).then_inc(s_xl, 1)

                def hidden(t, i):
                    for q in range(2):
                        hs = slice(q * HQ, (q + 1) * HQ)
                        dve.wait_ge(s_sl, 2 * t + q + 1)
                        nc.vector.scalar_tensor_tensor(hv[:, q, :], psH[2 + q][:, :], HS / (XS * WS), sl[:, q, :],
                                                       ALU.mult, ALU.mult).then_inc(s_hv, 1)
                        dve.wait_ge(s_hh, 2 * t + q + 1)
                        nc.vector.tensor_tensor(hh[:, i, 1, hs], hv[:, q, :], hh[:, i, 0, hs], ALU.subtract).then_inc(s_hl, 1)

                halves_x(0, 0)
                halves_x(1, 1)
                hidden(0, 0)
                with loop(nc, dve, 0, T2 // 2 - 1) as g:
                    for i in (1, 0):
                        t = g * 2 + 2 - i
                        halves_x(t + 1, 1 - i)
                        hidden(t, i)
                hidden(T2 - 1, 1)

            @block.tensor
            def _(pe):
                pe.wait_ge(s_rw, 16)
                for b in range(NB):
                    pe.wait_ge(s_n3, b + 1)
                    if b >= 2:
                        pe.wait_ge(s_xt3, b - 1)
                    for k in range(2):
                        last = nc.tensor.transpose(psT3[b % 2][:, k, 0:PB], xn2[:, b, 128 * k:128 * (k + 1)], ident[0:PB, 0:PB])
                    last.then_inc(s_t3, 1)
                    pe.wait_ge(s_xt3, b + 1)
                    for k in range(2):
                        last = nc.tensor.matmul(psL[:, b, :], xTf[:, b % 2, k, :], rw[:, k, :], start=(k == 0), stop=(k == 1))
                    last.then_inc(s_lg, 1)
                pe.wait_ge(s_k3, 1)
                pe.wait_ge(s_M, 1)
                for n in range(2):
                    mn = M[:, NB * n:NB * (n + 1), :].rearrange("p j e -> p (j e)")
                    nc.tensor.matmul(psH[2 * n][0:PB, 0:HX], later3[0:PB, :], mn, start=True, stop=True)
                    last = nc.tensor.matmul(psH[2 * n + 1][0:PB, 0:HX], ones3[0:PB, :], mn, start=True, stop=True)
                last.then_inc(s_tot, 1)
                pe.sem_inc(s_up, 4)
                pe.sem_inc(s_dn, 2)
                pe.wait_ge(s_elo, X * PIECES)
                pe.wait_ge(s_ex, 1)

                def experts(t, n):
                    return registers(nc, pe, ex_i[0:1, bass.ds(t, n)], X - 1)

                def weights(e, piece, s, c, w):
                    return we[:, bass.ds(e * (PIECES * PW) + piece * PW + s * HP + c, w)]

                def turn(t, i, loads):
                    pe.wait_ge(s_xs[i], 16 * loads)
                    if not isinstance(t, int):
                        pe.wait_ge(s_xl, t - 1)
                    for k in range(2):
                        last = nc.tensor.transpose(psT3[i][:, k, :], xs[:, i, 128 * k:128 * (k + 1)], ident[:, :])
                    last.then_inc(s_xsT, 1)

                def up(t, i, e):
                    pe.wait_ge(s_xl, t + 1)
                    for q in range(2):
                        if not (isinstance(t, int) and t == 0):
                            wait_apart(pe, s_hv, 2 * t + q - 1, s_tick[2])
                        for w3 in range(2):
                            for m in range(3):
                                terms = [(sw, sx, k) for k in range(2) for sw, sx in ((0, 0), (0, 1), (1, 0))]
                                for n, (sw, sx, k) in enumerate(terms):
                                    last = nc.tensor.matmul(psH[2 * w3 + q][:, 128 * m:128 * (m + 1)],
                                                            weights(e, 2 * w3 + k, sw, (3 * q + m) * 128, 128),
                                                            xh[:, i, sx, 128 * k:128 * (k + 1)],
                                                            start=(n == 0), stop=(n == len(terms) - 1))
                        last.then_inc(s_up, 1)

                def down(t, i, e):
                    if not (isinstance(t, int) and t == 0):
                        wait_apart(pe, s_yv, t, s_tick[2])
                    for n in range(2):
                        wait_apart(pe, s_hl, 2 * t + n + 1, s_tick[2])
                        for m in range(3 * n, 3 * n + 3):
                            for j, (sh, sw) in enumerate(((0, 0), (0, 1), (1, 0))):
                                last = nc.tensor.matmul(psY[:, :], hh[:, i, sh, 128 * m:128 * (m + 1)],
                                                        weights(e, 4 + n, sw, (m - 3 * n) * D, D),
                                                        start=(m == 0 and j == 0), stop=(m == HM - 1 and j == 2))
                    last.then_inc(s_dn, 1)

                turn(0, 0, 1)
                turn(1, 1, 1)
                up(0, 0, experts(0, 1)[0])
                with loop(nc, pe, 0, T2 // 2 - 1) as g:
                    e = experts(g * 2, 3)
                    for i in (1, 0):
                        t = g * 2 + 2 - i
                        turn(t + 1, 1 - i, g + 2)
                        up(t, i, e[2 - i])
                        down(t - 1, 1 - i, e[1 - i])
                e = experts(T2 - 2, 2)
                up(T2 - 1, 1, e[1])
                down(T2 - 2, 0, e[0])
                down(T2 - 1, 1, e[1])

        free_semaphores()

        xn3 = at("xn3", 31 * KB, [PB, NB, D])
        yg = at("yg", 60 * KB, [PB, 8, D])
        row = at("row", 70 * KB, [PB, NB, RW])
        wx = at("wx", 77 * KB, [128, 2, NH + OD + NH])
        wt = at("wt", 78 * KB, [OD, D])
        wlr = at("wlr", 79 * KB, [OD, 2, NH])
        el = at("el", 79 * KB + 64, [PB, NB * NH])
        f1 = at("f1", 131 * KB, [128, 2, 2, FH], F16)
        f2 = at("f2", 139 * KB, [128, 2, FH // 128, D], F16)
        fraw = at("fraw", 147 * KB, [128, 2, 2 * FH])
        tab_d = dram("tab_d", (N, RW))
        s_yg = [sem(f"s_yg{i}") for i in range(8)]
        s_res = sem("s_res")
        s_wt = sem("s_wt")
        s_wlr = sem("s_wlr")
        s_wx = sem("s_wx")
        s_one = sem("s_one")
        s_fraw = sem("s_fraw")
        s_fhi = sem("s_fhi")
        s_flo = sem("s_flo")
        s_v4 = sem("s_v4")
        s_d4 = sem("s_d4")
        s_n4 = sem("s_n4")
        s_t4 = sem("s_t4")
        s_xt4 = sem("s_xt4")
        s_row = sem("s_row")
        s_rowc = sem("s_rowc")
        s_tab = sem("s_tab")
        s_c4 = sem("s_c4")

        def normalise(dve, ch, src, dst, c, s_var, s_dev, s_out):
            for b in range(5):
                ch.mark(nc.vector.bn_stats(bst3[:, b, :], src[:, 5 * c + b, :]))
            dve.wait_ge(ch.sem, ch.n)
            for b in range(5):
                ch.mark(nc.vector.bn_aggr(mv3[:, b, :], bst3[:, b, :]))
            dve.wait_ge(ch.sem, ch.n)
            nc.vector.tensor_scalar(mv3[:, :, 1], mv3[:, :, 1], LN_EPS, None, ALU.add).then_inc(s_var, 1)
            dve.wait_ge(s_dev, c + 1)
            ch.step(nc.vector.reciprocal(sd3[:, 1, :], sd3[:, 0, :]))
            for b in range(5):
                nc.vector.tensor_scalar(dst[:, 5 * c + b, :], src[:, 5 * c + b, :], mv3[:, b, 0:1], sd3[:, 1, b:b + 1],
                                        ALU.subtract, ALU.mult).then_inc(s_out, 1)
            dve.wait_ge(s_out, 5 * c + 5)

        with ExitStack() as p4:
            psT4 = [p4.enter_context(nc.psum_tensor(f"psT4{i}", [128, 2, 128], F32)) for i in range(2)]
            psX = [p4.enter_context(nc.psum_tensor(f"psX{i}", [128, NH + OD + NH], F32)) for i in range(2)]
            psW = p4.enter_context(nc.psum_tensor("psW", [128, 2, 2 * NH], F32))
            block = p4.enter_context(nc.Block())

            @block.sync
            def _(sp):
                sp.dma_start(wt[:, :], a["L1_gnn_WT"]).then_inc(s_wt, 16)
                for j, name in enumerate(("r", "l")):
                    sp.dma_start(wlr[:, j, :], a["L1_gnn_W" + name]).then_inc(s_wlr, 16)
                sp.dma_start(wx[:, :, NH:NH + OD], a["L1_gnn_W"].rearrange("(k p) n -> p k n", p=128)).then_inc(s_wlr, 16)
                sp.dma_start(fraw[:, 0, :].rearrange("p (k n) -> p k n", k=2),
                             a["L1_ffn_w1"].rearrange("(k p) n -> p k n", p=128)).then_inc(s_fraw, 16)
                sp.dma_start(fraw[:, 1, :].rearrange("p (k n) -> p k n", n=D),
                             a["L1_ffn_w2"].rearrange("(k p) n -> p k n", p=128)).then_inc(s_fraw, 16)
                sp.wait_ge(s_one, 1)
                for c in range(5):
                    sp.wait_ge(s_rowc, 5 * c + 5)
                    sp.dma_start(tab_d.rearrange("(b p) d -> p b d", p=PB)[:, 5 * c:5 * c + 5, :],
                                 row[:, 5 * c:5 * c + 5, :]).then_inc(s_tab, 16)
                sp.wait_ge(s_tab, 80)

            @block.gpsimd
            def _(pool):
                nc.gpsimd.memset(row[:, :, NH + OD:RW], 1.0).then_inc(s_one, 1)
                for j in range(NB * K2):
                    if j >= 8:
                        pool.wait_ge(s_res, j - 7)
                    pool.indirect_dma_start(
                        out=yg[:, j % 8, :], out_offset=None, in_=y_d,
                        in_offset=bass.IndirectOffsetOnAxis(ap=slot_i[:, j:j + 1], axis=0)).then_inc(s_yg[j % 8], 16)

            @block.scalar
            def _(act):
                act.wait_ge(s_fraw, 32)
                for n, f in enumerate((f1, f2)):
                    nc.scalar.activation(f[:, 0, :, :].rearrange("p k n -> p (k n)"), fraw[:, n, :], ACT.Copy,
                                         scale=WS).then_inc(s_fhi, 1)
                act.wait_ge(s_wx, 1)
                for j in range(2):
                    nc.scalar.activation(wx[:, :, j * (NH + OD):j * (NH + OD) + NH], psW[:, :, j * NH:(j + 1) * NH],
                                         ACT.Copy).then_inc(s_wx, 1)
                for c in range(5):
                    act.wait_ge(s_v4, c + 1)
                    nc.scalar.activation(sd3[:, 0, :], mv3[:, :, 1], ACT.Sqrt).then_inc(s_d4, 1)
                    for b in range(5 * c, 5 * c + 5):
                        act.wait_ge(s_t4, b + 1)
                        if b >= 2:
                            act.wait_ge(s_row, b - 1)
                        nc.scalar.activation(xTf[:, b % 2, :, :], psT4[b % 2][:, :, 0:PB], ACT.Copy).then_inc(s_xt4, 1)
                        act.wait_ge(s_row, b + 1)
                        nc.scalar.activation(row[:, b, 0:NH + OD], psX[b % 2][0:PB, 0:NH + OD], ACT.Copy)
                        nc.scalar.activation(el[:, b * NH:(b + 1) * NH], psX[b % 2][0:PB, NH + OD:NH + OD + NH],
                                             ACT.Copy).then_inc(s_rowc, 1)

            @block.vector
            def _(dve):
                ch = Chain(dve, s_c4)
                for n, f in enumerate((f1, f2)):
                    dve.wait_ge(s_fhi, n + 1)
                    nc.vector.scalar_tensor_tensor(f[:, 1, :, :].rearrange("p k n -> p (k n)"), fraw[:, n, :], WS,
                                                   f[:, 0, :, :].rearrange("p k n -> p (k n)"),
                                                   ALU.mult, ALU.subtract).then_inc(s_flo, 1)
                for c in range(5):
                    for j in range(5 * c * K2, 5 * (c + 1) * K2):
                        b, k = j // K2, j % K2
                        dve.wait_ge(s_yg[j % 8], 16 * (j // 8 + 1))
                        dve.wait_ge(s_res, j)
                        nc.vector.scalar_tensor_tensor(x2[:, b, :], yg[:, j % 8, :], gate[:, b, k:k + 1], x2[:, b, :],
                                                       ALU.mult, ALU.add).then_inc(s_res, 1)
                    dve.wait_ge(s_res, 5 * (c + 1) * K2)
                    normalise(dve, ch, x2, xn3, c, s_v4, s_d4, s_n4)

            @block.tensor
            def _(pe):
                pe.wait_ge(s_wt, 16)
                pe.wait_ge(s_wlr, 48)
                for k in range(2):
                    last = nc.tensor.matmul(psW[:, k, :], wt[:, 128 * k:128 * (k + 1)],
                                            wlr[:, :, :].rearrange("p j h -> p (j h)"), start=True, stop=True)
                last.then_inc(s_wx, 1)
                pe.wait_ge(s_wx, 3)
                for b in range(NB):
                    pe.wait_ge(s_n4, b + 1)
                    if b >= 2:
                        pe.wait_ge(s_xt4, b - 1)
                    for k in range(2):
                        last = nc.tensor.transpose(psT4[b % 2][:, k, 0:PB], xn3[:, b, 128 * k:128 * (k + 1)], ident[0:PB, 0:PB])
                    last.then_inc(s_t4, 1)
                    pe.wait_ge(s_xt4, b + 1)
                    if b >= 2:
                        pe.wait_ge(s_rowc, b - 1)
                    for k in range(2):
                        last = nc.tensor.matmul(psX[b % 2][0:PB, :], xTf[:, b % 2, k, :], wx[:, k, :], start=(k == 0), stop=(k == 1))
                    last.then_inc(s_row, 1)

        VW = OD + 1
        acc = at("acc", 80 * KB, [PB, NB, NH * VW])
        recs = at("recs", 106 * KB, [128, T3, 2], I32)
        place = at("place", 110 * KB, [128, T3])
        g3 = at("g3", 112 * KB, [128, 4, HT, RW])
        oh3 = at("oh3", 118 * KB, [128, 4, HT, PB])
        ohT = at("ohT", 147 * KB, [PB, 2, HT * 128])
        vv = at("vv", 151 * KB, [128, 2, HT, NH * VW])
        zz = at("zz", 160 * KB, [128, 2, HT, NH])
        pp = at("pp", 160 * KB + 128, [128, 2, HT, NH])
        blk3 = at("blk3", 161 * KB, [1, T3 + HT], I32)
        st3 = at("st3", 163 * KB, [128, 4, HT], I32)
        s_rl = sem("s_rl")
        s_bl = sem("s_bl")
        s_pl = sem("s_pl")
        s_st3 = [sem(f"s_st3{i}") for i in range(4)]
        s_g3 = [sem(f"s_g3{i}") for i in range(4 * HT)]
        s_oh3 = sem("s_oh3")
        s_ot = sem("s_ot")
        s_otc = sem("s_otc")
        s_el = sem("s_el")
        s_z = sem("s_z")
        s_lk = sem("s_lk")
        s_p = sem("s_p")
        s_V = sem("s_V")
        s_sct = sem("s_sct")
        s_ac = sem("s_ac")
        s_a0 = sem("s_a0")
        s_bw = sem("s_bw")
        s_halves = sem("s_halves5")
        s_tick = [None, None, sem("s_tick_pe5")]
        NS = T3 // HT
        BODY = 4
        with ExitStack() as p5:
            psOT = [p5.enter_context(nc.psum_tensor(f"psOT{i}", [PB, HT * 128], F32)) for i in range(2)]
            psE = [p5.enter_context(nc.psum_tensor(f"psE{i}", [128, HT, NH], F32)) for i in range(2)]
            psS = [p5.enter_context(nc.psum_tensor(f"psS{i}", [PB, NH * VW], F32)) for i in range(HT)]
            block = p5.enter_context(nc.Block())

            @block.sync
            def _(sp):
                sp.dma_start(recs[:, :, :].rearrange("p t r -> p (t r)"), rec_d).then_inc(s_rl, 16)
                sp.wait_ge(s_bw, 1)
                sp.dma_start(blk3[:, HT:], blk_d).then_inc(s_bl, 16)

            @block.gpsimd
            def _(pool):
                nc.gpsimd.memset(acc[:, :, :], 0.0).then_inc(s_a0, 1)
                pool.wait_ge(s_rl, 16)

                def step(n, s):
                    pool.wait_ge(s_V, n + 1)
                    nc.gpsimd.tensor_copy(st3[:, s, :], recs[:, bass.ds(n * HT, HT), 1]).then_inc(s_st3[0], 1)
                    pool.wait_ge(s_st3[0], n + 1)
                    pool.sem_inc(s_halves, 1)
                    for j in range(HT):
                        pool.indirect_dma_start(
                            out=g3[:, s, j, :], out_offset=None, in_=tab_d,
                            in_offset=bass.IndirectOffsetOnAxis(ap=st3[:, s, j:j + 1], axis=0)).then_inc(s_g3[s * HT + j], 16)

                with loop(nc, pool, 0, NS // BODY) as g:
                    for s in range(BODY):
                        step(g * BODY + s, s)

            @block.scalar
            def _(act):
                def copy_turned(n, s):
                    act.wait_ge(s_ot, n + 1)
                    act.wait_ge(s_el, n + 1)
                    nc.scalar.activation(ohT[:, s % 2, :], psOT[s % 2][:, :], ACT.Copy).then_inc(s_otc, 1)

                def exps(n, s):
                    act.wait_ge(s_lk, n + 1)
                    nc.scalar.activation(pp[:, s % 2, :, :], zz[:, s % 2, :, :], ACT.Exp).then_inc(s_p, 1)

                def step(n, s):
                    if not isinstance(n, int) or 0 <= n + 1 < NS:
                        exps(n + 1, (s + 1) % BODY)
                    if not isinstance(n, int) or 0 <= n + 3 < NS:
                        copy_turned(n + 3, (s + 3) % BODY)

                for n in range(-3, BODY):
                    step(n, n % BODY)
                with loop(nc, act, 1, NS // BODY - 1) as g:
                    for s in range(BODY):
                        step(g * BODY + s, s)
                for n in range(NS - BODY, NS):
                    step(n, n % BODY)

            @block.vector
            def _(dve):
                dve.wait_ge(s_rl, 16)
                nc.vector.tensor_copy(place[:, :], recs[:, :, 0]).then_inc(s_pl, 1)
                nc.vector.memset(blk3[:, 0:HT], 0.0).then_inc(s_bw, 1)
                dve.wait_ge(s_pl, 1)
                dve.wait_ge(s_a0, 1)
                dve.wait_ge(s_bl, 16)
                dve.sem_inc(s_V, 4)
                dve.sem_inc(s_z, 2)
                dve.sem_inc(s_ac, HT)

                def one_hots(n, s):
                    dve.wait_ge(s_sct, n + 1)
                    nc.vector.tensor_tensor(
                        oh3[:, s, :, :], iota[:, 0:PB].unsqueeze(1).to_broadcast([128, HT, PB]),
                        place[:, bass.ds(n * HT, HT)].unsqueeze(2).to_broadcast([128, HT, PB]),
                        ALU.is_equal).then_inc(s_oh3, 1)

                def sums(n, s, loads):
                    dve.wait_ge(s_el, n + 3)
                    for j in range(HT):
                        dve.wait_ge(s_g3[s * HT + j], 16 * loads)
                    nc.vector.tensor_tensor(zz[:, s % 2, :, :], psE[s % 2][:, :, :], g3[:, s, :, 0:NH], ALU.add).then_inc(s_z, 1)

                def leaky(n, s):
                    dve.wait_ge(s_z, n + 3)
                    z = zz[:, s % 2, :, :]
                    nc.vector.scalar_tensor_tensor(z, z, 0.2, z, ALU.mult, ALU.max).then_inc(s_lk, 1)

                def weigh(n, s):
                    dve.wait_ge(s_p, n + 1)
                    dve.wait_ge(s_sct, n + 3)
                    nc.vector.tensor_tensor(
                        vv[:, s % 2, :, :].rearrange("p j (h f) -> p j h f", h=NH),
                        g3[:, s, :, NH:RW].unsqueeze(2).to_broadcast([128, HT, NH, VW]),
                        pp[:, s % 2, :, :].unsqueeze(3).to_broadcast([128, HT, NH, VW]), ALU.mult).then_inc(s_V, 1)

                def accumulate(n, s, at_, tiles=range(HT)):
                    for j in tiles:
                        if j == 0:
                            dve.wait_ge(s_sct, n + 5)
                        dve.wait_ge(s_ac, n * HT + HT + j)
                        b = acc[:, bass.ds(at_[j], 1), :].rearrange("p b f -> p (b f)")
                        nc.vector.tensor_tensor(b, b, psS[j][:, :], ALU.add).then_inc(s_ac, 1)

                def step(n, s, at_, g=None):
                    if not isinstance(n, int) or n >= 0:
                        weigh(n, s)
                    m = n + 1
                    if not isinstance(n, int) or 0 <= m < NS:
                        sums(m, (s + 1) % BODY, m // BODY + 1 if isinstance(n, int) else g + 1 + (s + 1) // BODY)
                    halves_ = range(HT // 2), range(HT // 2, HT)
                    if not isinstance(n, int) or n >= 1:
                        accumulate(n - 1, (s - 1) % BODY, at_, halves_[0])
                    if not isinstance(n, int) or 0 <= m < NS:
                        leaky(m, (s + 1) % BODY)
                    if not isinstance(n, int) or n >= 1:
                        accumulate(n - 1, (s - 1) % BODY, at_, halves_[1])
                    if not isinstance(n, int) or 0 <= n + 3 < NS:
                        one_hots(n + 3, (s + 3) % BODY)

                def blocks_before(n, steps):
                    return registers(nc, dve, blk3[0:1, bass.ds(n * HT, steps * HT)], NB - 1)

                for n in range(-3, BODY):
                    step(n, n % BODY, blocks_before(n, 1) if n >= 1 else None)
                with loop(nc, dve, 1, NS // BODY - 1) as g:
                    at_ = blocks_before(g * BODY, BODY)
                    for s in range(BODY):
                        step(g * BODY + s, s, at_[s * HT:(s + 1) * HT], g)
                for n in range(NS - BODY, NS):
                    step(n, n % BODY, blocks_before(n, 1))
                accumulate(NS - 1, (NS - 1) % BODY, blocks_before(NS, 1))

            @block.tensor
            def _(pe):
                pe.wait_ge(s_bl, 16)
                pe.wait_ge(s_bw, 1)
                pe.sem_inc(s_sct, 4)
                pe.sem_inc(s_el, 2)

                def turn(n, s):
                    pe.wait_ge(s_oh3, n + 1)
                    if not isinstance(n, int) or n >= 2:
                        pe.wait_ge(s_otc, n - 1)
                    for j in range(HT):
                        last = nc.tensor.transpose(psOT[s % 2][:, 128 * j:128 * (j + 1)], oh3[:, s, j, :], ident[:, :])
                    last.then_inc(s_ot, 1)

                def pick(n, s, at_):
                    pe.wait_ge(s_otc, n + 1)
                    wait_apart(pe, s_z, n + 1, s_tick[2])
                    for j in range(HT):
                        last = nc.tensor.matmul(psE[s % 2][:, j, :], ohT[:, s % 2, 128 * j:128 * (j + 1)],
                                                el[:, bass.ds(at_[j] * NH, NH)], start=True, stop=True)
                    last.then_inc(s_el, 1)

                def scatter(n, s):
                    pe.wait_ge(s_V, n + 5)
                    for j in range(HT):
                        pe.wait_ge(s_ac, n * HT + j + 1)
                        last = nc.tensor.matmul(psS[j][:, :], oh3[:, s, j, :], vv[:, s % 2, j, :], start=True, stop=True)
                    last.then_inc(s_sct, 1)

                def step(n, s, at_):
                    if not isinstance(n, int) or n >= 0:
                        scatter(n, s)
                    if not isinstance(n, int) or 0 <= n + 2 < NS:
                        pick(n + 2, (s + 2) % BODY, at_)
                    if not isinstance(n, int) or 0 <= n + 3 < NS:
                        turn(n + 3, (s + 3) % BODY)

                def blocks_of(n, steps):
                    return registers(nc, pe, blk3[0:1, bass.ds(n * HT + HT, steps * HT)], NB - 1)

                for n in range(-3, BODY):
                    step(n, n % BODY, blocks_of(n + 2, 1) if n >= -2 else None)
                with loop(nc, pe, 1, NS // BODY - 1) as g:
                    at_ = blocks_of(g * BODY + 2, BODY)
                    for s in range(BODY):
                        step(g * BODY + s, s, at_[s * HT:(s + 1) * HT])
                for n in range(NS - BODY, NS):
                    step(n, n % BODY, blocks_of(n + 2, 1) if n + 2 < NS else None)

        xn4 = at("xn4", 31 * KB, [PB, NB, D])
        xt6 = at("xt6", 106 * KB, [128, 2, 2, N], F16)
        outb = at("outb", 80 * KB, [PB, NB, D])
        fh = at("fh", 171 * KB, [128, 2, 2, FH // 128, 4 * PB], F16)
        wb = at("wb", 158 * KB, [PB, N])
        junk = at("junk", 147 * KB, [PB, N], mybir.dt.bfloat16)
        gl = at("gl", 154 * KB, [128, 2, 4 * PB])
        wrb = at("wrb", 57 * KB, [PB, D])
        b2b = at("b2b", 58 * KB, [PB, D])
        bgb = at("bgb", 59 * KB, [PB, OD])
        brb = at("brb", 59 * KB + 256, [PB, 1])
        bf1 = at("bf1", 59 * KB + 288, [128, FH // 128])
        wv = at("wv", 59 * KB + 320, [PB, NB])
        wk = at("wk", 59 * KB + 448, [PB, NB])
        cnt = at("cnt", 59 * KB + 576, [PB, NB, 3])
        rk = at("rk", 60 * KB, [PB, NB])
        den = at("den", 60 * KB + 128, [PB, 5, NH])
        earlier = at("earlier", 61 * KB, [PB, PB])
        og = at("og", 62 * KB, [PB, 5, NH, OD])
        eg = at("eg", 67 * KB, [PB, 5, NH, OD])
        junk_d = at("junk_d", 72 * KB, [PB, D])
        yt = at("yt", 73 * KB, [PB, 2, D])
        w_d = dram("w_d", (1, N))
        KEPT = max(1, N // 2) - 1
        s_b6 = sem("s_b6")
        s_og = sem("s_og")
        s_eg = sem("s_eg")
        s_v6 = sem("s_v6")
        s_d6 = sem("s_d6")
        s_n6 = sem("s_n6")
        s_wd = sem("s_wd")
        s_wbl = sem("s_wbl")
        s_wv = sem("s_wv")
        s_be = sem("s_be")
        s_k6 = sem("s_k6")
        s_c6 = sem("s_c6")
        s_ob = sem("s_ob")
        s_t6 = sem("s_t6")
        s_th = sem("s_th")
        s_tl = sem("s_tl")
        s_fu = sem("s_fu")
        s_gl = sem("s_gl")
        s_gh = sem("s_gh")
        s_gL = sem("s_gL")
        s_fd = sem("s_fd")
        s_yt = sem("s_yt")
        s_fin = sem("s_fin")
        s_out = sem("s_out")
        FM = FH // 128
        CB = 4
        CHUNKS = [(b, min(CB, NB - b)) for b in range(0, NB, CB)]
        with ExitStack() as p6:
            psT6 = [p6.enter_context(nc.psum_tensor(f"psT6{i}", [128, 2, 128], F32)) for i in range(2)]
            psU = [p6.enter_context(nc.psum_tensor(f"psU{i}", [128, CB * PB], F32)) for i in range(2)]
            psD = [p6.enter_context(nc.psum_tensor(f"psD{i}", [PB, D], F32)) for i in range(2)]
            block = p6.enter_context(nc.Block())

            @block.sync
            def _(sp):
                sp.dma_start(bgb[:, :], a["L1_gnn_b"].partition_broadcast(PB)).then_inc(s_b6, 16)
                sp.dma_start(wrb[:, :], a["L1_ffn_wr"].partition_broadcast(PB)).then_inc(s_b6, 16)
                sp.dma_start(brb[:, :], a["L1_ffn_br"].partition_broadcast(PB)).then_inc(s_b6, 16)
                sp.dma_start(b2b[:, :], a["L1_ffn_b2"].partition_broadcast(PB)).then_inc(s_b6, 16)
                sp.dma_start(bf1[:, :], a["L1_ffn_b1"]).then_inc(s_b6, 16)
                sp.wait_ge(s_wv, 1)
                with nc.allow_non_contiguous_dma(reason="one weight of a node"):
                    sp.dma_start(w_d.rearrange("o (b p) -> p (o b)", p=PB), wv[:, :]).then_inc(s_wd, 16)
                sp.wait_ge(s_wd, 16)
                sp.dma_start(wb[:, :], w_d[0, :].partition_broadcast(PB)).then_inc(s_wbl, 16)
                ov = out[0].rearrange("(b p) d -> p b d", p=PB)
                for b0, n in CHUNKS:
                    sp.wait_ge(s_fin, b0 + n)
                    sp.dma_start(ov[:, b0:b0 + n, :], outb[:, b0:b0 + n, :]).then_inc(s_out, 16)
                sp.wait_ge(s_out, 16 * len(CHUNKS))

            @block.gpsimd
            def _(pool):
                ch = Chain(pool, s_be)
                ch.step(nc.gpsimd.memset(earlier[:, :], 1.0))
                nc.gpsimd.affine_select(out=earlier[:, :], in_=earlier[:, :], compare_op=ALU.is_gt, fill=0.0,
                                        base=0, pattern=[[-1, PB]], channel_multiplier=1).then_inc(s_k6, 1)

            @block.scalar
            def _(act):
                for c in range(5):
                    act.wait_ge(s_og, c + 1)
                    nc.scalar.activation(eg[:, :, :, :], og[:, :, :, :], ACT.Exp).then_inc(s_eg, 1)
                    act.wait_ge(s_v6, c + 1)
                    nc.scalar.activation(sd3[:, 0, :], mv3[:, :, 1], ACT.Sqrt).then_inc(s_d6, 1)
                for b in range(NB):
                    act.wait_ge(s_t6, b + 1)
                    nc.scalar.activation(xt6[:, 0, :, PB * b:PB * (b + 1)], psT6[b % 2][:, :, 0:PB], ACT.Copy,
                                         scale=XS).then_inc(s_th, 1)
                n = 0
                act.wait_ge(s_b6, 80)
                for c, (b0, nb) in enumerate(CHUNKS):
                    w = nb * PB
                    for m in range(FM):
                        act.wait_ge(s_fu, n + 1)
                        if n >= 2:
                            act.wait_ge(s_gL, n - 1)
                        nc.scalar.activation(gl[:, n % 2, 0:w], psU[n % 2][:, 0:w], ACT.Gelu_apprx_tanh,
                                             bias=bf1[:, m:m + 1], scale=1.0 / (XS * WS)).then_inc(s_gl, 1)
                        act.wait_ge(s_gl, n + 1)
                        if c >= 2 and m == 0:
                            act.wait_ge(s_fd, CHUNKS[c - 2][0] + CHUNKS[c - 2][1])
                        nc.scalar.activation(fh[:, c % 2, 0, m, 0:w], gl[:, n % 2, 0:w], ACT.Copy, scale=HS).then_inc(s_gh, 1)
                        n += 1

            @block.vector
            def _(dve):
                ch = Chain(dve, s_c6)
                dve.wait_ge(s_b6, 80)
                v = acc[:, :, :].rearrange("p b (h f) -> p b h f", h=NH)
                for c in range(5):
                    cs = slice(5 * c, 5 * c + 5)
                    ch.step(nc.vector.tensor_scalar(den[:, :, :], v[:, cs, :, OD], 1e-12, None, ALU.max))
                    ch.step(nc.vector.reciprocal(den[:, :, :], den[:, :, :]))
                    for b in range(5):
                        ch.mark(nc.vector.tensor_tensor(og[:, b, :, :], v[:, 5 * c + b, :, 0:OD],
                                                        den[:, b, :].unsqueeze(2).to_broadcast([PB, NH, OD]), ALU.mult))
                    dve.wait_ge(ch.sem, ch.n)
                    for b in range(5):
                        nc.vector.tensor_tensor(og[:, b, :, :], og[:, b, :, :],
                                                bgb[:, :].unsqueeze(1).to_broadcast([PB, NH, OD]), ALU.add).then_inc(s_ob, 1)
                    dve.wait_ge(s_ob, 5 * c + 5)
                    dve.sem_inc(s_og, 1)
                    dve.wait_ge(s_eg, c + 1)
                    ch.step(nc.vector.tensor_scalar(eg[:, :, :, :], eg[:, :, :, :], 1.0, -1.0, ALU.min, ALU.add))
                    ch.step(nc.vector.tensor_tensor(og[:, :, :, :], og[:, :, :, :], eg[:, :, :, :], ALU.max))
                    ch.step(nc.vector.tensor_tensor(x2[:, cs, :].rearrange("p b d -> p (b d)"),
                                                    x2[:, cs, :].rearrange("p b d -> p (b d)"),
                                                    og[:, :, :, :].rearrange("p b h f -> p (b h f)"), ALU.add))
                    normalise(dve, ch, x2, xn4, c, s_v6, s_d6, s_n6)
                    for b in range(5 * c, 5 * c + 5):
                        ch.mark(nc.vector.scalar_tensor_tensor(junk_d[:, :], xn4[:, b, :], 1.0, wrb[:, :], ALU.mult, ALU.mult,
                                                               accum_out=wv[:, b:b + 1]))
                        dve.wait_ge(ch.sem, ch.n)
                    ch.step(nc.vector.tensor_tensor(x2[:, cs, :], x2[:, cs, :], xn4[:, cs, :], ALU.add))
                nc.vector.tensor_scalar(wv[:, :], wv[:, :], brb[:, :], None, ALU.add).then_inc(s_wv, 1)
                for b in range(NB):
                    dve.wait_ge(s_th, b + 1)
                    nc.vector.scalar_tensor_tensor(xt6[:, 1, :, PB * b:PB * (b + 1)], psT6[b % 2][:, :, 0:PB], XS,
                                                   xt6[:, 0, :, PB * b:PB * (b + 1)], ALU.mult, ALU.subtract).then_inc(s_tl, 1)
                dve.wait_ge(s_k6, 1)
                dve.wait_ge(s_wbl, 16)
                dve.wait_ge(s_wv, 1)

                def finish(c):
                    b0, nb = CHUNKS[c]
                    for b in range(b0, b0 + nb):
                        dve.wait_ge(s_fd, b + 1)
                        ch.step(nc.vector.scalar_tensor_tensor(yt[:, b % 2, :], psD[b % 2][:, :], 1.0 / (HS * WS), b2b[:, :],
                                                               ALU.mult, ALU.add))
                        dve.sem_inc(s_yt, 1)
                        nc.vector.scalar_tensor_tensor(outb[:, b, :], yt[:, b % 2, :], wk[:, b:b + 1], x2[:, b, :],
                                                       ALU.mult, ALU.add).then_inc(s_fin, 1)

                n = 0
                for c, (b0, nb) in enumerate(CHUNKS):
                    ch.step(nc.vector.memset(cnt[:, b0:b0 + nb, :], 0.0))
                    for b in range(b0, b0 + nb):
                        if b:
                            ch.step(nc.vector.tensor_scalar(junk[:, 0:PB * b], wb[:, 0:PB * b], wv[:, b:b + 1], 0.0,
                                                            ALU.is_ge, ALU.add, accum_out=cnt[:, b, 0:1]))
                        ch.step(nc.vector.tensor_scalar(junk[:, PB * b:N], wb[:, PB * b:N], wv[:, b:b + 1], 0.0,
                                                        ALU.is_gt, ALU.add, accum_out=cnt[:, b, 1:2]))
                        ch.step(nc.vector.scalar_tensor_tensor(junk[:, 0:PB], wb[:, PB * b:PB * (b + 1)], wv[:, b:b + 1],
                                                               earlier[:, :], ALU.is_equal, ALU.mult, accum_out=cnt[:, b, 2:3]))
                    bs = slice(b0, b0 + nb)
                    ch.step(nc.vector.tensor_reduce(rk[:, bs], cnt[:, bs, :], AX_X, ALU.add))
                    ch.step(nc.vector.scalar_tensor_tensor(wk[:, bs], rk[:, bs], float(KEPT), wv[:, bs], ALU.is_lt, ALU.mult))
                    w = nb * PB
                    for m in range(FM):
                        dve.wait_ge(s_gh, n + 1)
                        nc.vector.scalar_tensor_tensor(fh[:, c % 2, 1, m, 0:w], gl[:, n % 2, 0:w], HS,
                                                       fh[:, c % 2, 0, m, 0:w], ALU.mult, ALU.subtract).then_inc(s_gL, 1)
                        n += 1
                    if c >= 1:
                        finish(c - 1)
                finish(len(CHUNKS) - 1)

            @block.tensor
            def _(pe):
                for b in range(NB):
                    pe.wait_ge(s_n6, b + 1)
                    if b >= 2:
                        pe.wait_ge(s_tl, b - 1)
                    for k in range(2):
                        last = nc.tensor.transpose(psT6[b % 2][:, k, 0:PB], xn4[:, b, 128 * k:128 * (k + 1)], ident[0:PB, 0:PB])
                    last.then_inc(s_t6, 1)

                def down(c):
                    b0, nb = CHUNKS[c]
                    pe.wait_ge(s_gL, FM * (c + 1))
                    for b in range(b0, b0 + nb):
                        if b >= 2:
                            pe.wait_ge(s_yt, b - 1)
                        cols = slice(PB * (b - b0), PB * (b - b0 + 1))
                        for m in range(FM):
                            for j, (sh, sw) in enumerate(((0, 0), (0, 1), (1, 0))):
                                last = nc.tensor.matmul(psD[b % 2][:, :], fh[:, c % 2, sh, m, cols], f2[:, sw, m, :],
                                                        start=(m == 0 and j == 0), stop=(m == FM - 1 and j == 2))
                        last.then_inc(s_fd, 1)

                n = 0
                for c, (b0, nb) in enumerate(CHUNKS):
                    cols = slice(PB * b0, PB * (b0 + nb))
                    pe.wait_ge(s_tl, b0 + nb)
                    for m in range(FM):
                        if n >= 2:
                            pe.wait_ge(s_gl, n - 1)
                        terms = [(sw, sx, k) for k in range(2) for sw, sx in ((0, 0), (0, 1), (1, 0))]
                        for i, (sw, sx, k) in enumerate(terms):
                            last = nc.tensor.matmul(psU[n % 2][:, 0:nb * PB], f1[:, sw, k, 128 * m:128 * (m + 1)],
                                                    xt6[:, sx, k, cols], start=(i == 0), stop=(i == len(terms) - 1))
                        last.then_inc(s_fu, 1)
                        n += 1
                    if c >= 1:
                        down(c - 1)
                down(len(CHUNKS) - 1)




def kernel(**inputs):
    import numpy as np
    import concourse.bacc as bacc
    from concourse.bass_utils import run_bass_kernel_spmd
    nc = bacc.Bacc("TRN2", target_bir_lowering=False, num_devices=1)
    arrays, args = {}, {}
    for name, v in [*inputs.items(), ("L1_gnn_WT", np.asarray(inputs["L1_gnn_W"]).T)]:
        v = np.ascontiguousarray(v)
        if name in ("src", "dst"):
            padded = np.full((T1 * ET,), N, v.dtype)
            padded[0:E] = v
            v = np.ascontiguousarray(padded.reshape(T1, ET).T)
        if name in VECTORS or name == "L1_ffn_b1":
            v = np.ascontiguousarray(v.reshape(-1, 128).T)
        if name in ("L0_ffn_router_w", "L1_gnn_Wl", "L1_gnn_Wr"):
            v = np.ascontiguousarray(v.T)
        if name == "L1_ffn_wr":
            v = v.reshape(-1)
        if name in ("L0_ffn_w1", "L0_ffn_w3"):
            v = np.concatenate([v.transpose(0, 2, 1), np.zeros((X, D, HP - v.shape[1]), v.dtype)], axis=2)
        if name == "L0_ffn_w2":
            v = np.concatenate([v.transpose(0, 2, 1), np.zeros((X, HP - v.shape[2], D), v.dtype)], axis=1)
        if v.ndim == 0:
            v = v.reshape(1)
        arrays["in_" + name] = v
        args[name] = nc.dram_tensor("in_" + name, v.shape, mybir.dt.from_np(v.dtype), kind="ExternalInput").ap()
    outs = [nc.dram_tensor("out_0", (N, D), F32, kind="ExternalOutput").ap()]
    program(nc, args, outs)
    r = run_bass_kernel_spmd(nc, [arrays], core_ids=[0])
    return r.results[0]["out_0"]
```

```python
from contextlib import ExitStack

import concourse.bass as bass
from concourse import mybir

F32 = mybir.dt.float32
F16 = mybir.dt.float16
I32 = mybir.dt.int32
U32 = mybir.dt.uint32
ALU = mybir.AluOpType
ACT = mybir.ActivationFunctionType
AX_X = mybir.AxisListType.X
RMAX = bass.bass_isa.ReduceOp.max

N = 3125
D = 256
E = 50000
PB = 125
NB = N // PB
ET = 128
TPR = 8
HT = TPR // 2
R1 = -(-E // (ET * TPR))
T1 = R1 * TPR
R3 = (T1 * ET + NB * (ET - 1)) // ET // TPR
T3 = R3 * TPR
WIN = 128
X = 8
K2 = 2
HM = 6
HP = HM * 128
T2 = (K2 * N + X * 127) // 128
XS = 256.0
WS = 1024.0
HS = 64.0
NACC = N + WIN
NH, OD = 4, 64
RW = NH + OD + 1
FH = 1024
LN_EPS = 1e-5
BN_EPS = 1e-5
MAGIC = 1.5 * 2.0 ** 23
assert T3 * ET >= T1 * ET + NB * (ET - 1) - ET + 1 and NB * PB == N


VECTORS = [f"L0_gnn_{v}{l}" for v in ("b", "g", "beta") for l in (1, 2, 3)]


def wait_apart(eng, sem, value, tick):
    eng.wait_ge(sem, value)
    eng.sem_inc(tick, 1)


def loop(nc, eng, start, end):
    return nc.Fori(start, end, engines=[eng.engine], hint_back_edge=True)


def registers(nc, eng, values, top):
    return nc.values_load_multi_w_load_instructions(
        values, engines=[eng.engine], min_val=0, max_val=top,
        skip_runtime_bounds_check_because="the kernel clamps them where it computes them")[1]


class Chain:

    def __init__(self, eng, sem):
        self.eng, self.sem, self.n = eng, sem, 0

    def mark(self, ins):
        ins.then_inc(self.sem, 1)
        self.n += 1

    def step(self, ins):
        self.mark(ins)
        self.eng.wait_ge(self.sem, self.n)


def program(nc, a, out):
    with ExitStack() as ctx:
        taken = []

        def sem(name):
            taken.append(nc.alloc_semaphore(name))
            return taken[-1]

        def free_semaphores():
            nc.clear_and_free_semaphores(taken)
            nc.all_engine_barrier()
            taken.clear()

        def psum(name, shape, dt=F32):
            return ctx.enter_context(nc.psum_tensor(name, shape, dt))

        KB = 1024
        BASE = 16512

        def at(name, offset, shape, dt=F32):
            return nc.alloc_sbuf_tensor_at(name, shape, dt, offset=BASE + offset)

        def dram(name, shape, dt=F32):
            return nc.dram_tensor(name, shape, dt, kind="Internal").ap()

        xn_d = dram("xn_d", (N, D))
        rec_d = dram("rec_d", (ET, T3 * 2), I32)

        ident = at("ident", 0, [128, 128])
        iota = at("iota", 512, [128, 128])
        rec = at("rec", 1 * KB, [128, T1, 2], I32)
        kb = at("kb", 1 * KB + 3136, [128, T1])
        accT = at("accT", 6 * KB, [128, 2, NACC])
        s_c = [sem(f"s_c{i}") for i in range(4)]

        W2 = at("W2", 158 * KB, [128, 2, 4, 1024], F16)
        W3 = at("W3", 174 * KB, [128, 2, 8, 512], F16)
        W1 = at("W1", 190 * KB, [128, 2, 512])
        W4 = at("W4", 194 * KB, [128, 2, 4, 256], F16)
        pieces = []
        for r in range(4):
            pieces.append((a["L0_gnn_W2"][128 * r:128 * (r + 1), :], [W2[:, s, r, :] for s in range(2)], 1024))
        for r in range(4):
            pieces.append((a["L0_gnn_W3"].rearrange("(k p) n -> p k n", p=128)[:, 2 * r:2 * r + 2, :],
                           [W3[:, s, 2 * r:2 * r + 2, :] for s in range(2)], 512))
        pieces.append((a["L0_gnn_W4"].rearrange("(k p) n -> p k n", p=128), [W4[:, s, :, :] for s in range(2)], 256))

        def staged(n):
            t, w = wst[:, n % 2, :], pieces[n][2]
            return t if w == 1024 else t.rearrange("p (k n) -> p k n", n=w)

        VAT = (0, 1, 3, 4)
        vec = at("vec", 206 * KB, [128, 3, 16])
        s_vec = sem("s_vec")
        s_w1 = sem("s_w1")
        s_wst = [sem(f"s_wst{i}") for i in range(2)]
        s_whi = sem("s_whi")
        s_wlo = sem("s_wlo")
        s_rec0 = sem("s_rec0")
        s_recst = sem("s_recst")
        s_rank = sem("s_rank")

        o = 104 * KB
        S = at("S", 33 * KB, [128, NB, T1])
        same = at("same", 72 * KB, [128, NB, T1], F16)
        wst = at("wst", 92 * KB, [128, 2, 1024])
        rec0 = at("rec0", 198 * KB, [128, T3 * 2], I32)
        x = at("x", o, [PB, NB, D]); o += 25600
        G = at("G", o, [128, TPR, D]); o += 8192
        oh = at("oh", 202 * KB, [128, TPR, WIN])
        src_i = at("src_i", o, [128, T1], I32); o += 1568
        dst_i = at("dst_i", o, [128, T1], I32); o += 1568
        gat_i = at("gat_i", o, [128, T1], I32); o += 1568
        srcf = at("srcf", o, [128, T1]); o += 1568
        tmpf = at("tmpf", o, [128, T1]); o += 1568
        span = at("span", o, [128, 2, T1]); o += 3136
        spanr = at("spanr", 100 * KB, [128, 2, T1])
        dstw = at("dstw", o, [128, T1 + TPR]); o += 1600
        basef = at("basef", o, [128, T1]); o += 1568
        base_i = at("base_i", o, [1, T1], I32); o += 1568
        stage_i = at("stage_i", o, [128, 2, HT], I32); o += 32
        bst = at("bst", o, [PB, NB, 6]); o += 608
        mv = at("mv", o, [PB, NB, 2]); o += 224
        std = at("std", o, [PB, NB]); o += 128
        rstd = at("rstd", o, [PB, NB]); o += 128
        eps1 = at("eps1", o, [128, 1]); o += 32
        nwf = at("nwf", o, [128, 8]); o += 32
        nw_i = at("nw_i", o, [128, 8], I32); o += 32

        assert o <= 158 * KB
        s_x = [sem(f"s_x{c}") for c in range(5)]
        s_edges = sem("s_edges")
        s_eps = sem("s_eps")
        s_const = sem("s_const")
        s_var = sem("s_var")
        s_std = sem("s_std")
        s_xn = sem("s_xn")
        s_xnst = sem("s_xnst")
        s_tr = sem("s_tr")
        s_trc = sem("s_trc")
        s_eps1 = sem("s_eps1")
        s_span = sem("s_span")
        s_spanr = sem("s_spanr")
        s_idx = sem("s_idx")
        s_nw = sem("s_nw")
        s_pad = sem("s_pad")
        s_staged = sem("s_staged")
        s_gat = [sem(f"s_gat{i}") for i in range(TPR)]
        s_oh = [sem("s_ohA"), sem("s_ohB")]
        s_slots = sem("s_slots")
        s_banks = sem("s_banks")
        s_pass = sem("s_pass")
        s_halves = sem("s_halves")
        s_tick = [sem("s_tick_act"), sem("s_tick_dve"), sem("s_tick_pe"), sem("s_tick_sp")]

        GRP = [(q, min(4, NB - q)) for q in range(0, NB, 4)]

        with ExitStack() as p1:
            psT = [p1.enter_context(nc.psum_tensor(f"psT{i}", [128, 4 * PB], F32)) for i in range(2)]
            psA = [p1.enter_context(nc.psum_tensor(f"psA{i}", [128, 2, 2, WIN], F32)) for i in range(4)]
            block = p1.enter_context(nc.Block())
            CH = NB // 5

            def store_xn(sp):
                for c in range(5):
                    sp.wait_ge(s_xn, CH * (c + 1))
                    sp.dma_start(xn_d.rearrange("(b p) d -> p b d", p=PB)[:, CH * c:CH * (c + 1), :],
                                 x[:, CH * c:CH * (c + 1), :]).then_inc(s_xnst, 16)

            @block.sync
            def _(sp):
                for c in range(5):
                    sp.dma_start(x[:, CH * c:CH * (c + 1), :],
                                 a["x"].rearrange("(b p) d -> p b d", p=PB)[:, CH * c:CH * (c + 1), :]).then_inc(s_x[c], 16)
                sp.dma_start(src_i[:, :], a["src"]).then_inc(s_edges, 16)
                sp.dma_start(dst_i[:, :], a["dst"]).then_inc(s_edges, 16)
                sp.dma_start(eps1[:, :], a["L0_gnn_eps"].partition_broadcast(128)).then_inc(s_eps, 16)
                sp.dma_start(W1[:, :, :], a["L0_gnn_W1"].rearrange("(k p) n -> p k n", p=128)).then_inc(s_w1, 16)
                for n in range(len(pieces)):
                    if n == 2:
                        store_xn(sp)
                    if n >= 2:
                        sp.wait_ge(s_wlo, n - 1)
                    sp.dma_start(staged(n), pieces[n][0]).then_inc(s_wst[n % 2], 16)
                sp.wait_ge(s_rec0, 1)
                sp.dma_start(rec_d, rec0[:, :]).then_inc(s_recst, 16)
                for l in range(3):
                    for j, name in enumerate(("b", "g", "beta")):
                        sp.dma_start(vec[:, j, 4 * VAT[l]:4 * VAT[l + 1]], a[f"L0_gnn_{name}{l + 1}"]).then_inc(s_vec, 16)

            @block.gpsimd
            def _(pool):
                ch = Chain(pool, s_c[0])
                nc.gpsimd.iota(iota[:, :], pattern=[[1, 128]], base=0, channel_multiplier=0,
                               allow_small_or_imprecise_dtypes=True).then_inc(s_const, 1)
                ch.step(nc.gpsimd.memset(ident[:, :], 0.0))
                nc.gpsimd.affine_select(out=ident[:, :], in_=ident[:, :], compare_op=ALU.not_equal, fill=1.0,
                                        base=0, pattern=[[-1, 128]], channel_multiplier=1).then_inc(s_const, 1)
                nc.gpsimd.memset(accT[:, :, N:NACC], 0.0).then_inc(s_pad, 1)
                nc.gpsimd.memset(rec0[:, :], PB).then_inc(s_rec0, 1)
                pool.wait_ge(s_span, 1)
                nc.gpsimd.partition_all_reduce(spanr[:, :, :].rearrange("p a t -> p (a t)"),
                                               span[:, :, :].rearrange("p a t -> p (a t)"), 128, RMAX).then_inc(s_spanr, 1)
                pool.wait_ge(s_nw, 1)
                nw = pool.value_load(nw_i[0:1, 0:1], min_val=1, max_val=NB)
                pool.wait_ge(s_idx, 1)
                pool.wait_ge(s_xnst, 80)
                with loop(nc, pool, 0, nw) as w:
                    with loop(nc, pool, 0, R1) as g:
                        it = w * R1 + g
                        for h in range(2):
                            pool.wait_ge(s_slots, it * TPR + HT * (h + 1))
                            nc.gpsimd.tensor_copy(stage_i[:, h, :], gat_i[:, bass.ds(g * TPR + h * HT, HT)]).then_inc(s_staged, 1)
                            pool.wait_ge(s_staged, it * 2 + h + 1)
                            pool.sem_inc(s_halves, 1)
                            for j in range(HT):
                                i = h * HT + j
                                pool.indirect_dma_start(
                                    out=G[:, i, :], out_offset=None, in_=xn_d,
                                    in_offset=bass.IndirectOffsetOnAxis(ap=stage_i[:, h, j:j + 1], axis=0)).then_inc(s_gat[i], 16)

            @block.scalar
            def _(act):
                for c in range(5):
                    act.wait_ge(s_var, c + 1)
                    nc.scalar.activation(std[:, CH * c:CH * (c + 1)], mv[:, CH * c:CH * (c + 1), 1], ACT.Sqrt).then_inc(s_std, 1)
                for n in range(len(pieces)):
                    act.wait_ge(s_wst[n % 2], 16 * (n // 2 + 1))
                    nc.scalar.activation(pieces[n][1][0], staged(n), ACT.Copy, scale=WS).then_inc(s_whi, 1)
                act.wait_ge(s_eps1, 1)
                for q, (b0, n) in enumerate(GRP):
                    for h in range(2):
                        act.wait_ge(s_tr, 2 * q + h + 1)
                        nc.scalar.activation(accT[:, h, PB * b0:PB * (b0 + n)], psT[h][:, 0:PB * n], ACT.Copy,
                                             scale=eps1[:, :]).then_inc(s_trc, 1)

            @block.vector
            def _(dve):
                ch = Chain(dve, s_c[1])
                dve.wait_ge(s_edges, 32)
                nc.vector.tensor_copy(span[:, 1, :], dst_i[:, :])
                ch.step(nc.vector.tensor_copy(srcf[:, :], src_i[:, :]))
                ch.step(nc.vector.tensor_scalar(span[:, 0, :], span[:, 1, :], -1.0, None, ALU.mult))
                dve.sem_inc(s_span, 1)
                ch.step(nc.vector.tensor_scalar(tmpf[:, :], srcf[:, :], float(N - 1), None, ALU.min))
                nc.vector.tensor_copy(gat_i[:, :], tmpf[:, :]).then_inc(s_idx, 1)
                ch.step(nc.vector.tensor_scalar(kb[:, :], srcf[:, :], 1.0 / PB, -(PB // 2 * 1.0) / PB, ALU.mult, ALU.add))
                ch.step(nc.vector.tensor_scalar(kb[:, :], kb[:, :], MAGIC, MAGIC, ALU.add, ALU.subtract))
                ch.step(nc.vector.tensor_scalar(kb[:, :], kb[:, :], float(NB - 1), None, ALU.min))
                ch.step(nc.vector.scalar_tensor_tensor(tmpf[:, :], kb[:, :], -float(PB), srcf[:, :], ALU.mult, ALU.add))
                nc.vector.tensor_copy(rec[:, :, 0], tmpf[:, :])
                ch.step(nc.vector.tensor_scalar(rec[:, :, 1], span[:, 1, :], float(N - 1), None, ALU.min))
                dve.wait_ge(s_eps, 16)
                nc.vector.tensor_scalar(eps1[:, :], eps1[:, :], 1.0, None, ALU.add).then_inc(s_eps1, 1)
                for c in range(5):
                    dve.wait_ge(s_x[c], 16)
                    for b in range(CH * c, CH * (c + 1)):
                        ch.mark(nc.vector.bn_stats(bst[:, b, :], x[:, b, :]))
                    dve.wait_ge(ch.sem, ch.n)
                    for b in range(CH * c, CH * (c + 1)):
                        ch.mark(nc.vector.bn_aggr(mv[:, b, :], bst[:, b, :]))
                    dve.wait_ge(ch.sem, ch.n)
                    cs = slice(CH * c, CH * (c + 1))
                    nc.vector.tensor_scalar(mv[:, cs, 1], mv[:, cs, 1], LN_EPS, None, ALU.add).then_inc(s_var, 1)
                    dve.wait_ge(s_std, c + 1)
                    ch.step(nc.vector.reciprocal(rstd[:, cs], std[:, cs]))
                    for b in range(CH * c, CH * (c + 1)):
                        nc.vector.tensor_scalar(x[:, b, :], x[:, b, :], mv[:, b, 0:1], rstd[:, b:b + 1],
                                                ALU.subtract, ALU.mult).then_inc(s_xn, 1)
                dve.wait_ge(s_spanr, 1)
                ch.step(nc.vector.tensor_tensor(tmpf[:, :], spanr[:, 0, :], spanr[:, 1, :], ALU.add))
                ch.step(nc.vector.tensor_reduce(nwf[:, 0:1], tmpf[:, :], AX_X, ALU.max))
                ch.step(nc.vector.tensor_copy(nw_i[:, 1:2], nwf[:, 0:1]))
                ch.step(nc.vector.tensor_scalar(nw_i[:, 2:3], nw_i[:, 1:2], WIN.bit_length() - 1, None, ALU.arith_shift_right))
                nc.vector.tensor_scalar(nw_i[:, 0:1], nw_i[:, 2:3], 1.0, None, ALU.add).then_inc(s_nw, 1)
                nc.vector.memset(dstw[:, T1:T1 + TPR], -1.0)
                nc.vector.tensor_scalar(basef[:, :], spanr[:, 0, :], -1.0, -float(WIN), ALU.mult, ALU.add)
                ch.step(nc.vector.tensor_tensor(dstw[:, 0:T1], span[:, 1, :], spanr[:, 0, :], ALU.add))
                ch.step(nc.vector.tensor_scalar(dstw[:, 0:T1], dstw[:, 0:T1], float(WIN), None, ALU.add))
                dve.wait_ge(s_nw, 1)
                nw = dve.value_load(nw_i[0:1, 0:1], min_val=1, max_val=NB)
                for n in range(len(pieces)):
                    dve.wait_ge(s_whi, n + 1)
                    nc.vector.scalar_tensor_tensor(pieces[n][1][1], staged(n), WS, pieces[n][1][0],
                                                   ALU.mult, ALU.subtract).then_inc(s_wlo, 1)
                dve.wait_ge(s_const, 2)
                dve.wait_ge(s_trc, 2 * len(GRP))
                dve.wait_ge(s_pad, 1)
                dve.sem_inc(s_banks, TPR)

                def one_hots(h, col):
                    nc.vector.tensor_tensor(
                        oh[:, h * HT:(h + 1) * HT, :],
                        iota[:, :].unsqueeze(1).to_broadcast([128, HT, WIN]),
                        dstw[:, bass.ds(col, HT)].unsqueeze(2).to_broadcast([128, HT, WIN]),
                        ALU.is_equal).then_inc(s_oh[h], 1)

                with loop(nc, dve, 0, nw) as w:
                    nc.vector.tensor_scalar(dstw[:, 0:T1], dstw[:, 0:T1], -float(WIN), None, ALU.add)
                    nc.vector.tensor_scalar(basef[:, :], basef[:, :], float(WIN), None, ALU.add).then_inc(s_pass, 1)
                    dve.wait_ge(s_pass, w * 2 + 1)
                    nc.vector.tensor_scalar(base_i[:, :], basef[0:1, :], float(N), None, ALU.min).then_inc(s_pass, 1)
                    dve.wait_ge(s_pass, w * 2 + 2)
                    dve.wait_ge(s_slots, w * (R1 * TPR) + TPR)
                    one_hots(0, 0)

                    def round_(g, rank):
                        it = w * R1 + g
                        if rank:
                            nc.vector.tensor_scalar(same[:, bass.ds(g, 1), :].rearrange("p a t -> p (a t)"), kb[:, :],
                                                    iota[:, bass.ds(g, 1)], None, ALU.is_equal).then_inc(s_rank, 1)
                        at_ = registers(nc, dve, base_i[0:1, bass.ds(g * TPR, TPR)], N)
                        dve.wait_ge(s_slots, it * TPR + TPR)
                        one_hots(1, g * TPR + HT)
                        for i in range(TPR):
                            if i == HT:
                                one_hots(0, g * TPR + TPR)
                            if i % 2 == 0:
                                dve.wait_ge(s_slots, it * TPR + TPR + i + 2)
                            dve.wait_ge(s_banks, it * TPR + TPR + i)
                            nc.vector.tensor_tensor(accT[:, :, bass.ds(at_[i], WIN)], accT[:, :, bass.ds(at_[i], WIN)],
                                                    psA[i // 2][:, i % 2, :, :], ALU.add).then_inc(s_banks, 1)
                        if rank:
                            dve.wait_ge(s_rank, w * NB + g + 1)
                            flat = same[:, bass.ds(g, 1), :].rearrange("p a t -> p (a t)")
                            nc.vector.tensor_tensor_scan(S[:, bass.ds(g, 1), :].rearrange("p a t -> p (a t)"),
                                                         flat, flat, 0.0, ALU.add, ALU.max)

                    with loop(nc, dve, 0, NB) as g:
                        round_(g, True)
                    with loop(nc, dve, NB, R1) as g:
                        round_(g, False)

            @block.tensor
            def _(pe):
                pe.wait_ge(s_const, 2)
                for q, (b0, n) in enumerate(GRP):
                    for h in range(2):
                        pe.wait_ge(s_xn, b0 + n)
                        if q:
                            pe.wait_ge(s_trc, 2 * q - 1 + h)
                        for b in range(n):
                            last = nc.tensor.transpose(psT[h][:, PB * b:PB * (b + 1)], x[:, b0 + b, 128 * h:128 * (h + 1)],
                                                       ident[0:PB, 0:PB])
                        last.then_inc(s_tr, 1)
                pe.wait_ge(s_nw, 1)
                nw = pe.value_load(nw_i[0:1, 0:1], min_val=1, max_val=NB)
                pe.sem_inc(s_slots, TPR)
                with loop(nc, pe, 0, nw) as w:
                    with loop(nc, pe, 0, R1) as g:
                        it = w * R1 + g
                        for i in range(TPR):
                            pe.wait_ge(s_gat[i], it * 16 + 16)
                            if i % HT == 0:
                                if i == 0:
                                    pe.wait_ge(s_oh[0], it + w + 1)
                                else:
                                    pe.wait_ge(s_oh[1], it + 1)
                            if i % 2 == 0:
                                pe.wait_ge(s_banks, it * TPR + i + 2)
                            for h in range(2):
                                last = nc.tensor.matmul(psA[i // 2][:, i % 2, h, :], G[:, i, 128 * h:128 * (h + 1)],
                                                        oh[:, i, :], start=True, stop=True)
                            last.then_inc(s_slots, 1)

        z2 = at("z2", 6 * KB, [128, 8, N])
        z1 = at("z1", 104 * KB, [128, 4, N])
        eb = at("eb", 198 * KB, [128, 2, 500])
        yb = at("yb", 202 * KB, [128, 2, 500])
        bst2 = at("bst2", 206 * KB + 192, [128, 8, 7, 6])
        mv2 = at("mv2", 206 * KB + 1536, [128, 8, 2])
        cf = at("cf", 206 * KB + 1600, [128, 3, 8])
        x2 = at("x2", 6 * KB, [PB, NB, D])
        b4 = at("b4", 33 * KB, [PB, D])
        ones16 = at("ones16", 1 * KB + 4800, [128, 128], F16)
        later = at("later", 92 * KB, [128, 128])
        ones = at("ones", 92 * KB + 512, [128, 128])
        pos = at("pos", 94 * KB, [128, T1])
        pos_i = at("pos_i", 96 * KB, [128, T1], I32)
        row_i = at("row_i", 98 * KB, [128, T1], I32)
        iotaT = at("iotaT", 100 * KB, [T3 // HT, HT])
        gr = at("gr", 102 * KB, [128, 4, NB])
        gr_i = at("gr_i", 102 * KB + 512, [128, 2, NB], I32)
        behind = at("behind", 101 * KB, [T3 // HT, HT, NB])
        blk_i = at("blk_i", 101 * KB + 512, [T3 // HT, HT], I32)
        posd = at("posd", 1 * KB + 3136, [128, T1], I32)
        stp = at("stp", 1 * KB + 4704, [128, 2, HT], I32)
        str_ = at("str_", 1 * KB + 4736, [128, 2, HT, 2], I32)
        LATE = 12
        blk_d = dram("blk_d", (1, T3), I32)
        zero = at("zero", 153 * KB, [128, D])
        xs_d = dram("xs_d", (T2 * 128, D))

        s_c2 = [sem(f"s_c2{i}") for i in range(4)]
        s_k2 = sem("s_k2")
        s_zero = sem("s_zero")
        s_zst = sem("s_zst")
        s_cnt = sem("s_cnt")
        s_pos = sem("s_pos")
        s_blk = sem("s_blk")
        s_blkst = sem("s_blkst")
        s_stg = sem("s_stg")
        s_sc = [sem("s_sc0"), sem("s_sc1")]
        s_sq = sem("s_sq")
        s_sd = sem("s_sd")
        s_cf = sem("s_cf")
        s_mm = [sem(f"s_mm{l}") for l in range(4)]
        s_ev = [sem(f"s_ev{l}") for l in range(4)]
        s_e = [None] + [sem(f"s_e{l}") for l in range(1, 4)]
        s_u = [None] + [sem(f"s_u{l}") for l in range(1, 4)]
        s_hi = [None] + [sem(f"s_hi{l}") for l in range(1, 4)]
        s_h = [None] + [sem(f"s_h{l}") for l in range(1, 4)]
        s_y = [None] + [sem(f"s_y{l}") for l in range(1, 4)]
        s_st = sem("s_st")
        s_xr = sem("s_xr")
        s_b4 = sem("s_b4")
        s_b4c = sem("s_b4c")
        s_ones16 = sem("s_ones16")

        PIECES = 6
        PW = HP * 2
        we = at("we", 57 * KB, [128, X * PIECES * PW], F16)
        raw = at("raw", 63 * KB, [128, X * PIECES, HP])
        s_raw = [sem(f"s_raw{e}") for e in range(X)]
        s_last = sem("s_last")
        s_ex = sem("s_ex")
        EARLY = (0, 1, 5, 6)

        def load_expert(sp, e):
            for j, name in enumerate(("w1", "w3")):
                sp.dma_start(raw[:, e * PIECES + 2 * j:e * PIECES + 2 * j + 2, :],
                             a["L0_ffn_" + name][e].rearrange("(k p) h -> p k h", p=128)).then_inc(s_raw[e], 16)
            for j in range(2):
                if e == X - 1 and j == 1:
                    sp.wait_ge(s_ex, 1)
                sp.dma_start(raw[:, e * PIECES + 4 + j, :].rearrange("p (k c) -> p k c", c=D),
                             a["L0_ffn_w2"][e].rearrange("(k p) c -> p k c", p=128)[:, 3 * j:3 * j + 3, :]).then_inc(
                                 s_raw[e] if e < X - 1 or j == 0 else s_last, 16)

        ZIN = [accT, z1, z2, z1]
        ZOUT = [z1, z2, z1, None]
        KR = [2, 4, 8, 4]
        MR = [4, 8, 4, 2]
        CW, CN = 4 * PB, 6
        with ExitStack() as p2:
            psZ = [p2.enter_context(nc.psum_tensor(f"psZ{i}", [128, 500], F32)) for i in range(4)]
            psR = p2.enter_context(nc.psum_tensor("psR", [128, 512], F32))
            psO = [p2.enter_context(nc.psum_tensor(f"psO{i}", [PB, 2, D], F32)) for i in range(2)]
            block = p2.enter_context(nc.Block())

            def halves(l, k, c0, w):
                f = ZIN[l][:, k, :].bitcast(F16)
                return f[:, bass.ds(c0 * 2, w)], f[:, bass.ds(c0 * 2 + w, w)]

            def stage(pool, g, h):
                nc.gpsimd.tensor_copy(stp[:, h, :], posd[:, bass.ds(g * TPR + h * HT, HT)])
                nc.gpsimd.tensor_copy(str_[:, h, :, :], rec[:, bass.ds(g * TPR + h * HT, HT), :]).then_inc(s_stg, 1)
                pool.wait_ge(s_stg, g * 2 + h + 1)
                pool.sem_inc(s_halves, 1)
                for j in range(HT):
                    pool.indirect_dma_start(
                        out=rec_d.rearrange("p (t r) -> (p t) r", r=2),
                        out_offset=bass.IndirectOffsetOnAxis(ap=stp[:, h, j:j + 1], axis=0),
                        in_=str_[:, h, j, :], in_offset=None).then_inc(s_sc[h], 16)

            @block.sync
            def _(sp):
                sp.wait_ge(s_zero, 1)
                sp.dma_start(xs_d.rearrange("(t p) d -> p t d", p=128),
                             zero[:, :].unsqueeze(1).to_broadcast([128, T2, D])).then_inc(s_zst, 16)
                sp.wait_ge(s_blk, 1)
                sp.dma_start(blk_d.rearrange("o (p j) -> (o p) j", j=HT), blk_i[:, :]).then_inc(s_blkst, 16)
                sp.wait_ge(s_mm[2], 4 * 7)
                sp.dma_start(x2[:, :, :], a["x"].rearrange("(b p) d -> p b d", p=PB)).then_inc(s_xr, 16)
                sp.dma_start(b4[:, :], a["L0_gnn_b4"].partition_broadcast(PB)).then_inc(s_b4, 16)
                sp.wait_ge(s_blkst, 16)
                sp.wait_ge(s_zst, 16)
                for e in EARLY:
                    load_expert(sp, e)

            @block.gpsimd
            def _(pool):
                ch = Chain(pool, s_c2[0])
                nc.gpsimd.memset(zero[:, :], 0.0).then_inc(s_zero, 1)
                nc.gpsimd.memset(ones[:, :], 1.0)
                ch.step(nc.gpsimd.memset(later[:, :], 1.0))
                ch.step(nc.gpsimd.affine_select(out=later[:, :], in_=later[:, :], compare_op=ALU.is_gt, fill=0.0,
                                                base=0, pattern=[[1, 128]], channel_multiplier=-1))
                ch.step(nc.gpsimd.iota(iotaT[:, :], pattern=[[1, HT]], base=0, channel_multiplier=HT,
                                       allow_small_or_imprecise_dtypes=True))
                pool.sem_inc(s_k2, 1)
                pool.wait_ge(s_recst, 16)
                pool.wait_ge(s_pos, 1)
                stage(pool, 0, 0)
                stage(pool, 0, 1)
                with loop(nc, pool, 1, R1 - LATE) as g:
                    for h in range(2):
                        pool.wait_ge(s_sc[h], g * (16 * HT))
                        stage(pool, g, h)

            def rows_of(l, m):
                k, n = KR[l], MR[l]
                return [r for r in range(k) if r * n // k == m] if k >= n else ([m * k // n] if m * k % n == 0 else [])

            @block.scalar
            def _(act):
                act.wait_ge(s_vec, 16 * 9)

                def evac(l, m, c, w):
                    wait_apart(act, s_mm[l], c * MR[l] + m + 1, s_tick[0])
                    nc.scalar.activation(ZOUT[l][:, m, bass.ds(c * CW, w)], psZ[m % 4][:, 0:w], ACT.Identity,
                                         bias=vec[:, 0, 4 * VAT[l] + m:4 * VAT[l] + m + 1],
                                         scale=1.0 if l == 0 else 1.0 / (WS * HS)).then_inc(s_ev[l], 1)

                def row(l, k, c, w):
                    r = c * KR[l] + k
                    zin = ZIN[l][:, k, bass.ds(c * CW, w)]
                    wait_apart(act, s_u[l], r + 1, s_tick[0])
                    nc.scalar.activation(eb[:, k % 2, 0:w], zin, ACT.Exp, bias=cf[:, 1, k:k + 1],
                                         scale=cf[:, 0, k:k + 1]).then_inc(s_e[l], 1)
                    wait_apart(act, s_h[l], r + 1, s_tick[0])
                    nc.scalar.activation(yb[:, k % 2, 0:w], zin, ACT.Identity, bias=cf[:, 2, k:k + 1],
                                         scale=cf[:, 0, k:k + 1]).then_inc(s_y[l], 1)

                def layer(l):
                    def chunk(c, w, nw):
                        for m in range(MR[l]):
                            if nw and l:
                                for k in rows_of(l, m):
                                    row(l, k, c + 1, nw)
                            if l < 3:
                                evac(l, m, c, w)
                    if l == 1:
                        act.wait_ge(s_blkst, 16)
                    if l:
                        act.wait_ge(s_sq, l)
                        nc.scalar.activation(mv2[:, 0:KR[l], 1], mv2[:, 0:KR[l], 1], ACT.Sqrt).then_inc(s_sd, 1)
                        act.wait_ge(s_cf, l)
                        for k in range(KR[l]):
                            row(l, k, 0, CW)
                    with loop(nc, act, 0, CN - 1) as c:
                        chunk(c, CW, CW)
                    chunk(CN - 1, CW, PB)
                    chunk(CN, PB, 0)

                for l in range(4):
                    layer(l)

            @block.vector
            def _(dve):
                ch = Chain(dve, s_c2[1])
                dve.wait_ge(s_cnt, 1)
                ch.step(nc.vector.tensor_scalar(gr_i[:, 0, :], psR[:, 32:32 + NB], ET - 1.0, None, ALU.add))
                ch.step(nc.vector.tensor_scalar(gr_i[:, 1, :], gr_i[:, 0, :], 7, None, ALU.arith_shift_right))
                ch.step(nc.vector.tensor_copy(gr[:, 0, :], gr_i[:, 1, :]))
                ch.step(nc.vector.tensor_tensor_scan(gr[:, 1, :], gr[:, 0, :], gr[:, 0, :], 0.0, ALU.add, ALU.max))
                ch.step(nc.vector.tensor_tensor(gr[:, 3, :], gr[:, 1, :], gr[:, 0, :], ALU.subtract))
                ch.step(nc.vector.tensor_scalar(gr[:, 3, :], gr[:, 3, :], float(ET), -1.0, ALU.mult, ALU.add))
                ch.step(nc.vector.tensor_tensor(gr[:, 2, :], gr[:, 3, :], psR[:, 0:NB], ALU.add))
                ch.step(nc.vector.tensor_tensor(S[:, :, :], S[:, :, :],
                                                gr[:, 2, :].unsqueeze(2).to_broadcast([128, NB, T1]), ALU.add))
                ch.step(nc.vector.tensor_tensor(S[:, :, :], S[:, :, :], same[:, :, :], ALU.mult))
                ch.step(nc.vector.tensor_reduce(pos[:, :], S[:, :, :].rearrange("p k t -> p t k"), AX_X, ALU.add))
                ch.step(nc.vector.tensor_copy(pos_i[:, :], pos[:, :]))
                nc.vector.tensor_scalar(row_i[:, :], pos_i[:, :], ET - 1, None, ALU.bitwise_and)
                ch.step(nc.vector.tensor_scalar(pos_i[:, :], pos_i[:, :], 7, None, ALU.arith_shift_right))
                nc.vector.scalar_tensor_tensor(posd[:, :], row_i[:, :], float(T3), pos_i[:, :], ALU.mult, ALU.add).then_inc(s_pos, 1)
                dve.wait_ge(s_k2, 1)
                PT = T3 // HT
                ch.step(nc.vector.tensor_tensor(behind[:, :, :], iotaT[:, :].unsqueeze(2).to_broadcast([PT, HT, NB]),
                                                gr[0:PT, 1, :].unsqueeze(1).to_broadcast([PT, HT, NB]), ALU.is_ge))
                ch.step(nc.vector.tensor_reduce(iotaT[:, :], behind[:, :, :], AX_X, ALU.add))
                nc.vector.tensor_scalar(blk_i[:, :], iotaT[:, :], NB - 1.0, None, ALU.min).then_inc(s_blk, 1)

                def stats(l, m, c, ci, w):
                    wait_apart(dve, s_ev[l], c * MR[l] + m + 5, s_tick[1])
                    if isinstance(ci, int):
                        o_ = bst2[:, m, ci, :]
                    else:
                        o_ = bst2[:, m, bass.ds(ci, 1), :].rearrange("p a s -> p (a s)")
                    nc.vector.bn_stats(o_, ZOUT[l][:, m, bass.ds(c * CW, w)]).then_inc(s_st, 1)

                def row(l, k, c, w):
                    r = c * KR[l] + k
                    u = yb[:, k % 2, 0:w]
                    hi, lo = halves(l, k, c * CW, w)
                    dve.wait_ge(s_y[l], r + 1)
                    dve.wait_ge(s_e[l], r + 1)
                    nc.vector.scalar_tensor_tensor(u, eb[:, k % 2, 0:w], 1.0, u, ALU.min, ALU.max).then_inc(s_u[l], 1)
                    dve.wait_ge(s_u[l], r + 3)
                    nc.vector.tensor_scalar(hi, u, HS, None, ALU.mult).then_inc(s_hi[l], 1)
                    dve.wait_ge(s_hi[l], r + 1)
                    nc.vector.scalar_tensor_tensor(lo, u, HS, hi, ALU.mult, ALU.subtract).then_inc(s_h[l], 1)

                def out_blocks(m, c, w):
                    n = 2 if w == CW else (1 if m == 0 else 0)
                    if n:
                        dve.wait_ge(s_mm[3], c * 2 + m + 1)
                        xs = x2[:, bass.ds(c * 4 + 2 * m, n), :]
                        nc.vector.scalar_tensor_tensor(xs, psO[m][:, 0:n, :], 1.0 / (WS * HS), xs,
                                                       ALU.mult, ALU.add).then_inc(s_ev[3], 1)

                def layer(l):
                    def chunk(c, w, nw):
                        for m in range(MR[l]):
                            if nw and l:
                                for k in rows_of(l, m):
                                    row(l, k, c + 1, nw)
                            if l < 3:
                                stats(l, m, c, c, w)
                            else:
                                out_blocks(m, c, w)
                    if l:
                        n, v = KR[l], 4 * VAT[l - 1]
                        dve.wait_ge(s_st, 7 * sum(MR[:l]))
                        if l == 3:
                            nc.vector.memset(ones16[:, :], 1.0).then_inc(s_ones16, 1)
                        for k in range(n):
                            ch.mark(nc.vector.bn_aggr(mv2[:, k, :], bst2[:, k, :, :].rearrange("p c s -> p (c s)")))
                        dve.wait_ge(ch.sem, ch.n)
                        nc.vector.tensor_scalar(mv2[:, 0:n, 1], mv2[:, 0:n, 1], BN_EPS, None, ALU.add).then_inc(s_sq, 1)
                        dve.wait_ge(s_sd, l)
                        ch.step(nc.vector.reciprocal(cf[:, 0, 0:n], mv2[:, 0:n, 1]))
                        ch.step(nc.vector.tensor_tensor(cf[:, 0, 0:n], cf[:, 0, 0:n], vec[:, 1, v:v + n], ALU.mult))
                        ch.step(nc.vector.tensor_tensor(cf[:, 1, 0:n], cf[:, 0, 0:n], mv2[:, 0:n, 0], ALU.mult))
                        ch.step(nc.vector.tensor_tensor(cf[:, 1, 0:n], vec[:, 2, v:v + n], cf[:, 1, 0:n], ALU.subtract))
                        nc.vector.tensor_scalar(cf[:, 2, 0:n], cf[:, 1, 0:n], 1.0, None, ALU.add).then_inc(s_cf, 1)
                        dve.wait_ge(s_cf, l)
                        for k in range(n):
                            row(l, k, 0, CW)
                    if l == 3:
                        dve.wait_ge(s_b4, 16)
                        dve.wait_ge(s_b4c, 1)
                        ch.step(nc.vector.scalar_tensor_tensor(b4[:, :], psR[0:PB, 0:D], -1.0 / WS, b4[:, :], ALU.mult, ALU.add))
                        dve.wait_ge(s_xr, 16)
                        ch.step(nc.vector.tensor_tensor(x2[:, :, :], x2[:, :, :], b4[:, :].unsqueeze(1).to_broadcast([PB, NB, D]), ALU.add))
                    with loop(nc, dve, 0, CN - 1) as c:
                        chunk(c, CW, CW)
                    chunk(CN - 1, CW, PB)
                    chunk(CN, PB, 0)

                for l in range(4):
                    layer(l)

            @block.tensor
            def _(pe):
                pe.wait_ge(s_k2, 1)
                nc.tensor.matmul(psR[:, 0:NB], later[:, :], S[:, :, T1 - 1], start=True, stop=True)
                nc.tensor.matmul(psR[:, 32:32 + NB], ones[:, :], S[:, :, T1 - 1], start=True, stop=True).then_inc(s_cnt, 1)
                pe.wait_ge(s_w1, 16)
                pe.wait_ge(s_wlo, len(pieces))
                W = [None, W2, W3]
                for l in range(1, 3):
                    pe.sem_inc(s_u[l], 2)
                    pe.sem_inc(s_h[l], 2)
                pe.sem_inc(s_u[3], 2)
                pe.sem_inc(s_h[3], 2)

                def chunk(l, c, w):
                    if l:
                        pe.wait_ge(s_h[l], c * KR[l] + KR[l] + 2)
                    for m in range(MR[l]):
                        pe.wait_ge(s_ev[l], c * MR[l] + m + 1)
                        ms = slice(128 * m, 128 * (m + 1))
                        if l == 0:
                            for k in range(2):
                                last = nc.tensor.matmul(psZ[m % 4][:, 0:w], W1[:, k, ms], accT[:, k, bass.ds(c * CW, w)],
                                                        start=(k == 0), stop=(k == 1))
                        else:
                            terms = [(sw, sh, k) for k in range(KR[l]) for sw, sh in ((0, 0), (0, 1), (1, 0))]
                            for n, (sw, sh, k) in enumerate(terms):
                                last = nc.tensor.matmul(psZ[m % 4][:, 0:w], W[l][:, sw, k, ms], halves(l, k, c * CW, w)[sh],
                                                        start=(n == 0), stop=(n == len(terms) - 1))
                        last.then_inc(s_mm[l], 1)

                def last_layer(c, w):
                    pe.wait_ge(s_h[3], c * KR[3] + KR[3] + 2)
                    for m in range(2):
                        n = 2 if w == CW else (1 if m == 0 else 0)
                        if not n:
                            continue
                        wait_apart(pe, s_ev[3], c * 2 + m + 1, s_tick[2])
                        terms = [(sw, sh, k) for k in range(4) for sh, sw in ((0, 0), (0, 1), (1, 0))]
                        for j in range(n):
                            for i, (sw, sh, k) in enumerate(terms):
                                f = ZIN[3][:, k, :].bitcast(F16)
                                hx = f[:, bass.ds(c * (2 * CW) + sh * w + (2 * m + j) * PB, PB)]
                                last = nc.tensor.matmul(psO[m][:, j, :], hx, W4[:, sw, k, :], start=(i == 0),
                                                        stop=(i == len(terms) - 1))
                        last.then_inc(s_mm[3], 1)

                for l in range(4):
                    if l < 3:
                        pe.sem_inc(s_ev[l], 4)
                        with loop(nc, pe, 0, CN) as c:
                            chunk(l, c, CW)
                        chunk(l, CN, PB)
                    else:
                        pe.wait_ge(s_ones16, 1)
                        for i in range(8):
                            last = nc.tensor.matmul(psR[0:PB, 0:D], ones16[:, 0:PB], W4[:, i // 4, i % 4, :],
                                                    start=(i == 0), stop=(i == 7))
                        last.then_inc(s_b4c, 1)
                        pe.sem_inc(s_ev[3], 2)
                        with loop(nc, pe, 0, CN) as c:
                            last_layer(c, CW)
                        last_layer(CN, PB)

        xn2 = at("xn2", 31 * KB, [PB, NB, D])
        later3 = at("later3", 56 * KB, [128, PB])
        ones3 = at("ones3", 56 * KB + 512, [128, PB])
        M = at("M", 57 * KB, [PB, NB * K2, X])
        T = at("T", 57 * KB + 1600, [PB, NB * K2, X])
        top = at("top", 57 * KB + 3200, [PB, NB, X])
        topi = at("topi", 57 * KB + 4000, [PB, NB, X], U32)
        o = 204 * KB
        xTf = at("xTf", o, [128, 2, 2, PB]); o += 2016
        lg = at("lg", o, [PB, NB, X]); o += 800
        rw = at("rw", o, [128, 2, X]); o += 64
        o = 207 * KB
        choice = at("choice", o, [PB, 2, NB * K2]); o += 416
        slot_i = choice[:, 0, :].bitcast(I32)
        gate = choice[:, 1, :].rearrange("p (b k) -> p b k", k=K2)
        ex_i = at("ex_i", o, [1, T2], I32); o += 224
        bst3 = at("bst3", o, [PB, 5, 6]); o += 128
        mv3 = at("mv3", o, [PB, 5, 2]); o += 64
        sd3 = at("sd3", o, [PB, 2, 5]); o += 40
        assert BASE + o <= 229368
        o = 31 * KB
        xs = at("xs", o, [128, 2, D]); o += 2048
        xh = at("xh", o, [128, 2, 2, D], F16); o += 2048
        sl = at("sl", o, [128, 2, HP // 2]); o += 3072
        hv = at("hv", o, [128, 2, 2, HP // 2]); o += 6144
        hh = at("hh", o, [128, 2, 2, HP], F16); o += 6144
        yv = at("yv", o, [128, 2, D]); o += 2048
        y_d = dram("y_d", (T2 * 128, D))
        s_c3 = [sem(f"s_c3{i}") for i in range(4)]
        s_rw = sem("s_rw")
        s_k3 = sem("s_k3")
        s_ehi = sem("s_ehi")
        s_elo = sem("s_elo")
        s_v3 = sem("s_v3")
        s_d3 = sem("s_d3")
        s_n3 = sem("s_n3")
        s_t3 = sem("s_t3")
        s_xt3 = sem("s_xt3")
        s_lg = sem("s_lg")
        s_gx = sem("s_gx")
        s_gxe = sem("s_gxe")
        s_M = sem("s_M")
        s_tot = sem("s_tot")
        s_slot = sem("s_slot")
        s_scx = sem("s_scx")
        s_xs = [sem("s_xs0"), sem("s_xs1")]
        s_xsT = sem("s_xsT")
        s_xh = sem("s_xh")
        s_xl = sem("s_xl")
        s_up = sem("s_up")
        s_sl = sem("s_sl")
        s_hv = sem("s_hv")
        s_ht = sem("s_ht")
        s_hh = sem("s_hh")
        s_hl = sem("s_hl")
        s_dn = sem("s_dn")
        s_yv = sem("s_yv")
        s_yst = [sem("s_yst0"), sem("s_yst1")]

        with ExitStack() as p3:
            psTx = p3.enter_context(nc.psum_tensor("psTx", [128, 2, 128], F32))
            psHT = [p3.enter_context(nc.psum_tensor(f"psHT{i}", [128, HP // 2], F32)) for i in range(2)]
            psT3 = [psTx, psHT[0][:, 0:256].rearrange("p (k t) -> p k t", k=2)]
            psL = psHT[1][0:PB, 0:NB * X].rearrange("p (b e) -> p b e", e=X)
            psH = [p3.enter_context(nc.psum_tensor(f"psH{i}", [128, HP // 2], F32)) for i in range(4)]
            psY = p3.enter_context(nc.psum_tensor("psY", [128, D], F32))
            block = p3.enter_context(nc.Block())
            HX = NB * K2 * X // 2

            HQ = HP // 2

            def dst_half(n, s):
                return we[:, n * PW + s * HP:n * PW + (s + 1) * HP]

            @block.sync
            def _(sp):
                sp.dma_start(rw[:, :, :], a["L0_ffn_router_w"].rearrange("(k p) e -> p k e", p=128)).then_inc(s_rw, 16)
                for e in range(X):
                    if e not in EARLY:
                        load_expert(sp, e)
                sp.wait_ge(s_scx, 16 * NB * K2)

                def load(t, i):
                    sp.dma_start(xs[:, i, :], xs_d[bass.ds(t * 128, 128), :]).then_inc(s_xs[i], 16)

                load(0, 0)
                load(1, 1)
                with loop(nc, sp, 0, T2 // 2 - 1) as g:
                    for i in range(2):
                        wait_apart(sp, s_xsT, g * 2 + i + 1, s_tick[3])
                        load(g * 2 + i + 2, i)

            @block.gpsimd
            def _(pool):
                ch = Chain(pool, s_c3[0])
                nc.gpsimd.memset(ones3[:, :], 1.0)
                ch.step(nc.gpsimd.memset(later3[:, :], 1.0))
                ch.step(nc.gpsimd.affine_select(out=later3[:, :], in_=later3[:, :], compare_op=ALU.is_gt, fill=0.0,
                                                base=0, pattern=[[1, PB]], channel_multiplier=-1))
                pool.sem_inc(s_k3, 1)
                pool.wait_ge(s_slot, 1)
                for b in range(NB):
                    for k in range(K2):
                        j = b * K2 + k
                        pool.indirect_dma_start(
                            out=xs_d, out_offset=bass.IndirectOffsetOnAxis(ap=slot_i[:, j:j + 1], axis=0),
                            in_=xn2[:, b, :], in_offset=None).then_inc(s_scx, 16)

                def store(t, i):
                    wait_apart(pool, s_yv, 1 + t + 1, s_halves)
                    pool.dma_start(y_d[bass.ds(t * 128, 128), :], yv[:, i, :]).then_inc(s_yst[i], 16)

                with loop(nc, pool, 0, LATE) as g:
                    for i in range(2):
                        store(g * 2 + i, i)
                        pool.wait_ge(s_sc[i], (g + (R1 - LATE)) * (16 * HT))
                        stage(pool, g + (R1 - LATE), i)
                with loop(nc, pool, LATE, T2 // 2) as g:
                    for i in range(2):
                        store(g * 2 + i, i)
                for h in range(2):
                    pool.wait_ge(s_sc[h], 16 * HT * R1)
                for i in range(2):
                    pool.wait_ge(s_yst[i], 16 * (T2 // 2))

            @block.scalar
            def _(act):
                for c in range(6):
                    if c < 5:
                        act.wait_ge(s_v3, c + 1)
                        nc.scalar.activation(sd3[:, 0, :], mv3[:, :, 1], ACT.Sqrt).then_inc(s_d3, 1)
                    for b in range(max(5 * c - 5, 0), 5 * c):
                        act.wait_ge(s_t3, b + 1)
                        if b >= 2:
                            act.wait_ge(s_lg, b - 1)
                        nc.scalar.activation(xTf[:, b % 2, :, :], psT3[b % 2][:, :, 0:PB], ACT.Copy).then_inc(s_xt3, 1)
                act.wait_ge(s_gx, 1)
                nc.scalar.activation(top[:, :, :], top[:, :, :], ACT.Exp).then_inc(s_gxe, 1)
                act.wait_ge(s_ex, 1)
                for n in range(X * PIECES):
                    act.wait_ge(s_raw[n // PIECES], 64 if n < (X - 1) * PIECES else 48)
                    if n == X * PIECES - 1:
                        act.wait_ge(s_last, 16)
                    if n >= 2:
                        act.wait_ge(s_elo, n - 1)
                    nc.scalar.activation(dst_half(n, 0), raw[:, n, :], ACT.Copy, scale=WS).then_inc(s_ehi, 1)

                def halves_x(t, i):
                    act.wait_ge(s_xsT, t + 1)
                    act.wait_ge(s_up, 2 * t + 2)
                    nc.scalar.activation(xh[:, i, 0, :], psTx[:, :, :], ACT.Copy, scale=XS).then_inc(s_xh, 1)

                def silu(t, q, first=False):
                    act.wait_ge(s_up, 4 + 2 * t + q + 1)
                    if not first:
                        act.wait_ge(s_hv, 2 * t + q - 1)
                    nc.scalar.activation(sl[:, q, :], psH[q][:, :], ACT.Silu, scale=1.0 / (XS * WS)).then_inc(s_sl, 1)

                def halves_h(t, i):
                    for q in range(2):
                        act.wait_ge(s_ht, 4 + 2 * t + q + 1)
                        act.wait_ge(s_dn, t + 1)
                        nc.scalar.activation(hh[:, i, 0, q * HQ:(q + 1) * HQ], psHT[q][:, :], ACT.Copy).then_inc(s_hh, 1)

                def result(t, i, stored):
                    act.wait_ge(s_dn, 2 + t + 1)
                    if stored is not None:
                        act.wait_ge(s_yst[i], stored * 16)
                    nc.scalar.activation(yv[:, i, :], psY[:, :], ACT.Copy, scale=1.0 / (WS * HS)).then_inc(s_yv, 1)

                def step(t, i, stored):
                    halves_x(t + 1, 1 - i)
                    silu(t, 0)
                    halves_h(t - 1, 1 - i)
                    silu(t, 1)
                    result(t - 1, 1 - i, stored)

                act.sem_inc(s_yv, 1)
                halves_x(0, 0)
                halves_x(1, 1)
                silu(0, 0, True)
                silu(0, 1, True)
                for t in (1, 2):
                    step(t, t % 2, None)
                with loop(nc, act, 1, T2 // 2 - 1) as g:
                    for i in (1, 0):
                        step(g * 2 + 2 - i, i, g)
                silu(T2 - 1, 0)
                halves_h(T2 - 2, 0)
                silu(T2 - 1, 1)
                result(T2 - 2, 0, T2 // 2 - 1)
                halves_h(T2 - 1, 1)
                result(T2 - 1, 1, T2 // 2 - 1)

            @block.vector
            def _(dve):
                ch = Chain(dve, s_c3[1])
                for c in range(5):
                    for b in range(5):
                        ch.mark(nc.vector.bn_stats(bst3[:, b, :], x2[:, 5 * c + b, :]))
                    dve.wait_ge(ch.sem, ch.n)
                    for b in range(5):
                        ch.mark(nc.vector.bn_aggr(mv3[:, b, :], bst3[:, b, :]))
                    dve.wait_ge(ch.sem, ch.n)
                    nc.vector.tensor_scalar(mv3[:, :, 1], mv3[:, :, 1], LN_EPS, None, ALU.add).then_inc(s_v3, 1)
                    dve.wait_ge(s_d3, c + 1)
                    ch.step(nc.vector.reciprocal(sd3[:, 1, :], sd3[:, 0, :]))
                    for b in range(5):
                        nc.vector.tensor_scalar(xn2[:, 5 * c + b, :], x2[:, 5 * c + b, :], mv3[:, b, 0:1], sd3[:, 1, b:b + 1],
                                                ALU.subtract, ALU.mult).then_inc(s_n3, 1)
                    dve.wait_ge(s_n3, 5 * c + 5)
                dve.wait_ge(s_lg, NB)
                ch.step(nc.vector.tensor_copy(lg[:, :, :], psL[:, :, :]))
                for b in range(NB):
                    ch.mark(nc.vector.max(top[:, b, :], lg[:, b, :]))
                dve.wait_ge(ch.sem, ch.n)
                for b in range(NB):
                    ch.mark(nc.vector.max_index(topi[:, b, :], top[:, b, :], lg[:, b, :]))
                dve.wait_ge(ch.sem, ch.n)
                ch.step(nc.vector.tensor_tensor(T[:, 0:NB, :], top[:, :, :], top[:, :, 0:1].to_broadcast([PB, NB, X]), ALU.subtract))
                nc.vector.tensor_copy(top[:, :, :], T[:, 0:NB, :]).then_inc(s_gx, 1)
                gf = gate[:, :, :].rearrange("p b k -> p (b k)")
                ch.step(nc.vector.tensor_copy(gate[:, :, :], topi[:, :, 0:K2]))
                nc.vector.tensor_tensor(M[:, :, :], gf.unsqueeze(2).to_broadcast([PB, NB * K2, X]),
                                        iota[0:PB, 0:X].unsqueeze(1).to_broadcast([PB, NB * K2, X]), ALU.is_equal).then_inc(s_M, 1)
                dve.wait_ge(s_gxe, 1)
                dve.wait_ge(s_M, 1)
                ch.step(nc.vector.tensor_reduce(lg[:, :, 0:1], top[:, :, :], AX_X, ALU.add))
                ch.step(nc.vector.reciprocal(lg[:, :, 1], lg[:, :, 0]))
                ch.step(nc.vector.tensor_tensor(lg[:, :, 2:4], top[:, :, 0:2], lg[:, :, 1:2].to_broadcast([PB, NB, 2]), ALU.mult))
                ch.step(nc.vector.tensor_tensor(lg[:, :, 4], lg[:, :, 2], lg[:, :, 3], ALU.add))
                ch.step(nc.vector.tensor_scalar(lg[:, :, 4], lg[:, :, 4], 1e-9, None, ALU.add))
                ch.step(nc.vector.reciprocal(lg[:, :, 5], lg[:, :, 4]))
                ch.step(nc.vector.tensor_tensor(gate[:, :, :], lg[:, :, 2:4], lg[:, :, 5:6].to_broadcast([PB, NB, 2]), ALU.mult))
                dve.wait_ge(s_tot, 1)
                Tn = [T[:, NB * n:NB * (n + 1), :].rearrange("p j e -> p (j e)") for n in range(2)]
                for n in range(2):
                    ch.step(nc.vector.tensor_copy(Tn[n], psH[2 * n + 1][0:PB, 0:HX]))
                for e in range(X):
                    ch.mark(nc.vector.tensor_tensor_scan(T[:, :, e], T[:, :, e], T[:, :, e], 0.0, ALU.add, ALU.max))
                dve.wait_ge(ch.sem, ch.n)
                q = lg[:, :, :].rearrange("p b e -> p (b e)")
                qi = lg[:, :, :].rearrange("p b e -> p (b e)").bitcast(I32)
                ch.step(nc.vector.tensor_scalar(qi[:, 0:X], T[:, NB * K2 - 1, :], 127.0, None, ALU.add))
                ch.step(nc.vector.tensor_scalar(qi[:, 8:16], qi[:, 0:8], 7, None, ALU.arith_shift_right))
                ch.step(nc.vector.tensor_copy(q[:, 16:24], qi[:, 8:16]))
                ch.step(nc.vector.tensor_tensor_scan(q[:, 24:32], q[:, 16:24], q[:, 16:24], 0.0, ALU.add, ALU.max))
                ch.step(nc.vector.tensor_tensor(q[:, 32:40], q[:, 24:32], q[:, 16:24], ALU.subtract))
                ch.step(nc.vector.tensor_scalar(q[:, 32:40], q[:, 32:40], 128.0, None, ALU.mult))
                for n in range(2):
                    ch.step(nc.vector.tensor_tensor(Tn[n], Tn[n], psH[2 * n + 1][0:PB, 0:HX], ALU.subtract))
                    ch.step(nc.vector.tensor_tensor(Tn[n], Tn[n], psH[2 * n][0:PB, 0:HX], ALU.add))
                ch.step(nc.vector.tensor_tensor(T[:, :, :], T[:, :, :], q[:, 32:40].unsqueeze(1).to_broadcast([PB, NB * K2, X]), ALU.add))
                ch.step(nc.vector.tensor_tensor(T[:, :, :], T[:, :, :], M[:, :, :], ALU.mult))
                ch.step(nc.vector.tensor_reduce(q[:, 64:64 + NB * K2], T[:, :, :], AX_X, ALU.add))
                nc.vector.tensor_copy(slot_i[:, :], q[:, 64:64 + NB * K2]).then_inc(s_slot, 1)
                cmp_ = at("cmp_", 57 * KB + 4800, [1, T2, X], F16)
                tids = iota[0:1, 0:T2].unsqueeze(2).to_broadcast([1, T2, X])
                ch.step(nc.vector.tensor_tensor(cmp_[:, :, :], tids, q[0:1, 24:32].unsqueeze(1).to_broadcast([1, T2, X]), ALU.is_ge))
                ch.step(nc.vector.tensor_reduce(q[0:1, 128:128 + T2], cmp_[:, :, :], AX_X, ALU.add))
                nc.vector.tensor_scalar(ex_i[:, :], q[0:1, 128:128 + T2], X - 1.0, None, ALU.min).then_inc(s_ex, 1)
                for n in range(X * PIECES):
                    dve.wait_ge(s_ehi, n + 1)
                    nc.vector.scalar_tensor_tensor(dst_half(n, 1), raw[:, n, :], WS, dst_half(n, 0),
                                                   ALU.mult, ALU.subtract).then_inc(s_elo, 1)

                def halves_x(t, i):
                    dve.wait_ge(s_xh, t + 1)
                    nc.vector.scalar_tensor_tensor(xh[:, i, 1, :], psTx[:, :, :].rearrange("p k t -> p (k t)"), XS,
                                                   xh[:, i, 0, :], ALU.mult, ALU.subtract).then_inc(s_xl, 1)

                def hidden(t, i, q):
                    dve.wait_ge(s_sl, 2 * t + q + 1)
                    dve.wait_ge(s_ht, 2 * t + q + 1)
                    nc.vector.scalar_tensor_tensor(hv[:, i, q, :], psH[2 + q][:, :], HS / (XS * WS), sl[:, q, :],
                                                   ALU.mult, ALU.mult).then_inc(s_hv, 1)

                def halves_h(t, i):
                    for q in range(2):
                        hs = slice(q * HQ, (q + 1) * HQ)
                        dve.wait_ge(s_hh, 2 * t + q + 1)
                        nc.vector.tensor_tensor(hh[:, i, 1, hs], psHT[q][:, :], hh[:, i, 0, hs], ALU.subtract).then_inc(s_hl, 1)

                dve.sem_inc(s_hl, 2)

                def step(t, i):
                    halves_x(t + 1, 1 - i)
                    hidden(t, i, 0)
                    halves_h(t - 1, 1 - i)
                    hidden(t, i, 1)

                halves_x(0, 0)
                halves_x(1, 1)
                hidden(0, 0, 0)
                hidden(0, 0, 1)
                with loop(nc, dve, 0, T2 // 2 - 1) as g:
                    for i in (1, 0):
                        step(g * 2 + 2 - i, i)
                hidden(T2 - 1, 1, 0)
                halves_h(T2 - 2, 0)
                hidden(T2 - 1, 1, 1)
                halves_h(T2 - 1, 1)

            @block.tensor
            def _(pe):
                pe.wait_ge(s_rw, 16)
                for b in range(NB + 1):
                    if b < NB:
                        pe.wait_ge(s_n3, b + 1)
                        if b >= 2:
                            pe.wait_ge(s_xt3, b - 1)
                        for k in range(2):
                            last = nc.tensor.transpose(psT3[b % 2][:, k, 0:PB], xn2[:, b, 128 * k:128 * (k + 1)],
                                                       ident[0:PB, 0:PB])
                        last.then_inc(s_t3, 1)
                    if b:
                        pe.wait_ge(s_xt3, b)
                        for k in range(2):
                            last = nc.tensor.matmul(psL[:, b - 1, :], xTf[:, (b - 1) % 2, k, :], rw[:, k, :],
                                                    start=(k == 0), stop=(k == 1))
                        last.then_inc(s_lg, 1)
                pe.wait_ge(s_k3, 1)
                pe.wait_ge(s_M, 1)
                for n in range(2):
                    mn = M[:, NB * n:NB * (n + 1), :].rearrange("p j e -> p (j e)")
                    nc.tensor.matmul(psH[2 * n][0:PB, 0:HX], later3[0:PB, :], mn, start=True, stop=True)
                    last = nc.tensor.matmul(psH[2 * n + 1][0:PB, 0:HX], ones3[0:PB, :], mn, start=True, stop=True)
                last.then_inc(s_tot, 1)
                pe.sem_inc(s_up, 4)
                pe.sem_inc(s_ht, 4)
                pe.sem_inc(s_dn, 2)
                pe.wait_ge(s_elo, X * PIECES)
                pe.wait_ge(s_ex, 1)

                def experts(t, n):
                    return registers(nc, pe, ex_i[0:1, bass.ds(t, n)], X - 1)

                def weights(e, piece, s, c, w):
                    return we[:, bass.ds(e * (PIECES * PW) + piece * PW + s * HP + c, w)]

                def turn(t, i, loads):
                    pe.wait_ge(s_xs[i], 16 * loads)
                    if not isinstance(t, int) or t:
                        pe.wait_ge(s_xl, t)
                    for k in range(2):
                        last = nc.tensor.transpose(psTx[:, k, :], xs[:, i, 128 * k:128 * (k + 1)], ident[:, :])
                    last.then_inc(s_xsT, 1)

                def up(t, i, e, q):
                    pe.wait_ge(s_xl, t + 1)
                    if not isinstance(t, int) or t:
                        wait_apart(pe, s_hv, 2 * t + q - 1, s_tick[2])
                    for w3 in range(2):
                        terms = [(sx, sw, k) for k in range(2) for sx, sw in ((0, 0), (0, 1), (1, 0))]
                        for n, (sx, sw, k) in enumerate(terms):
                            last = nc.tensor.matmul(psH[2 * w3 + q][:, :], xh[:, i, sx, 128 * k:128 * (k + 1)],
                                                    weights(e, 2 * w3 + k, sw, q * HQ, HQ),
                                                    start=(n == 0), stop=(n == len(terms) - 1))
                    last.then_inc(s_up, 1)

                def turn_hidden(t, i):
                    pe.wait_ge(s_hv, 2 * t + 2)
                    pe.wait_ge(s_hl, 2 + 2 * t)
                    for q in range(2):
                        for m in range(3):
                            ms = slice(128 * m, 128 * (m + 1))
                            last = nc.tensor.transpose(psHT[q][:, ms], hv[:, i, q, ms], ident[:, :])
                        last.then_inc(s_ht, 1)

                def down(t, i, e):
                    wait_apart(pe, s_yv, 1 + t, s_tick[2])
                    for n in range(2):
                        wait_apart(pe, s_hl, 2 + 2 * t + n + 1, s_tick[2])
                        for m in range(3 * n, 3 * n + 3):
                            for j, (sh, sw) in enumerate(((0, 0), (0, 1), (1, 0))):
                                last = nc.tensor.matmul(psY[:, :], hh[:, i, sh, 128 * m:128 * (m + 1)],
                                                        weights(e, 4 + n, sw, (m - 3 * n) * D, D),
                                                        start=(m == 0 and j == 0), stop=(m == HM - 1 and j == 2))
                    last.then_inc(s_dn, 1)

                turn(0, 0, 1)
                turn(1, 1, 1)
                e = experts(0, 1)
                up(0, 0, e[0], 0)
                up(0, 0, e[0], 1)
                with loop(nc, pe, 0, T2 // 2 - 1) as g:
                    e = experts(g * 2, 3)
                    for i in (1, 0):
                        t = g * 2 + 2 - i
                        turn(t + 1, 1 - i, g + 2)
                        up(t, i, e[2 - i], 0)
                        turn_hidden(t - 1, 1 - i)
                        up(t, i, e[2 - i], 1)
                        down(t - 1, 1 - i, e[1 - i])
                e = experts(T2 - 2, 2)
                up(T2 - 1, 1, e[1], 0)
                turn_hidden(T2 - 2, 0)
                up(T2 - 1, 1, e[1], 1)
                down(T2 - 2, 0, e[0])
                turn_hidden(T2 - 1, 1)
                down(T2 - 1, 1, e[1])

        free_semaphores()

        xn3 = at("xn3", 31 * KB, [PB, NB, D])
        yg = at("yg", 60 * KB, [PB, 8, D])
        row = at("row", 70 * KB, [PB, NB, RW])
        wx = at("wx", 77 * KB, [128, 2, NH + OD + NH])
        wt = at("wt", 78 * KB, [OD, D])
        wlr = at("wlr", 79 * KB, [OD, 2, NH])
        el = at("el", 79 * KB + 64, [PB, NB * NH])
        f1 = at("f1", 131 * KB, [128, 2, 2, FH], F16)
        f2 = at("f2", 139 * KB, [128, 2, FH // 128, D], F16)
        fraw = at("fraw", 147 * KB, [128, 2, 2 * FH])
        tab_d = dram("tab_d", (N, RW))
        s_yg = [sem(f"s_yg{i}") for i in range(8)]
        s_res = sem("s_res")
        s_wt = sem("s_wt")
        s_wlr = sem("s_wlr")
        s_wx = sem("s_wx")
        s_one = sem("s_one")
        s_fraw = sem("s_fraw")
        s_fhi = sem("s_fhi")
        s_flo = sem("s_flo")
        s_v4 = sem("s_v4")
        s_d4 = sem("s_d4")
        s_n4 = sem("s_n4")
        s_t4 = sem("s_t4")
        s_xt4 = sem("s_xt4")
        s_row = sem("s_row")
        s_rowc = sem("s_rowc")
        s_tab = sem("s_tab")
        s_c4 = sem("s_c4")

        VW = OD + 1
        acc = at("acc", 80 * KB, [PB, NB, NH * VW])
        recs = at("recs", 106 * KB, [128, T3, 2], I32)
        place = at("place", 110 * KB, [128, T3])
        g3 = at("g3", 112 * KB, [128, 4, HT, RW])
        oh3 = at("oh3", 118 * KB, [128, 4, HT, PB])
        ohT = at("ohT", 147 * KB, [PB, 2, HT * 128])
        vv = at("vv", 151 * KB, [128, 2, HT, NH * VW])
        zz = at("zz", 160 * KB, [128, 2, HT, NH])
        pp = at("pp", 160 * KB + 128, [128, 2, HT, NH])
        blk3 = at("blk3", 164 * KB, [1, T3 + HT], I32)
        st3 = at("st3", 163 * KB, [128, 4, HT], I32)
        s_rl = sem("s_rl")
        s_bl = sem("s_bl")
        s_pl = sem("s_pl")
        s_st3 = [sem(f"s_st3{i}") for i in range(4)]
        s_g3 = [sem(f"s_g3{i}") for i in range(4 * HT)]
        s_oh3 = sem("s_oh3")
        s_ot = sem("s_ot")
        s_otc = sem("s_otc")
        s_el = sem("s_el")
        s_z = sem("s_z")
        s_lk = sem("s_lk")
        s_p = sem("s_p")
        s_V = sem("s_V")
        s_sct = sem("s_sct")
        s_ac = sem("s_ac")
        s_a0 = sem("s_a0")
        s_bw = sem("s_bw")
        s_halves = sem("s_halves5")
        s_tick = [None, None, sem("s_tick_pe5")]

        def normalise(dve, ch, src, dst, c, s_var, s_dev, s_out):
            for b in range(5):
                ch.mark(nc.vector.bn_stats(bst3[:, b, :], src[:, 5 * c + b, :]))
            dve.wait_ge(ch.sem, ch.n)
            for b in range(5):
                ch.mark(nc.vector.bn_aggr(mv3[:, b, :], bst3[:, b, :]))
            dve.wait_ge(ch.sem, ch.n)
            nc.vector.tensor_scalar(mv3[:, :, 1], mv3[:, :, 1], LN_EPS, None, ALU.add).then_inc(s_var, 1)
            dve.wait_ge(s_dev, c + 1)
            ch.step(nc.vector.reciprocal(sd3[:, 1, :], sd3[:, 0, :]))
            for b in range(5):
                nc.vector.tensor_scalar(dst[:, 5 * c + b, :], src[:, 5 * c + b, :], mv3[:, b, 0:1], sd3[:, 1, b:b + 1],
                                        ALU.subtract, ALU.mult).then_inc(s_out, 1)
            dve.wait_ge(s_out, 5 * c + 5)

        with ExitStack() as p4:
            psT4 = [p4.enter_context(nc.psum_tensor(f"psT4{i}", [128, 2, 128], F32)) for i in range(2)]
            psX = [p4.enter_context(nc.psum_tensor(f"psX{i}", [128, NH + OD + NH], F32)) for i in range(2)]
            psW = p4.enter_context(nc.psum_tensor("psW", [128, 2, 2 * NH], F32))
            block = p4.enter_context(nc.Block())

            @block.sync
            def _(sp):
                sp.dma_start(wt[:, :], a["L1_gnn_WT"]).then_inc(s_wt, 16)
                for j, name in enumerate(("r", "l")):
                    sp.dma_start(wlr[:, j, :], a["L1_gnn_W" + name]).then_inc(s_wlr, 16)
                sp.dma_start(wx[:, :, NH:NH + OD], a["L1_gnn_W"].rearrange("(k p) n -> p k n", p=128)).then_inc(s_wlr, 16)
                sp.dma_start(fraw[:, 0, :].rearrange("p (k n) -> p k n", k=2),
                             a["L1_ffn_w1"].rearrange("(k p) n -> p k n", p=128)).then_inc(s_fraw, 16)
                sp.dma_start(fraw[:, 1, :].rearrange("p (k n) -> p k n", n=D),
                             a["L1_ffn_w2"].rearrange("(k p) n -> p k n", p=128)).then_inc(s_fraw, 16)
                sp.wait_ge(s_one, 1)
                sp.dma_start(recs[:, :, :].rearrange("p t r -> p (t r)"), rec_d).then_inc(s_rl, 16)
                sp.wait_ge(s_bw, 1)
                sp.dma_start(blk3[:, HT:], blk_d).then_inc(s_bl, 16)
                for c in range(5):
                    sp.wait_ge(s_rowc, 5 * c + 5)
                    sp.dma_start(tab_d.rearrange("(b p) d -> p b d", p=PB)[:, 5 * c:5 * c + 5, :],
                                 row[:, 5 * c:5 * c + 5, :]).then_inc(s_tab, 16)
                sp.wait_ge(s_tab, 80)

            @block.gpsimd
            def _(pool):
                nc.gpsimd.memset(row[:, :, NH + OD:RW], 1.0).then_inc(s_one, 1)
                for j in range(NB * K2):
                    if j >= 8:
                        pool.wait_ge(s_res, j - 7)
                    pool.indirect_dma_start(
                        out=yg[:, j % 8, :], out_offset=None, in_=y_d,
                        in_offset=bass.IndirectOffsetOnAxis(ap=slot_i[:, j:j + 1], axis=0)).then_inc(s_yg[j % 8], 16)

            @block.scalar
            def _(act):
                act.wait_ge(s_fraw, 32)
                for n, f in enumerate((f1, f2)):
                    nc.scalar.activation(f[:, 0, :, :].rearrange("p k n -> p (k n)"), fraw[:, n, :], ACT.Copy,
                                         scale=WS).then_inc(s_fhi, 1)
                act.wait_ge(s_wx, 1)
                for j in range(2):
                    nc.scalar.activation(wx[:, :, j * (NH + OD):j * (NH + OD) + NH], psW[:, :, j * NH:(j + 1) * NH],
                                         ACT.Copy).then_inc(s_wx, 1)
                def rows(b):
                    act.wait_ge(s_row, b + 1)
                    nc.scalar.activation(row[:, b, 0:NH + OD], psX[b % 2][0:PB, 0:NH + OD], ACT.Copy)
                    nc.scalar.activation(el[:, b * NH:(b + 1) * NH], psX[b % 2][0:PB, NH + OD:NH + OD + NH],
                                         ACT.Copy).then_inc(s_rowc, 1)

                for c in range(6):
                    if c < 5:
                        act.wait_ge(s_v4, c + 1)
                        nc.scalar.activation(sd3[:, 0, :], mv3[:, :, 1], ACT.Sqrt).then_inc(s_d4, 1)
                    for b in range(max(5 * c - 5, 0), 5 * c):
                        act.wait_ge(s_t4, b + 1)
                        if b >= 2:
                            act.wait_ge(s_row, b - 1)
                        nc.scalar.activation(xTf[:, b % 2, :, :], psT4[b % 2][:, :, 0:PB], ACT.Copy).then_inc(s_xt4, 1)
                        if b:
                            rows(b - 1)
                rows(NB - 1)

            @block.vector
            def _(dve):
                ch = Chain(dve, s_c4)
                nc.vector.memset(blk3[:, 0:HT], 0.0).then_inc(s_bw, 1)
                for c in range(5):
                    for j in range(5 * c * K2, 5 * (c + 1) * K2):
                        b, k = j // K2, j % K2
                        dve.wait_ge(s_yg[j % 8], 16 * (j // 8 + 1))
                        dve.wait_ge(s_res, j)
                        nc.vector.scalar_tensor_tensor(x2[:, b, :], yg[:, j % 8, :], gate[:, b, k:k + 1], x2[:, b, :],
                                                       ALU.mult, ALU.add).then_inc(s_res, 1)
                    dve.wait_ge(s_res, 5 * (c + 1) * K2)
                    normalise(dve, ch, x2, xn3, c, s_v4, s_d4, s_n4)
                nc.vector.memset(acc[:, :, :], 0.0).then_inc(s_a0, 1)
                dve.wait_ge(s_rl, 16)
                nc.vector.tensor_copy(place[:, :], recs[:, :, 0]).then_inc(s_pl, 1)
                for n, f in enumerate((f1, f2)):
                    dve.wait_ge(s_fhi, n + 1)
                    nc.vector.scalar_tensor_tensor(f[:, 1, :, :].rearrange("p k n -> p (k n)"), fraw[:, n, :], WS,
                                                   f[:, 0, :, :].rearrange("p k n -> p (k n)"),
                                                   ALU.mult, ALU.subtract).then_inc(s_flo, 1)

            @block.tensor
            def _(pe):
                pe.wait_ge(s_wt, 16)
                pe.wait_ge(s_wlr, 48)
                for k in range(2):
                    last = nc.tensor.matmul(psW[:, k, :], wt[:, 128 * k:128 * (k + 1)],
                                            wlr[:, :, :].rearrange("p j h -> p (j h)"), start=True, stop=True)
                last.then_inc(s_wx, 1)
                pe.wait_ge(s_wx, 3)
                for b in range(NB + 1):
                    if b < NB:
                        pe.wait_ge(s_n4, b + 1)
                        if b >= 2:
                            pe.wait_ge(s_xt4, b - 1)
                        for k in range(2):
                            last = nc.tensor.transpose(psT4[b % 2][:, k, 0:PB], xn3[:, b, 128 * k:128 * (k + 1)],
                                                       ident[0:PB, 0:PB])
                        last.then_inc(s_t4, 1)
                    if b:
                        pe.wait_ge(s_xt4, b)
                        if b >= 3:
                            pe.wait_ge(s_rowc, b - 2)
                        for k in range(2):
                            last = nc.tensor.matmul(psX[(b - 1) % 2][0:PB, :], xTf[:, (b - 1) % 2, k, :], wx[:, k, :],
                                                    start=(k == 0), stop=(k == 1))
                        last.then_inc(s_row, 1)

        NS = T3 // HT
        BODY = 4
        with ExitStack() as p5:
            psOT = [p5.enter_context(nc.psum_tensor(f"psOT{i}", [PB, HT * 128], F32)) for i in range(2)]
            psE = [p5.enter_context(nc.psum_tensor(f"psE{i}", [128, HT, NH], F32)) for i in range(2)]
            psS = [p5.enter_context(nc.psum_tensor(f"psS{i}", [PB, NH * VW], F32)) for i in range(HT)]
            block = p5.enter_context(nc.Block())

            @block.gpsimd
            def _(pool):
                pool.wait_ge(s_rl, 16)

                def step(n, s):
                    pool.wait_ge(s_V, n + 1)
                    nc.gpsimd.tensor_copy(st3[:, s, :], recs[:, bass.ds(n * HT, HT), 1]).then_inc(s_st3[0], 1)
                    pool.wait_ge(s_st3[0], n + 1)
                    pool.sem_inc(s_halves, 1)
                    for j in range(HT):
                        pool.indirect_dma_start(
                            out=g3[:, s, j, :], out_offset=None, in_=tab_d,
                            in_offset=bass.IndirectOffsetOnAxis(ap=st3[:, s, j:j + 1], axis=0)).then_inc(s_g3[s * HT + j], 16)

                with loop(nc, pool, 0, NS // BODY) as g:
                    for s in range(BODY):
                        step(g * BODY + s, s)

            @block.scalar
            def _(act):
                def copy_turned(n, s):
                    act.wait_ge(s_ot, n + 1)
                    act.wait_ge(s_el, n + 1)
                    nc.scalar.activation(ohT[:, s % 2, :], psOT[s % 2][:, :], ACT.Copy).then_inc(s_otc, 1)

                def exps(n, s):
                    act.wait_ge(s_lk, n + 1)
                    nc.scalar.activation(pp[:, s % 2, :, :], zz[:, s % 2, :, :], ACT.Exp).then_inc(s_p, 1)

                def step(n, s):
                    if not isinstance(n, int) or 0 <= n + 1 < NS:
                        exps(n + 1, (s + 1) % BODY)
                    if not isinstance(n, int) or 0 <= n + 3 < NS:
                        copy_turned(n + 3, (s + 3) % BODY)

                for n in range(-3, BODY):
                    step(n, n % BODY)
                with loop(nc, act, 1, NS // BODY - 1) as g:
                    for s in range(BODY):
                        step(g * BODY + s, s)
                for n in range(NS - BODY, NS):
                    step(n, n % BODY)

            @block.vector
            def _(dve):
                dve.wait_ge(s_pl, 1)
                dve.wait_ge(s_a0, 1)
                dve.wait_ge(s_bl, 16)
                dve.sem_inc(s_V, 4)
                dve.sem_inc(s_z, 2)
                dve.sem_inc(s_ac, HT)

                def one_hots(n, s):
                    dve.wait_ge(s_sct, n + 1)
                    nc.vector.tensor_tensor(
                        oh3[:, s, :, :], iota[:, 0:PB].unsqueeze(1).to_broadcast([128, HT, PB]),
                        place[:, bass.ds(n * HT, HT)].unsqueeze(2).to_broadcast([128, HT, PB]),
                        ALU.is_equal).then_inc(s_oh3, 1)

                def sums(n, s, loads):
                    dve.wait_ge(s_el, n + 3)
                    for j in range(HT):
                        dve.wait_ge(s_g3[s * HT + j], 16 * loads)
                    nc.vector.tensor_tensor(zz[:, s % 2, :, :], psE[s % 2][:, :, :], g3[:, s, :, 0:NH], ALU.add).then_inc(s_z, 1)

                def leaky(n, s):
                    dve.wait_ge(s_z, n + 3)
                    z = zz[:, s % 2, :, :]
                    nc.vector.scalar_tensor_tensor(z, z, 0.2, z, ALU.mult, ALU.max).then_inc(s_lk, 1)

                def weigh(n, s):
                    dve.wait_ge(s_p, n + 1)
                    dve.wait_ge(s_sct, n + 3)
                    nc.vector.tensor_tensor(
                        vv[:, s % 2, :, :].rearrange("p j (h f) -> p j h f", h=NH),
                        g3[:, s, :, NH:RW].unsqueeze(2).to_broadcast([128, HT, NH, VW]),
                        pp[:, s % 2, :, :].unsqueeze(3).to_broadcast([128, HT, NH, VW]), ALU.mult).then_inc(s_V, 1)

                def accumulate(n, s, at_, tiles=range(HT)):
                    for j in tiles:
                        if j == 0:
                            dve.wait_ge(s_sct, n + 5)
                        dve.wait_ge(s_ac, n * HT + HT + j)
                        b = acc[:, bass.ds(at_[j], 1), :].rearrange("p b f -> p (b f)")
                        nc.vector.tensor_tensor(b, b, psS[j][:, :], ALU.add).then_inc(s_ac, 1)

                def step(n, s, at_, g=None):
                    if not isinstance(n, int) or n >= 0:
                        weigh(n, s)
                    m = n + 1
                    if not isinstance(n, int) or 0 <= m < NS:
                        sums(m, (s + 1) % BODY, m // BODY + 1 if isinstance(n, int) else g + 1 + (s + 1) // BODY)
                    halves_ = range(HT // 2), range(HT // 2, HT)
                    if not isinstance(n, int) or n >= 1:
                        accumulate(n - 1, (s - 1) % BODY, at_, halves_[0])
                    if not isinstance(n, int) or 0 <= m < NS:
                        leaky(m, (s + 1) % BODY)
                    if not isinstance(n, int) or n >= 1:
                        accumulate(n - 1, (s - 1) % BODY, at_, halves_[1])
                    if not isinstance(n, int) or 0 <= n + 3 < NS:
                        one_hots(n + 3, (s + 3) % BODY)

                def blocks_before(n, steps):
                    return registers(nc, dve, blk3[0:1, bass.ds(n * HT, steps * HT)], NB - 1)

                for n in range(-3, BODY):
                    step(n, n % BODY, blocks_before(n, 1) if n >= 1 else None)
                with loop(nc, dve, 1, NS // BODY - 1) as g:
                    at_ = blocks_before(g * BODY, BODY)
                    for s in range(BODY):
                        step(g * BODY + s, s, at_[s * HT:(s + 1) * HT], g)
                for n in range(NS - BODY, NS):
                    step(n, n % BODY, blocks_before(n, 1))
                accumulate(NS - 1, (NS - 1) % BODY, blocks_before(NS, 1))

            @block.tensor
            def _(pe):
                pe.wait_ge(s_bl, 16)
                pe.sem_inc(s_sct, 4)
                pe.sem_inc(s_el, 2)

                def turn(n, s):
                    pe.wait_ge(s_oh3, n + 1)
                    if not isinstance(n, int) or n >= 2:
                        pe.wait_ge(s_otc, n - 1)
                    for j in range(HT):
                        last = nc.tensor.transpose(psOT[s % 2][:, 128 * j:128 * (j + 1)], oh3[:, s, j, :], ident[:, :])
                    last.then_inc(s_ot, 1)

                def pick(n, s, at_):
                    pe.wait_ge(s_otc, n + 1)
                    wait_apart(pe, s_z, n + 1, s_tick[2])
                    for j in range(HT):
                        last = nc.tensor.matmul(psE[s % 2][:, j, :], ohT[:, s % 2, 128 * j:128 * (j + 1)],
                                                el[:, bass.ds(at_[j] * NH, NH)], start=True, stop=True)
                    last.then_inc(s_el, 1)

                def scatter(n, s):
                    pe.wait_ge(s_V, n + 5)
                    for j in range(HT):
                        pe.wait_ge(s_ac, n * HT + j + 1)
                        last = nc.tensor.matmul(psS[j][:, :], oh3[:, s, j, :], vv[:, s % 2, j, :], start=True, stop=True)
                    last.then_inc(s_sct, 1)

                def step(n, s, at_):
                    if not isinstance(n, int) or n >= 0:
                        scatter(n, s)
                    if not isinstance(n, int) or 0 <= n + 2 < NS:
                        pick(n + 2, (s + 2) % BODY, at_)
                    if not isinstance(n, int) or 0 <= n + 3 < NS:
                        turn(n + 3, (s + 3) % BODY)

                def blocks_of(n, steps):
                    return registers(nc, pe, blk3[0:1, bass.ds(n * HT + HT, steps * HT)], NB - 1)

                for n in range(-3, BODY):
                    step(n, n % BODY, blocks_of(n + 2, 1) if n >= -2 else None)
                with loop(nc, pe, 1, NS // BODY - 1) as g:
                    at_ = blocks_of(g * BODY + 2, BODY)
                    for s in range(BODY):
                        step(g * BODY + s, s, at_[s * HT:(s + 1) * HT])
                for n in range(NS - BODY, NS):
                    step(n, n % BODY, blocks_of(n + 2, 1) if n + 2 < NS else None)

        xn4 = at("xn4", 31 * KB, [PB, NB, D])
        xt6 = at("xt6", 106 * KB, [128, 2, 2, N], F16)
        outb = at("outb", 80 * KB, [PB, NB, D])
        fh = at("fh", 171 * KB, [128, 2, 2, FH // 128, 4 * PB], F16)
        wb = at("wb", 158 * KB, [PB, N])
        junk = at("junk", 147 * KB, [PB, N], mybir.dt.bfloat16)
        gl = at("gl", 154 * KB, [128, 2, 4 * PB])
        wrb = at("wrb", 57 * KB, [PB, D])
        b2b = at("b2b", 58 * KB, [PB, D])
        bgb = at("bgb", 59 * KB, [PB, OD])
        brb = at("brb", 59 * KB + 256, [PB, 1])
        bf1 = at("bf1", 59 * KB + 288, [128, FH // 128])
        wv = at("wv", 59 * KB + 320, [PB, NB])
        wk = at("wk", 59 * KB + 448, [PB, NB])
        cnt = at("cnt", 59 * KB + 576, [PB, NB, 3])
        rk = at("rk", 60 * KB, [PB, NB])
        den = at("den", 62 * KB, [PB, NB * NH])
        earlier = at("earlier", 61 * KB, [PB, PB])
        og = at("og", 31 * KB, [PB, NB, D])
        eg = at("eg", 171 * KB, [PB, NB, D])
        junk_d = at("junk_d", 64 * KB, [PB, 5, D])
        junk_e = at("junk_e", 70 * KB, [PB, PB])
        yt = at("yt", 73 * KB, [PB, 2, D])
        w_d = dram("w_d", (1, N))
        KEPT = max(1, N // 2) - 1
        s_b6 = sem("s_b6")
        s_om = sem("s_om")
        s_og = sem("s_og")
        s_x6 = sem("s_x6")
        s_eg = sem("s_eg")
        s_v6 = sem("s_v6")
        s_d6 = sem("s_d6")
        s_n6 = sem("s_n6")
        s_wd = sem("s_wd")
        s_wbl = sem("s_wbl")
        s_wv = sem("s_wv")
        s_be = sem("s_be")
        s_k6 = sem("s_k6")
        s_c6 = sem("s_c6")
        s_t6 = sem("s_t6")
        s_th = sem("s_th")
        s_tl = sem("s_tl")
        s_fu = sem("s_fu")
        s_gl = sem("s_gl")
        s_gh = sem("s_gh")
        s_gL = sem("s_gL")
        s_fd = sem("s_fd")
        s_yt = sem("s_yt")
        s_fin = sem("s_fin")
        s_out = sem("s_out")
        FM = FH // 128
        CB = 4
        CHUNKS = [(b, min(CB, NB - b)) for b in range(0, NB, CB)]
        with ExitStack() as p6:
            psT6 = [p6.enter_context(nc.psum_tensor(f"psT6{i}", [128, 2, 128], F32)) for i in range(2)]
            psU = [p6.enter_context(nc.psum_tensor(f"psU{i}", [128, CB * PB], F32)) for i in range(2)]
            psD = [p6.enter_context(nc.psum_tensor(f"psD{i}", [PB, D], F32)) for i in range(2)]
            block = p6.enter_context(nc.Block())

            @block.sync
            def _(sp):
                sp.dma_start(bgb[:, :], a["L1_gnn_b"].partition_broadcast(PB)).then_inc(s_b6, 16)
                sp.dma_start(wrb[:, :], a["L1_ffn_wr"].partition_broadcast(PB)).then_inc(s_b6, 16)
                sp.dma_start(brb[:, :], a["L1_ffn_br"].partition_broadcast(PB)).then_inc(s_b6, 16)
                sp.dma_start(b2b[:, :], a["L1_ffn_b2"].partition_broadcast(PB)).then_inc(s_b6, 16)
                sp.dma_start(bf1[:, :], a["L1_ffn_b1"]).then_inc(s_b6, 16)
                sp.wait_ge(s_wv, 1)
                with nc.allow_non_contiguous_dma(reason="one weight of a node"):
                    sp.dma_start(w_d.rearrange("o (b p) -> p (o b)", p=PB), wv[:, :]).then_inc(s_wd, 16)
                sp.wait_ge(s_wd, 16)
                sp.dma_start(wb[:, :], w_d[0, :].partition_broadcast(PB)).then_inc(s_wbl, 16)
                ov = out[0].rearrange("(b p) d -> p b d", p=PB)
                for b0, n in CHUNKS:
                    sp.wait_ge(s_fin, b0 + n)
                    sp.dma_start(ov[:, b0:b0 + n, :], outb[:, b0:b0 + n, :]).then_inc(s_out, 16)
                sp.wait_ge(s_out, 16 * len(CHUNKS))

            @block.gpsimd
            def _(pool):
                ch = Chain(pool, s_be)
                ch.step(nc.gpsimd.memset(earlier[:, :], 1.0))
                nc.gpsimd.affine_select(out=earlier[:, :], in_=earlier[:, :], compare_op=ALU.is_gt, fill=0.0,
                                        base=0, pattern=[[-1, PB]], channel_multiplier=1).then_inc(s_k6, 1)
                pool.wait_ge(s_b6, 80)
                for c in range(5):
                    pool.wait_ge(s_om, c + 1)
                    o_ = og[:, 5 * c:5 * c + 5, :].rearrange("p b (h f) -> p (b h) f", h=NH)
                    nc.gpsimd.tensor_tensor(o_, o_, bgb[:, :].unsqueeze(1).to_broadcast([PB, 5 * NH, OD]), ALU.add).then_inc(s_og, 1)
                for c in range(5):
                    pool.wait_ge(s_n6, 5 * c + 5)
                    cs = slice(5 * c, 5 * c + 5)
                    nc.gpsimd.tensor_tensor(x2[:, cs, :], x2[:, cs, :], xn4[:, cs, :], ALU.add).then_inc(s_x6, 1)

            @block.scalar
            def _(act):
                for c in range(5):
                    act.wait_ge(s_og, c + 1)
                    nc.scalar.activation(eg[:, 5 * c:5 * c + 5, :], og[:, 5 * c:5 * c + 5, :], ACT.Exp).then_inc(s_eg, 1)
                for c in range(6):
                    if c < 5:
                        act.wait_ge(s_v6, c + 1)
                        nc.scalar.activation(sd3[:, 0, :], mv3[:, :, 1], ACT.Sqrt).then_inc(s_d6, 1)
                    for b in range(max(5 * c - 5, 0), 5 * c):
                        act.wait_ge(s_t6, b + 1)
                        nc.scalar.activation(xt6[:, 0, :, PB * b:PB * (b + 1)], psT6[b % 2][:, :, 0:PB], ACT.Copy,
                                             scale=XS).then_inc(s_th, 1)
                act.wait_ge(s_n6, NB)
                n = 0
                act.wait_ge(s_b6, 80)
                for c, (b0, nb) in enumerate(CHUNKS):
                    w = nb * PB
                    for m in range(FM):
                        act.wait_ge(s_fu, n + 1)
                        if n >= 2:
                            act.wait_ge(s_gL, n - 1)
                        nc.scalar.activation(gl[:, n % 2, 0:w], psU[n % 2][:, 0:w], ACT.Gelu_apprx_tanh,
                                             bias=bf1[:, m:m + 1], scale=1.0 / (XS * WS)).then_inc(s_gl, 1)
                        act.wait_ge(s_gl, n + 1)
                        if c >= 2 and m == 0:
                            act.wait_ge(s_fd, CHUNKS[c - 2][0] + CHUNKS[c - 2][1])
                        nc.scalar.activation(fh[:, c % 2, 0, m, 0:w], gl[:, n % 2, 0:w], ACT.Copy, scale=HS).then_inc(s_gh, 1)
                        n += 1

            @block.vector
            def _(dve):
                ch = Chain(dve, s_c6)
                dve.wait_ge(s_b6, 80)
                v = acc[:, :, :].rearrange("p b (h f) -> p (b h) f", h=NH)
                ch.step(nc.vector.tensor_scalar(den[:, :], v[:, :, OD], 1e-12, None, ALU.max))
                ch.step(nc.vector.reciprocal(den[:, :], den[:, :]))
                for c in range(5):
                    hs = slice(5 * c * NH, 5 * (c + 1) * NH)
                    nc.vector.tensor_tensor(og[:, 5 * c:5 * c + 5, :].rearrange("p b (h f) -> p (b h) f", h=NH), v[:, hs, 0:OD],
                                            den[:, hs].unsqueeze(2).to_broadcast([PB, 5 * NH, OD]), ALU.mult).then_inc(s_om, 1)

                def halves_x(b):
                    dve.wait_ge(s_th, b + 1)
                    nc.vector.scalar_tensor_tensor(xt6[:, 1, :, PB * b:PB * (b + 1)], psT6[b % 2][:, :, 0:PB], XS,
                                                   xt6[:, 0, :, PB * b:PB * (b + 1)], ALU.mult, ALU.subtract).then_inc(s_tl, 1)

                for c in range(5):
                    cs = slice(5 * c, 5 * c + 5)
                    dve.wait_ge(s_eg, c + 1)
                    ch.step(nc.vector.tensor_scalar(eg[:, cs, :], eg[:, cs, :], 1.0, -1.0, ALU.min, ALU.add))
                    ch.step(nc.vector.tensor_tensor(eg[:, cs, :], og[:, cs, :], eg[:, cs, :], ALU.max))
                    ch.step(nc.vector.tensor_tensor(x2[:, cs, :], x2[:, cs, :], eg[:, cs, :], ALU.add))
                    normalise(dve, ch, x2, xn4, c, s_v6, s_d6, s_n6)
                    for b in range(5 * c, 5 * c + 5):
                        ch.mark(nc.vector.scalar_tensor_tensor(junk_d[:, b % 5, :], xn4[:, b, :], 1.0, wrb[:, :], ALU.mult,
                                                               ALU.mult, accum_out=wv[:, b:b + 1]))
                    for b in range(max(5 * c - 5, 0), 5 * c):
                        halves_x(b)
                    dve.wait_ge(ch.sem, ch.n)
                nc.vector.tensor_scalar(wv[:, :], wv[:, :], brb[:, :], None, ALU.add).then_inc(s_wv, 1)
                for b in range(NB - 5, NB):
                    halves_x(b)
                dve.wait_ge(s_k6, 1)
                dve.wait_ge(s_wv, 1)
                ch.step(nc.vector.memset(cnt[:, :, :], 0.0))

                def rank(b):
                    if b:
                        ch.mark(nc.vector.tensor_scalar(junk[:, 0:PB * b], wb[:, 0:PB * b], wv[:, b:b + 1], 0.0,
                                                        ALU.is_ge, ALU.add, accum_out=cnt[:, b, 0:1]))
                    ch.mark(nc.vector.tensor_scalar(junk[:, PB * b:N], wb[:, PB * b:N], wv[:, b:b + 1], 0.0,
                                                    ALU.is_gt, ALU.add, accum_out=cnt[:, b, 1:2]))
                    ch.step(nc.vector.scalar_tensor_tensor(junk_e[:, :], wb[:, PB * b:PB * (b + 1)], wv[:, b:b + 1],
                                                           earlier[:, :], ALU.is_equal, ALU.mult, accum_out=cnt[:, b, 2:3]))

                def finish(c):
                    b0, nb = CHUNKS[c]
                    for b in range(b0, b0 + nb):
                        dve.wait_ge(s_fd, b + 1)
                        ch.step(nc.vector.scalar_tensor_tensor(yt[:, b % 2, :], psD[b % 2][:, :], 1.0 / (HS * WS), b2b[:, :],
                                                               ALU.mult, ALU.add))
                        dve.sem_inc(s_yt, 1)
                        nc.vector.scalar_tensor_tensor(outb[:, b, :], yt[:, b % 2, :], wk[:, b:b + 1], x2[:, b, :],
                                                       ALU.mult, ALU.add).then_inc(s_fin, 1)

                dve.wait_ge(s_x6, 5)
                n = 0
                for c, (b0, nb) in enumerate(CHUNKS):
                    w = nb * PB
                    for m in range(FM):
                        dve.wait_ge(s_gh, n + 1)
                        nc.vector.scalar_tensor_tensor(fh[:, c % 2, 1, m, 0:w], gl[:, n % 2, 0:w], HS,
                                                       fh[:, c % 2, 0, m, 0:w], ALU.mult, ALU.subtract).then_inc(s_gL, 1)
                        n += 1
                        if n == 1:
                            dve.wait_ge(s_wbl, 16)
                        if m % 2 == 1 and m // 2 < nb:
                            rank(b0 + m // 2)
                    bs = slice(b0, b0 + nb)
                    ch.step(nc.vector.tensor_reduce(rk[:, bs], cnt[:, bs, :], AX_X, ALU.add))
                    ch.step(nc.vector.scalar_tensor_tensor(wk[:, bs], rk[:, bs], float(KEPT), wv[:, bs], ALU.is_lt, ALU.mult))
                    if c >= 1:
                        finish(c - 1)
                finish(len(CHUNKS) - 1)

            @block.tensor
            def _(pe):
                for b in range(NB):
                    pe.wait_ge(s_n6, b + 1)
                    if b >= 2:
                        pe.wait_ge(s_tl, b - 1)
                    for k in range(2):
                        last = nc.tensor.transpose(psT6[b % 2][:, k, 0:PB], xn4[:, b, 128 * k:128 * (k + 1)], ident[0:PB, 0:PB])
                    last.then_inc(s_t6, 1)

                def down(c):
                    b0, nb = CHUNKS[c]
                    pe.wait_ge(s_gL, FM * (c + 1))
                    for b in range(b0, b0 + nb):
                        if b >= 2:
                            pe.wait_ge(s_yt, b - 1)
                        cols = slice(PB * (b - b0), PB * (b - b0 + 1))
                        for m in range(FM):
                            for j, (sh, sw) in enumerate(((0, 0), (0, 1), (1, 0))):
                                last = nc.tensor.matmul(psD[b % 2][:, :], fh[:, c % 2, sh, m, cols], f2[:, sw, m, :],
                                                        start=(m == 0 and j == 0), stop=(m == FM - 1 and j == 2))
                        last.then_inc(s_fd, 1)

                n = 0
                for c, (b0, nb) in enumerate(CHUNKS):
                    cols = slice(PB * b0, PB * (b0 + nb))
                    pe.wait_ge(s_tl, b0 + nb)
                    for m in range(FM):
                        if n >= 2:
                            pe.wait_ge(s_gl, n - 1)
                        terms = [(sw, sx, k) for k in range(2) for sw, sx in ((0, 0), (0, 1), (1, 0))]
                        for i, (sw, sx, k) in enumerate(terms):
                            last = nc.tensor.matmul(psU[n % 2][:, 0:nb * PB], f1[:, sw, k, 128 * m:128 * (m + 1)],
                                                    xt6[:, sx, k, cols], start=(i == 0), stop=(i == len(terms) - 1))
                        last.then_inc(s_fu, 1)
                        n += 1
                    if c >= 1:
                        down(c - 1)
                down(len(CHUNKS) - 1)




def kernel(**inputs):
    import numpy as np
    import concourse.bacc as bacc
    from concourse.bass_utils import run_bass_kernel_spmd
    nc = bacc.Bacc("TRN2", target_bir_lowering=False, num_devices=1)
    arrays, args = {}, {}
    for name, v in [*inputs.items(), ("L1_gnn_WT", np.asarray(inputs["L1_gnn_W"]).T)]:
        v = np.ascontiguousarray(v)
        if name in ("src", "dst"):
            padded = np.full((T1 * ET,), N, v.dtype)
            padded[0:E] = v
            v = np.ascontiguousarray(padded.reshape(T1, ET).T)
        if name in VECTORS or name == "L1_ffn_b1":
            v = np.ascontiguousarray(v.reshape(-1, 128).T)
        if name in ("L0_ffn_router_w", "L1_gnn_Wl", "L1_gnn_Wr"):
            v = np.ascontiguousarray(v.T)
        if name == "L1_ffn_wr":
            v = v.reshape(-1)
        if name in ("L0_ffn_w1", "L0_ffn_w3"):
            v = np.concatenate([v.transpose(0, 2, 1), np.zeros((X, D, HP - v.shape[1]), v.dtype)], axis=2)
        if name == "L0_ffn_w2":
            v = np.concatenate([v.transpose(0, 2, 1), np.zeros((X, HP - v.shape[2], D), v.dtype)], axis=1)
        if v.ndim == 0:
            v = v.reshape(1)
        arrays["in_" + name] = v
        args[name] = nc.dram_tensor("in_" + name, v.shape, mybir.dt.from_np(v.dtype), kind="ExternalInput").ap()
    outs = [nc.dram_tensor("out_0", (N, D), F32, kind="ExternalOutput").ap()]
    program(nc, args, outs)
    r = run_bass_kernel_spmd(nc, [arrays], core_ids=[0])
    return r.results[0]["out_0"]
```
